# Optimizing a Trainium2 kernel written in Bass

```python
import numpy as np
import jax
import jax.numpy as jnp

def _softmax(x, axis=-1):
    return jax.nn.softmax(x, axis=axis)

def _gelu(x):
    return jax.nn.gelu(x, approximate=True)

def _silu(x):
    return jax.nn.silu(x)

def _sigmoid(x):
    return jax.nn.sigmoid(x)

def _layernorm(x, axis=-1, eps=1e-05):
    m = jnp.mean(x, axis=axis, keepdims=True)
    v = jnp.var(x, axis=axis, keepdims=True)
    return (x - m) / jnp.sqrt(v + eps)

def _scatter_add(tgt, idx, src, axis=0):
    return tgt.at[idx].add(src)

def _segment_sum(src, seg, n):
    return jax.ops.segment_sum(src, seg, n)
kernel_name = 'mk_gnn_preln_d4_gnn_r64_5a35c5'

def setup_inputs(seed: int=0):
    np.random.seed(seed)
    _w = jnp.asarray

    def _rec_inputs():
        import jax
        import jax.numpy as jnp
        _gk = jax.random.key(seed)
        x = -0.0002117 + 1 * jax.random.normal(jax.random.fold_in(_gk, 1), (10000, 512), jnp.float32)
        src = jax.random.randint(jax.random.fold_in(_gk, 2), (5000,), 0, 10000, jnp.int32)
        dst = jax.random.randint(jax.random.fold_in(_gk, 3), (5000,), 0, 10000, jnp.int32)
        _o = jnp.argsort(dst, stable=True)
        src = src[_o]
        dst = dst[_o]
        edge_attr_128 = 0.000276752 + 1.00001 * jax.random.normal(jax.random.fold_in(_gk, 11), (5000, 128), jnp.float32)
        edge_type_8 = jax.random.randint(jax.random.fold_in(_gk, 13), (5000,), 0, 8, jnp.int32)
        edge_weight = jax.random.uniform(jax.random.fold_in(_gk, 14), (5000,), jnp.float32, 0.0, 0.999999)
        return (x, src, dst, edge_attr_128, edge_type_8, edge_weight)
    x, src, dst, edge_attr_128, edge_type_8, edge_weight = _rec_inputs()

    def _L0_gnn_setup():
        import jax, jax.numpy as jnp
        import numpy as np
        N_NODES = 50000
        N_EDGES = 2000
        F_NODE = 512
        F_EDGE = 128
        IN_SZ = F_NODE + F_EDGE
        HID = IN_SZ * 2
        IN2 = F_NODE + HID

        def _glorot(key, shape):
            fan_in, fan_out = shape
            lim = (6.0 / (fan_in + fan_out)) ** 0.5
            return jax.random.uniform(key, shape, jnp.float32, -lim, lim)
        key = jax.random.key(seed)
        ks = jax.random.split(key, 12)
        x = jax.random.normal(ks[0], (N_NODES, F_NODE), jnp.float32)
        edge_index = jax.random.randint(ks[1], (2, N_EDGES), 0, N_NODES, jnp.int64)
        edge_attr = jax.random.normal(ks[2], (N_EDGES, F_EDGE), jnp.float32)
        W1 = _glorot(ks[3], (IN_SZ, HID))
        b1 = jnp.zeros((HID,), jnp.float32)
        W2 = _glorot(ks[4], (HID, HID))
        b2 = jnp.zeros((HID,), jnp.float32)
        W3 = _glorot(ks[5], (IN2, IN_SZ))
        b3 = jnp.zeros((IN_SZ,), jnp.float32)
        W4 = _glorot(ks[6], (IN_SZ, F_NODE))
        b4 = jnp.zeros((F_NODE,), jnp.float32)
        return {'x': x, 'edge_index': edge_index, 'edge_attr': edge_attr, 'W1': W1, 'b1': b1, 'W2': W2, 'b2': b2, 'W3': W3, 'b3': b3, 'W4': W4, 'b4': b4}
    _L0_gnn_all = _L0_gnn_setup()
    _L0_gnn_in = {k: v for k, v in _L0_gnn_all.items() if k in ('W1', 'b1', 'W2', 'b2', 'W3', 'b3', 'W4', 'b4')}
    del _L0_gnn_all

    def _L1_gnn_setup():
        import jax, jax.numpy as jnp
        import numpy as np
        N, IN_DIM, H, D, E = (50000, 512, 8, 64, 12500)
        NEG_SLOPE = 0.2
        LN_EPS = 1e-05
        key = jax.random.key(seed)
        ks = jax.random.split(key, 8)
        x = jax.random.normal(ks[0], (N, IN_DIM), dtype=jnp.float32)
        edge_index = jax.random.randint(ks[1], (2, E), 0, N, dtype=jnp.int64)
        edge_type = jax.random.randint(ks[2], (E,), 0, 8, dtype=jnp.int64)
        edge_weight = jax.random.uniform(ks[3], (E,), dtype=jnp.float32)
        W = jax.random.normal(ks[4], (H * D, IN_DIM), dtype=jnp.float32) * (1.0 / np.sqrt(IN_DIM))
        a_src = jax.random.normal(ks[5], (H, D), dtype=jnp.float32) * (1.0 / np.sqrt(D))
        a_dst = jax.random.normal(ks[6], (H, D), dtype=jnp.float32) * (1.0 / np.sqrt(D))
        et_emb = jax.random.normal(ks[7], (8, H), dtype=jnp.float32)
        ln_gamma = jnp.ones((H * D,), dtype=jnp.float32)
        ln_beta = jnp.zeros((H * D,), dtype=jnp.float32)
        return {'x': x, 'edge_index': edge_index, 'edge_type': edge_type, 'edge_weight': edge_weight, 'W': W, 'a_src': a_src, 'a_dst': a_dst, 'et_emb': et_emb, 'ln_gamma': ln_gamma, 'ln_beta': ln_beta}
    _L1_gnn_all = _L1_gnn_setup()
    _L1_gnn_in = {k: v for k, v in _L1_gnn_all.items() if k in ('W', 'a_src', 'a_dst', 'et_emb', 'ln_gamma', 'ln_beta')}
    del _L1_gnn_all

    def _L2_gnn_setup():
        import jax, jax.numpy as jnp
        import numpy as np
        N_NODES = 50000
        N_EDGES = 6250
        IN_DIM = 512
        OUT_DIM = 512
        key = jax.random.key(seed)
        k1, k2, k3, k4 = jax.random.split(key, 4)
        x = jax.random.normal(k1, (N_NODES, IN_DIM), dtype=jnp.float32)
        edge_index = jax.random.randint(k2, (2, N_EDGES), 0, N_NODES, dtype=jnp.int64)
        W = jax.random.normal(k3, (OUT_DIM, IN_DIM), dtype=jnp.float32) / np.sqrt(IN_DIM)
        b = jax.random.normal(k4, (OUT_DIM,), dtype=jnp.float32) * 0.01
        return {'x': x, 'edge_index': edge_index, 'W': W, 'b': b}
    _L2_gnn_all = _L2_gnn_setup()
    _L2_gnn_in = {k: v for k, v in _L2_gnn_all.items() if k in ('W', 'b')}
    del _L2_gnn_all

    def _L3_gnn_setup():
        import jax, jax.numpy as jnp
        import numpy as np
        N = 100000
        E = 12500
        IN_FEATS = 512
        N_HIDDEN = 128
        key = jax.random.key(seed)
        k1, k2, k3, k4, k5, k6 = jax.random.split(key, 6)
        inputs = jax.random.normal(k1, (N, IN_FEATS), dtype=jnp.float32)
        edge_index = jax.random.randint(k2, (2, E), 0, N, dtype=jnp.int64)
        edge_attr = jax.random.uniform(k3, (E,), dtype=jnp.float32)
        s_gcn = jnp.sqrt(6.0 / (IN_FEATS + N_HIDDEN)).astype(jnp.float32)
        W_gcn = jax.random.uniform(k4, (IN_FEATS, N_HIDDEN), dtype=jnp.float32, minval=-s_gcn, maxval=s_gcn)
        b_gcn = jnp.zeros((N_HIDDEN,), dtype=jnp.float32)
        s_fc = jnp.sqrt(6.0 / (N_HIDDEN + IN_FEATS)).astype(jnp.float32)
        W_fc = jax.random.uniform(k5, (IN_FEATS, N_HIDDEN), dtype=jnp.float32, minval=-s_fc, maxval=s_fc)
        b_fc = jax.random.uniform(k6, (IN_FEATS,), dtype=jnp.float32, minval=-1.0 / np.sqrt(N_HIDDEN), maxval=1.0 / np.sqrt(N_HIDDEN))
        return {'inputs': inputs, 'edge_index': edge_index, 'edge_attr': edge_attr, 'W_gcn': W_gcn, 'b_gcn': b_gcn, 'W_fc': W_fc, 'b_fc': b_fc}
    _L3_gnn_all = _L3_gnn_setup()
    _L3_gnn_in = {k: v for k, v in _L3_gnn_all.items() if k in ('W_gcn', 'b_gcn', 'W_fc', 'b_fc')}
    del _L3_gnn_all
    return {'x': x, 'src': src, 'dst': dst, 'edge_attr_128': edge_attr_128, 'edge_type_8': edge_type_8, 'edge_weight': edge_weight, 'L0_gnn_W1': _L0_gnn_in['W1'], 'L0_gnn_b1': _L0_gnn_in['b1'], 'L0_gnn_W2': _L0_gnn_in['W2'], 'L0_gnn_b2': _L0_gnn_in['b2'], 'L0_gnn_W3': _L0_gnn_in['W3'], 'L0_gnn_b3': _L0_gnn_in['b3'], 'L0_gnn_W4': _L0_gnn_in['W4'], 'L0_gnn_b4': _L0_gnn_in['b4'], 'L1_gnn_W': _L1_gnn_in['W'], 'L1_gnn_a_src': _L1_gnn_in['a_src'], 'L1_gnn_a_dst': _L1_gnn_in['a_dst'], 'L1_gnn_et_emb': _L1_gnn_in['et_emb'], 'L1_gnn_ln_gamma': _L1_gnn_in['ln_gamma'], 'L1_gnn_ln_beta': _L1_gnn_in['ln_beta'], 'L2_gnn_W': _L2_gnn_in['W'], 'L2_gnn_b': _L2_gnn_in['b'], 'L3_gnn_W_gcn': _L3_gnn_in['W_gcn'], 'L3_gnn_b_gcn': _L3_gnn_in['b_gcn'], 'L3_gnn_W_fc': _L3_gnn_in['W_fc'], 'L3_gnn_b_fc': _L3_gnn_in['b_fc']}

def reference(x, src, dst, edge_attr_128, edge_type_8, edge_weight, L0_gnn_W1, L0_gnn_b1, L0_gnn_W2, L0_gnn_b2, L0_gnn_W3, L0_gnn_b3, L0_gnn_W4, L0_gnn_b4, L1_gnn_W, L1_gnn_a_src, L1_gnn_a_dst, L1_gnn_et_emb, L1_gnn_ln_gamma, L1_gnn_ln_beta, L2_gnn_W, L2_gnn_b, L3_gnn_W_gcn, L3_gnn_b_gcn, L3_gnn_W_fc, L3_gnn_b_fc):
    import jax
    import jax.numpy as jnp

    def _L0_gnn_ref(x, edge_index, edge_attr, W1, b1, W2, b2, W3, b3, W4, b4):
        import jax, jax.numpy as jnp
        import numpy as np
        N_NODES = 50000
        N_EDGES = 2000
        F_NODE = 512
        F_EDGE = 128
        IN_SZ = F_NODE + F_EDGE
        HID = IN_SZ * 2
        IN2 = F_NODE + HID

        def _glorot(key, shape):
            fan_in, fan_out = shape
            lim = (6.0 / (fan_in + fan_out)) ** 0.5
            return jax.random.uniform(key, shape, jnp.float32, -lim, lim)
        row, col = (edge_index[0], edge_index[1])
        h = jnp.concatenate([x[row], edge_attr], axis=1)
        h = jax.nn.relu(h @ W1 + b1) @ W2 + b2
        n = x.shape[0]
        sums = jax.ops.segment_sum(h, col, num_segments=n)
        cnt = jax.ops.segment_sum(jnp.ones((h.shape[0],), h.dtype), col, num_segments=n)
        agg = sums / jnp.maximum(cnt, 1.0)[:, None]
        z = jnp.concatenate([x, agg], axis=1)
        return jax.nn.relu(z @ W3 + b3) @ W4 + b4

    def _L1_gnn_ref(x, edge_index, edge_type, edge_weight, W, a_src, a_dst, et_emb, ln_gamma, ln_beta):
        import jax, jax.numpy as jnp
        import numpy as np
        N, IN_DIM, H, D, E = (50000, 512, 8, 64, 12500)
        NEG_SLOPE = 0.2
        LN_EPS = 1e-05
        n, h_, d_ = (x.shape[0], a_src.shape[0], a_src.shape[1])
        h = (x @ W.T).reshape(n, h_, d_)
        src, dst = (edge_index[0], edge_index[1])
        h_src = h[src]
        e_src = jnp.einsum('ehd,hd->eh', h_src, a_src)
        e_dst = jnp.einsum('ehd,hd->eh', h[dst], a_dst)
        e = jax.nn.leaky_relu(e_src + e_dst, NEG_SLOPE)
        e = e * (1.0 + et_emb[edge_type])
        e = e * edge_weight[:, None]
        e_max = jnp.zeros((n, h_), x.dtype).at[dst].max(e)
        e = jnp.exp(e - e_max[dst])
        e_sum = jnp.zeros((n, h_), x.dtype).at[dst].add(e)
        alpha = e / (e_sum[dst] + 1e-10)
        msg = h_src * alpha[:, :, None]
        out = jnp.zeros((n, h_, d_), x.dtype).at[dst].add(msg).reshape(n, h_ * d_)
        out = out + x
        mu = jnp.mean(out, axis=-1, keepdims=True)
        var = jnp.var(out, axis=-1, keepdims=True)
        return (out - mu) / jnp.sqrt(var + LN_EPS) * ln_gamma + ln_beta

    def _L2_gnn_ref(x, edge_index, W, b):
        import jax, jax.numpy as jnp
        import numpy as np
        N_NODES = 50000
        N_EDGES = 6250
        IN_DIM = 512
        OUT_DIM = 512
        n = x.shape[0]
        loops = jnp.arange(n, dtype=edge_index.dtype)
        row = jnp.concatenate([edge_index[0], loops])
        col = jnp.concatenate([edge_index[1], loops])
        deg = jax.ops.segment_sum(jnp.ones(row.shape[0], dtype=x.dtype), row, num_segments=n)
        dis = jax.lax.rsqrt(deg)
        norm = dis[row] * dis[col]
        h = x @ W.T + b
        out = jax.ops.segment_sum(norm[:, None] * h[row], col, num_segments=n)
        return jax.nn.relu(out)

    def _L3_gnn_ref(inputs, edge_index, edge_attr, W_gcn, b_gcn, W_fc, b_fc):
        import jax, jax.numpy as jnp
        import numpy as np
        N = 100000
        E = 12500
        IN_FEATS = 512
        N_HIDDEN = 128
        x = inputs @ W_gcn
        src, dst = (edge_index[0], edge_index[1])
        msg = x[src] * edge_attr[:, None]
        h = jax.ops.segment_sum(msg, dst, num_segments=inputs.shape[0]) + b_gcn
        return h @ W_fc.T + b_fc
    edge_index = jnp.stack([src, dst])
    h = jnp.maximum(_layernorm(x, axis=-1), 0.0)
    x = x + _L0_gnn_ref(h, edge_index, edge_attr_128, L0_gnn_W1, L0_gnn_b1, L0_gnn_W2, L0_gnn_b2, L0_gnn_W3, L0_gnn_b3, L0_gnn_W4, L0_gnn_b4)
    h = jnp.maximum(_layernorm(x, axis=-1), 0.0)
    x = x + _L1_gnn_ref(h, edge_index, edge_type_8, edge_weight, L1_gnn_W, L1_gnn_a_src, L1_gnn_a_dst, L1_gnn_et_emb, L1_gnn_ln_gamma, L1_gnn_ln_beta)
    h = jnp.maximum(_layernorm(x, axis=-1), 0.0)
    x = x + _L2_gnn_ref(h, edge_index, L2_gnn_W, L2_gnn_b)
    h = jnp.maximum(_layernorm(x, axis=-1), 0.0)
    x = x + _L3_gnn_ref(h, edge_index, edge_weight, L3_gnn_W_gcn, L3_gnn_b_gcn, L3_gnn_W_fc, L3_gnn_b_fc)
    return x

_drawn_inputs = setup_inputs


def setup_inputs(seed=0):
    import zlib

    import numpy as np

    out = dict(_drawn_inputs(seed))
    spreads = {'L0_gnn_b1': (0.0, 0.292),
     'L0_gnn_b2': (0.0, 0.1),
     'L0_gnn_b3': (0.0, 0.1),
     'L0_gnn_b4': (0.0, 0.1),
     'L1_gnn_ln_gamma': (1.0, 0.2),
     'L1_gnn_ln_beta': (0.0, 0.1),
     'L3_gnn_b_gcn': (0.0, 0.1)}
    factors = {'L1_gnn_a_src': 3.888, 'L1_gnn_a_dst': 4.362, 'L1_gnn_et_emb': 3.053, 'L2_gnn_b': 8.0}
    for name, (base, spread) in spreads.items():
        noise = np.random.default_rng([zlib.crc32(name.encode()), seed]).standard_normal(out[name].shape)
        drawn = base * np.exp(spread * noise) if base else spread * noise
        out[name] = jnp.asarray(drawn.astype(out[name].dtype))
    for name, factor in factors.items():
        out[name] = (out[name] * factor).astype(out[name].dtype)
    return out
```

```python
import concourse.bass as bass
from concourse import mybir
from contextlib import ExitStack

F32 = mybir.dt.float32
F32R = mybir.dt.float32r
I32 = mybir.dt.int32
U32 = mybir.dt.uint32
U16 = mybir.dt.uint16
ALU = mybir.AluOpType
ACT = mybir.ActivationFunctionType

P = 128
NODES = 10000
EDGES = 5000
F = 512
FE = 128
IN = F + FE
HID = 2 * IN
KF = F // P
KI = IN // P
KH = HID // P
HEADS = 8
HD = F // HEADS
GW = F // 2
HALF = IN // 2
GROUP = 4
NEW = P - 1
ET = 40
EG = ET // GROUP
ER = EG // 2
NT = 80
NG = NT // GROUP
NR = NG // 2
ROWS_E = ET * P
ROWS_N = NT * P
EPS = 1e-5
XW = F + 4
FAR = 1.0e6
assert ET * NEW >= EDGES and NT * P >= NODES and (ET - 1) * NEW < EDGES


def group_rows(table, g, cols):
    return table[bass.ds(g * (GROUP * P), GROUP * P), 0:cols].rearrange("(j p) f -> p j f", p=P)


def tiles(x, width=F):
    return [x[:, i // GROUP, i % GROUP, 0:width] for i in range(2 * GROUP)]


def over(ap, shape):
    return ap.broadcast_to(shape)


def layer_norm_stats(dve, rows, st, steps, base, var_ready):
    for i, row in enumerate(rows):
        dve.bn_stats(st["raw"][:, i, :], row).then_inc(steps, 1)
    dve.wait_ge(steps, base + len(rows))
    dve.sem_inc(st["go"], 1)
    for i in range(len(rows)):
        dve.bn_aggr(st["mv"][:, i, :], st["raw"][:, i, :]).then_inc(var_ready, 1)


def layer_norm_std(act, st, eps):
    return act.activation(st["std"][:, :], st["mv"][:, :, 1], ACT.Sqrt, bias=eps[:, 0:1])


def layer_norm_scale(dve, st, steps, base, norm_ready, times=None):
    dve.reciprocal(st["rstd"][:, :], st["std"][:, :]).then_inc(steps, 1)
    dve.wait_ge(steps, base)
    if times is not None:
        dve.tensor_tensor(st["rstd"][:, :], st["rstd"][:, :], times, ALU.mult).then_inc(steps, 1)
        dve.wait_ge(steps, base + 1)
    dve.scalar_tensor_tensor(out=st["shift"][:, :], in0=st["mv"][:, :, 0], scalar=-1.0, in1=st["rstd"][:, :],
                             op0=ALU.mult, op1=ALU.mult).then_inc(norm_ready, 1)


def relu_norm(act, out, x, st, i):
    return act.activation(out, x, ACT.Relu, bias=st["shift"][:, i:i + 1], scale=st["rstd"][:, i:i + 1])


class Core:

    def __init__(self, nc):
        self.nc = nc
        self.whole = ExitStack()
        self.sems = []

    def run(self, build, *args):
        self.sems = []
        build(self.nc, self, *args)
        self.nc.clear_and_free_semaphores(self.sems)
        self.nc.all_engine_barrier()

    def sem(self, name):
        self.sems.append(self.nc.alloc_semaphore(name))
        return self.sems[-1]

    def sb(self, stack, name, shape, dt=F32):
        return stack.enter_context(self.nc.sbuf_tensor(name, shape, dt))

    def ps(self, stack, name, shape):
        return stack.enter_context(self.nc.psum_tensor(name, shape, F32))

    def stats(self, stack, name):
        return {"go": self.sem(name + "_lngo"), "raw": self.sb(stack, name + "_raw", [P, 2 * GROUP, 6]),
                "mv": self.sb(stack, name + "_mv", [P, 2 * GROUP, 2]),
                "std": self.sb(stack, name + "_std", [P, 2 * GROUP]),
                "rstd": self.sb(stack, name + "_rstd", [P, 2 * GROUP]),
                "shift": self.sb(stack, name + "_shift", [P, 2 * GROUP])}


def split_on_act(act, raw, hi, loaded, count, hi_done):
    act.wait_ge(loaded, count)
    act.copy(hi, raw).then_inc(hi_done, 1)


def split_on_dve(dve, raw, hi, lo, hi_done, count, lo_done):
    dve.wait_ge(hi_done, count)
    dve.tensor_tensor(lo, raw, hi.bitcast(F32), ALU.subtract).then_inc(lo_done, 1)


def three(pe, out, a, b, first, last):
    (ah, al), (bh, bl) = a, b
    pe.matmul(out, ah, bh, start=first, stop=False)
    pe.matmul(out, ah, bl, start=False, stop=False)
    return pe.matmul(out, al, bh, start=False, stop=last)


def prepare(nc, core, a, keep, l0):
    sem = core.sem
    idx_loaded, rows_loaded, small_loaded = sem("a_idx"), sem("a_rows"), sem("a_small")
    w1_loaded = [sem("a_w1l0"), sem("a_w1l1")]
    w2_loaded = [sem("a_w2l0"), sem("a_w2l1")]
    w3b_loaded = sem("a_w3b")
    iota_ready, zero_ready = sem("a_iota"), sem("a_zero")
    dve_step = sem("a_dve")
    onehot_ready, hist_read, hist_done = sem("a_onehot"), sem("a_hist_read"), sem("a_hist")
    count_ready, root_ready, = sem("a_count"), sem("a_root")
    w1_hi, w1_lo = sem("a_w1hi"), sem("a_w1lo")
    fold_ready, fold_hi, fold_lo = sem("a_fold"), sem("a_fold_hi"), sem("a_fold_lo")
    c2_ready, ident_ready = sem("a_c2"), sem("a_ident")
    FAC_K = HEADS

    with ExitStack() as st:
        sb = lambda n, s, d=F32: core.sb(st, "a_" + n, s, d)
        dst_i, nxt_i, src_i, typ_i = (sb(n, [P, ET], I32) for n in ("dst", "nxt", "src", "typ"))
        row_i = sb("rowi", [P, 2, GROUP * P], I32)
        wgt = sb("wgt", [P, ET])
        emb = sb("emb", [P, 8 * HEADS])
        hl = sb("hl", [P, 4, ET], I32)
        last = sb("last", [P, ET])
        val = sb("val", [P, ET])
        iota_i = sb("iotai", [P, P], I32)
        iota_f = sb("iotaf", [P, P])
        slot_i = sb("sloti", [P, ET], I32)
        pick = sb("pick", [P, ET])
        term = sb("term", [P, ET, HEADS])
        onehot = sb("onehot", [P, 4, GROUP, P])
        zeros = sb("zeros", [P, P])
        found = sb("found", [P, NT])
        W1raw = sb("W1raw", [P, 2, HID])
        W3b = sb("W3b", [P, KH, IN])
        W2m = sb("W2m", [P, 2, KH, P])
        b2c = sb("b2c", [P, KH])
        b2w = sb("b2w", [P, KH, P])
        root = sb("root", [P, NT])
        hist = core.ps(st, "a_hist_ps", [P, 2, 512])
        fold = core.ps(st, "a_fold_ps", [P, 4, 512])
        c2p = core.ps(st, "a_c2_ps", [P, 2, 512])

        with nc.Block() as block:
            @block.sync
            def _(sp):
                sp.dma_start(dst_i[:, :], a["dst_win"]).then_inc(idx_loaded, 16)
                sp.dma_start(nxt_i[:, :], a["dst_next"]).then_inc(idx_loaded, 16)
                sp.dma_start(src_i[:, :], a["src_count"]).then_inc(idx_loaded, 16)
                sp.dma_start(typ_i[:, :], a["type_win"]).then_inc(idx_loaded, 16)
                sp.dma_start(keep["src"][:, :], a["src_win"]).then_inc(idx_loaded, 16)
                sp.dma_start(keep["dst"][:, :], a["dst_wide"]).then_inc(idx_loaded, 16)
                sp.dma_start(wgt[:, :], a["weight_win"]).then_inc(small_loaded, 16)
                sp.dma_start(emb[:, :], a["L1_gnn_et_emb"].rearrange("(o k) h -> o (k h)", o=1).broadcast_to([P, 8 * HEADS])
                             ).then_inc(small_loaded, 16)
                sp.dma_start(b2c[:, :], a["L0_gnn_b2"].rearrange("(k p) -> p k", p=P),
                             allow_slow_non_contiguous=True).then_inc(small_loaded, 16)
                sp.dma_start(l0["b1"][:, :], a["L0_gnn_b1"].rearrange("(k p) -> p k", p=P),
                             allow_slow_non_contiguous=True).then_inc(small_loaded, 16)
                sp.dma_start(W3b[:, :, :], a["L0_gnn_W3"][F:F + HID, :].rearrange("(k p) n -> p k n", p=P)
                             ).then_inc(w3b_loaded, 16)
                for k in range(KI):
                    if k >= 2:
                        sp.wait_ge(w1_lo, k - 1)
                    sp.dma_start(W1raw[:, k % 2, :], a["L0_gnn_W1"][k * P:(k + 1) * P, :]).then_inc(w1_loaded[k % 2], 16)
                for k in range(2, KH):
                    sp.wait_ge(fold_ready, k - 1)
                    sp.dma_start(W2m[:, k % 2, :, :], a["W2T"][:, k * P:(k + 1) * P].rearrange("(k p) m -> p k m", p=P)
                                   ).then_inc(w2_loaded[k % 2], 16)

            @block.scalar
            def _(act):
                for k in range(2):
                    act.dma_start(W2m[:, k, :, :], a["W2T"][:, k * P:(k + 1) * P].rearrange("(k p) m -> p k m", p=P)
                                  ).then_inc(w2_loaded[k], 16)
                for k in range(KI):
                    act.wait_ge(w1_loaded[k % 2], 16 * (k // 2 + 1))
                    act.copy(l0["W1h"][:, k, :], W1raw[:, k % 2, :]).then_inc(w1_hi, 1)
                act.wait_ge(count_ready, 1)
                act.activation(root[:, :], found[:, :], ACT.Sqrt).then_inc(root_ready, 1)
                with act.Fori(0, KH // 2) as it:
                    for b in range(2):
                        act.wait_ge(fold_ready, it * 2 + (b + 1))
                        for h in range(2):
                            act.copy(l0["W23h"][:, it * 2 + b, h * HALF:(h + 1) * HALF],
                                     fold[:, 2 * b + h, 0:HALF]).then_inc(fold_hi, 1)

            @block.gpsimd
            def _(pool):
                pool.iota(iota_i[:, :], [[1, P]], base=0, channel_multiplier=0).then_inc(iota_ready, 1)
                pool.iota(slot_i[:, :], [[P, ET]], base=1, channel_multiplier=1).then_inc(iota_ready, 1)
                pool.memset(zeros[:, :], 0.0).then_inc(zero_ready, 1)
                pool.memset(keep["ident"][:, :], 1.0).then_inc(ident_ready, 1)
                pool.wait_ge(ident_ready, 1)
                pool.affine_select(out=keep["ident"][:, :], in_=keep["ident"][:, :], compare_op=ALU.is_equal, fill=0.0,
                                   base=0, pattern=[[-1, P]], channel_multiplier=1).then_inc(ident_ready, 1)

            @block.vector
            def _(dve):
                n = 0

                def step(ins):
                    nonlocal n
                    n += 1
                    ins.then_inc(dve_step, 1)
                    dve.wait_ge(dve_step, n)

                step(dve.memset(keep["eps"][:, :], EPS))
                dve.wait_ge(iota_ready, 2)
                dve.wait_ge(idx_loaded, 16 * 6)
                step(dve.tensor_copy(iota_f[:, :], iota_i[:, :]))
                for k, ids in enumerate((src_i, dst_i)):
                    step(dve.tensor_scalar(hl[:, 2 * k, :], ids[:, :], 127, None, ALU.bitwise_and))
                    step(dve.tensor_scalar(hl[:, 2 * k + 1, :], ids[:, :], 7, None, ALU.logical_shift_right))
                step(dve.tensor_tensor(last[:, :], dst_i[:, :], nxt_i[:, :], ALU.not_equal))
                step(dve.tensor_tensor(val[:, :], last[:, :], slot_i[:, :], ALU.mult))
                dve.wait_ge(small_loaded, 16 * 4)
                fac = keep["fac"][:, :, :]
                step(dve.memset(fac, 1.0))
                for k in range(FAC_K):
                    step(dve.tensor_scalar(pick[:, :], typ_i[:, :], float(k), None, ALU.is_equal))
                    step(dve.tensor_tensor(term[:, :, :], over(pick[:, :].unsqueeze(2), [P, ET, HEADS]),
                                           over(emb[:, k * HEADS:(k + 1) * HEADS].unsqueeze(1), [P, ET, HEADS]), ALU.mult))
                    step(dve.tensor_tensor(fac, fac, term[:, :, :], ALU.add))
                step(dve.tensor_tensor(fac, fac, over(wgt[:, :].unsqueeze(2), [P, ET, HEADS]), ALU.mult))
                step(dve.tensor_copy(keep["wgt"][:, :], wgt[:, :]))
                step(dve.tensor_copy(b2w[:, :, :], over(b2c[:, :].unsqueeze(2), [P, KH, P])))
                c2 = n
                assert c2 == B2W_STEP
                for k in range(KI):
                    dve.wait_ge(w1_hi, k + 1)
                    dve.tensor_tensor(l0["W1l"][:, k, :], W1raw[:, k % 2, :], l0["W1h"][:, k, :].bitcast(F32),
                                      ALU.subtract).then_inc(w1_lo, 1)
                with dve.Fori(0, EG) as g:
                    dve.wait_ge(hist_read, g)
                    for q, (part, width) in enumerate(((0, P), (1, NT), (2, P), (3, NT))):
                        cols = over(hl[:, part, bass.ds(g * GROUP, GROUP)].unsqueeze(2), [P, GROUP, width])
                        dve.tensor_tensor(onehot[:, q, :, 0:width], over(iota_f[:, 0:width].unsqueeze(1), [P, GROUP, width]),
                                          cols, ALU.is_equal).then_inc(onehot_ready, 1)
                    dve.wait_ge(onehot_ready, g * 5 + 4)
                    dve.tensor_tensor(onehot[:, 3, :, 0:NT], onehot[:, 3, :, 0:NT],
                                      over(val[:, bass.ds(g * GROUP, GROUP)].unsqueeze(2), [P, GROUP, NT]),
                                      ALU.mult).then_inc(onehot_ready, 1)
                dve.wait_ge(hist_done, 1)
                dve.tensor_scalar(found[:, :], hist[:, 0, 0:NT], 1.0, None, ALU.add).then_inc(count_ready, 1)
                dve.wait_ge(root_ready, 1)
                step(dve.reciprocal(keep["dis"][:, 0:NT], root[:, :]))
                step(dve.tensor_scalar(keep["has"][:, 0:NT], hist[:, 1, 0:NT], 0.0, None, ALU.is_gt))
                step(dve.tensor_scalar(found[:, :], keep["has"][:, 0:NT], -FAR, FAR - 1.0, ALU.mult, ALU.add))
                step(dve.memset(keep["slot"][:, :], 1 << 20))
                step(dve.memset(keep["dis"][:, NT:NT + 8], 0.0))
                step(dve.memset(keep["has"][:, NT:NT + 8], 0.0))
                step(dve.tensor_tensor(keep["dis2"][:, :], keep["dis"][:, :], keep["dis"][:, :], ALU.mult))
                step(dve.tensor_tensor(keep["dish"][:, :], keep["dis"][:, :], keep["has"][:, :], ALU.mult))
                step(dve.tensor_tensor(keep["slot"][:, 0:NT], hist[:, 1, 0:NT], found[:, :], ALU.add))
                with dve.Fori(0, KH // 2) as it:
                    for b in range(2):
                        for h in range(2):
                            dve.wait_ge(fold_hi, it * 4 + (2 * b + h + 1))
                            dve.tensor_tensor(l0["W23l"][:, it * 2 + b, h * HALF:(h + 1) * HALF], fold[:, 2 * b + h, 0:HALF],
                                              l0["W23h"][:, it * 2 + b, h * HALF:(h + 1) * HALF].bitcast(F32),
                                              ALU.subtract).then_inc(fold_lo, 1)
                dve.wait_ge(c2_ready, 1)
                for h in range(2):
                    step(dve.tensor_copy(l0["c2"][:, h * HALF:(h + 1) * HALF], c2p[:, h, 0:HALF]))

            @block.tensor
            def _(pe):
                pe.wait_ge(zero_ready, 1)
                for q in range(2):
                    pe.matmul(hist[:, q, 0:NT], zeros[:, :], zeros[:, 0:NT], start=True, stop=False)
                with pe.Fori(0, EG) as g:
                    pe.wait_ge(onehot_ready, g * 5 + 5)
                    for j in range(GROUP):
                        for q in range(2):
                            mm = pe.matmul(hist[:, q, 0:NT], onehot[:, 2 * q, j, :], onehot[:, 2 * q + 1, j, 0:NT],
                                           start=False, stop=False)
                    mm.then_inc(hist_read, 1)
                for q in range(2):
                    mm = pe.matmul(hist[:, q, 0:NT], zeros[:, :], zeros[:, 0:NT], start=False, stop=True)
                mm.then_inc(hist_done, 1)
                pe.wait_ge(w3b_loaded, 16)
                with pe.Fori(0, KH // 2) as it:
                    for b in range(2):
                        pe.wait_ge(w2_loaded[b], it * 16 + 16)
                        pe.wait_ge(fold_lo, it * 4)
                        for h in range(2):
                            for k in range(KH):
                                mm = pe.matmul(fold[:, 2 * b + h, 0:HALF], W2m[:, b, k, :], W3b[:, k, h * HALF:(h + 1) * HALF],
                                               start=(k == 0), stop=(k == KH - 1))
                        mm.then_inc(fold_ready, 1)
                pe.wait_ge(dve_step, B2W_STEP)
                for h in range(2):
                    for k in range(KH):
                        mm = pe.matmul(c2p[:, h, 0:HALF], b2w[:, k, :], W3b[:, k, h * HALF:(h + 1) * HALF],
                                       start=(k == 0), stop=(k == KH - 1))
                mm.then_inc(c2_ready, 1)


B2W_STEP = 1 + 1 + 4 + 2 + 1 + 3 * HEADS + 1 + 1 + 1


def layer0_edges(nc, core, a, keep, l0, T0):
    sem = core.sem
    idx_staged, go = sem("b_idx"), sem("b_go")
    x_loaded = [sem("b_x0"), sem("b_x1")]
    attr_loaded = [sem("b_attr0"), sem("b_attr1")]
    rows_loaded = sem("b_rows")
    dve_init = sem("b_init")
    ln_step, var_ready, std_ready, norm_ready, h_ready = (sem("b_" + n) for n in ("lnstep", "var", "std", "norm", "h"))
    tp_ready, tp_free, hT_hi = sem("b_tp"), sem("b_tpfree"), sem("b_hThi")
    hid_ready, relu_ready, hid_hi, hid_lo = sem("b_hid"), sem("b_relu"), sem("b_hidhi"), sem("b_hidlo")
    y_ready = [sem("b_y0"), sem("b_y1")]
    y_out = [sem("b_yo0"), sem("b_yo1")]
    row_ready, carry_ready, match_ready = sem("b_row"), sem("b_carry"), sem("b_match")
    sum_ready, cnt_inv, sum_scaled = sem("b_sum"), sem("b_cnt"), sem("b_scaled")
    sum_stored = sem("b_stored")

    with ExitStack() as st:
        sb = lambda n, s, d=F32: core.sb(st, "b_" + n, s, d)
        X = sb("X", [P, 2, GROUP, F])
        attr = sb("attr", [P, 2, GROUP, FE])
        idx = sb("idx", [P, 2 * GROUP], I32)
        stt = core.stats(st, "b")
        hTh, hTl = sb("hTh", [P, KI, GROUP * P], F32R), sb("hTl", [P, KI, GROUP * P], F32R)
        R = sb("R", [P, 2, GROUP * P])
        Rh, Rl = sb("Rh", [P, KH, GROUP * P], F32R), sb("Rl", [P, KH, GROUP * P], F32R)
        Y = sb("Y", [P, 2, IN + 2])
        carry = sb("carry", [1, IN + 2])
        match = sb("match", [P, GROUP, P])
        inv = sb("inv", [P, 1])
        T = sb("T", [P, IN])
        tp = core.ps(st, "b_tp_ps", [P, 2, 512])
        hid = core.ps(st, "b_hid_ps", [P, 2, 512])
        y = core.ps(st, "b_y_ps", [P, 2, 512])
        s = core.ps(st, "b_s_ps", [P, 2, 512])
        rows16 = keep["rows"]
        SW = (HALF, HALF + 2)

        with nc.Block() as block:
            @block.gpsimd
            def _(pool):
                with pool.Fori(0, ER + 1) as r:
                    pool.tensor_copy(idx[:, :], keep["src"][:, bass.ds(r * (2 * GROUP), 2 * GROUP)]).then_inc(idx_staged, 1)
                    pool.wait_ge(idx_staged, r + 1)
                    pool.wait_ge(tp_ready, r * (2 * KI))
                    pool.sem_inc(go, 1)
                    for i in range(2 * GROUP):
                        pool.indirect_dma_start(X[:, i // GROUP, i % GROUP, :], None, a["x"][:, :],
                                                bass.IndirectOffsetOnAxis(idx[:, i:i + 1], 0),
                                                bounds_check=NODES - 1, oob_is_err=False).then_inc(x_loaded[i // GROUP], 16)
                    pool.wait_ge(x_loaded[0], r * 64 + 64)
                    pool.wait_ge(x_loaded[1], r * 64 + 64)
                    pool.sem_inc(go, 1)

            @block.sync
            def _(sp):
                for b in range(2):
                    sp.dma_start(attr[:, b, :, :], a["attr_win"][:, b, :, :]).then_inc(attr_loaded[b], 16)
                with sp.Fori(0, ER) as r:
                    for t in range(2 * GROUP):
                        sp.wait_ge(sum_scaled, (r * (2 * GROUP) + t) * 2 + 2)
                        sp.dma_start(T0[bass.ds((r * (2 * GROUP) + t) * P, P), :], T[:, :]).then_inc(sum_stored, 16)
                        if t in (4, 5):
                            b = t - 4
                            sp.wait_ge(tp_ready, r * (2 * KI) + 2 * KI)
                            sp.dma_start(attr[:, b, :, :], a["attr_win"][:, r * 2 + (2 + b), :, :]).then_inc(attr_loaded[b], 16)
                sp.wait_ge(sum_stored, 16 * ET)
                for b in range(2):
                    sp.wait_ge(attr_loaded[b], 16 * (ER + 1))

            @block.scalar
            def _(act):
                def norm(r):
                    act.wait_ge(var_ready, r * 8 + 8)
                    layer_norm_std(act, stt, keep["eps"]).then_inc(std_ready, 1)
                    act.wait_ge(norm_ready, r + 1)
                    for i in range(2 * GROUP):
                        xi = X[:, i // GROUP, i % GROUP, :]
                        relu_norm(act, xi, xi, stt, i).then_inc(h_ready, 1)

                def transposed(r, b):
                    act.wait_ge(hid_ready, r * 20 + 10 * b)
                    for c in range(KI):
                        act.wait_ge(tp_ready, r * 10 + (5 * b + c + 1))
                        act.copy(hTh[:, c, :], tp[:, (5 * b + c) % 2, :]).then_inc(hT_hi, 1)

                def hidden(r, b, m):
                    k = 10 * b + m
                    if m == 0:
                        act.wait_ge(y_ready[1], r * 8 + 4 * b)
                    act.wait_ge(hid_ready, r * 20 + (k + 1))
                    act.wait_ge(hid_lo, r * 20 + k)
                    act.activation(R[:, m % 2, :], hid[:, m % 2, :], ACT.Relu, bias=l0["b1"][:, m:m + 1]).then_inc(relu_ready, 1)
                    act.activation(Rh[:, m, :], hid[:, m % 2, :], ACT.Relu, bias=l0["b1"][:, m:m + 1]).then_inc(hid_hi, 1)

                def carry_out(r, t):
                    act.wait_ge(sum_ready, r * 8 + (t + 1))
                    act.wait_ge(row_ready, r * 8 + (t + 1))
                    act.copy(carry[0:1, 0:HALF], s[0:1, 0, 0:HALF]).then_inc(carry_ready, 1)
                    act.copy(carry[0:1, HALF:IN + 2], s[0:1, 1, 0:HALF + 2]).then_inc(carry_ready, 1)

                def edge_rows(r, t):
                    act.wait_ge(y_ready[0], r * 8 + (t + 1))
                    act.copy(Y[:, t % 2, 0:HALF], y[:, 0, 0:HALF]).then_inc(y_out[0], 1)
                    if t % 4:
                        carry_out(r, t - 1)
                    act.wait_ge(y_out[0], r * 8 + (t + 1))
                    act.wait_ge(y_out[1], r * 8 + (t + 1))
                    act.wait_ge(carry_ready, r * 16 + 2 * t)
                    act.copy(Y[0:1, t % 2, :], carry[0:1, :]).then_inc(row_ready, 1)

                act.wait_ge(dve_init, 2)
                norm(0)
                with act.Fori(0, ER) as r:
                    transposed(r, 0)
                    for m in range(KH):
                        hidden(r, 0, m)
                    transposed(r, 1)
                    for t in range(4):
                        edge_rows(r, t)
                    for m in range(KH):
                        hidden(r, 1, m)
                        if m == 3:
                            carry_out(r, 3)
                    norm(r + 1)
                    for t in range(4, 8):
                        edge_rows(r, t)
                    carry_out(r, 7)

            @block.vector
            def _(dve):
                dve.memset(Y[:, :, IN:IN + 2], 1.0).then_inc(dve_init, 1)
                dve.memset(carry[:, :], 0.0).then_inc(dve_init, 1)

                def norm(r):
                    dve.wait_ge(x_loaded[0], r * 64 + 64)
                    dve.wait_ge(x_loaded[1], r * 64 + 64)
                    layer_norm_stats(dve, tiles(X), stt, ln_step, r * 9, var_ready)
                    dve.wait_ge(std_ready, r + 1)
                    layer_norm_scale(dve, stt, ln_step, r * 9 + 9, norm_ready)

                def transposed(r, b):
                    for c in range(KI):
                        dve.wait_ge(hT_hi, r * 10 + (5 * b + c + 1))
                        dve.tensor_tensor(hTl[:, c, :], tp[:, (5 * b + c) % 2, :], hTh[:, c, :].bitcast(F32),
                                          ALU.subtract).then_inc(tp_free, 1)

                def hidden(r, b, m):
                    dve.wait_ge(hid_hi, r * 20 + (10 * b + m + 1))
                    dve.tensor_tensor(Rl[:, m, :], R[:, m % 2, :], Rh[:, m, :].bitcast(F32), ALU.subtract).then_inc(hid_lo, 1)

                def build_match(r, b):
                    dve.wait_ge(sum_ready, r * 8 + 4 * b)
                    g = r * 8 + 4 * b
                    dve.tensor_tensor(match[:, :, :], rows16[:, bass.ds(g * P, GROUP * P)].rearrange("p (j q) -> p j q", q=P),
                                      over(keep["dst"][:, bass.ds(g, GROUP)].unsqueeze(2), [P, GROUP, P]),
                                      ALU.is_equal).then_inc(match_ready, 1)

                def sums(r, t):
                    dve.wait_ge(carry_ready, r * 16 + (2 * t + 2))
                    dve.reciprocal(inv[:, :], s[:, 1, HALF:HALF + 1]).then_inc(cnt_inv, 1)
                    dve.wait_ge(cnt_inv, r * 8 + (t + 1))
                    dve.wait_ge(sum_stored, r * 128 + 16 * t)
                    for h in range(2):
                        dve.scalar_tensor_tensor(out=T[:, h * HALF:(h + 1) * HALF], in0=s[:, h, 0:HALF], scalar=inv[:, 0:1],
                                                 in1=l0["c2"][:, h * HALF:(h + 1) * HALF], op0=ALU.mult, op1=ALU.add
                                                 ).then_inc(sum_scaled, 1)

                def edge_rows(r, t):
                    dve.wait_ge(y_ready[1], r * 8 + (t + 1))
                    dve.tensor_copy(Y[:, t % 2, HALF:IN], y[:, 1, 0:HALF]).then_inc(y_out[1], 1)
                    if t % 4:
                        sums(r, t - 1)

                norm(0)
                with dve.Fori(0, ER) as r:
                    build_match(r, 0)
                    transposed(r, 0)
                    for m in range(KH):
                        hidden(r, 0, m)
                    transposed(r, 1)
                    for t in range(4):
                        edge_rows(r, t)
                    for m in range(KH):
                        hidden(r, 1, m)
                        if m == 3:
                            sums(r, 3)
                            build_match(r, 1)
                    norm(r + 1)
                    for t in range(4, 8):
                        edge_rows(r, t)
                    sums(r, 7)

            @block.tensor
            def _(pe):
                def transpose(r, b):
                    for c in range(KI):
                        k = 5 * b + c
                        if c == 0:
                            pe.wait_ge(h_ready, r * 8 + (4 * b + 4))
                        if c == KF:
                            pe.wait_ge(attr_loaded[b], r * 16 + 16)
                        pe.wait_ge(tp_free, r * 10 + (k + 1))
                        for j in range(GROUP):
                            rows = X[:, b, j, c * P:(c + 1) * P] if c < KF else attr[:, b, j, :]
                            mm = pe.transpose(tp[:, k % 2, j * P:(j + 1) * P], rows, keep["ident"][:, :])
                        mm.then_inc(tp_ready, 1)

                def first(r, b, m):
                    k = 10 * b + m
                    if m == 0:
                        pe.wait_ge(tp_free, r * 10 + (5 * b + 5 + 2))
                    pe.wait_ge(hid_hi, r * 20 + k)
                    for c in range(KI):
                        mm = three(pe, hid[:, m % 2, :],
                                   (l0["W1h"][:, c, m * P:(m + 1) * P], l0["W1l"][:, c, m * P:(m + 1) * P]),
                                   (hTh[:, c, :], hTl[:, c, :]), c == 0, c == KI - 1)
                    mm.then_inc(hid_ready, 1)

                def second(r, b, j):
                    t = 4 * b + j
                    if j == 0:
                        pe.wait_ge(hid_lo, r * 20 + (10 * b + 10))
                    for h in range(2):
                        pe.wait_ge(y_out[h], r * 8 + t)
                        for k in range(KH):
                            w = slice(h * HALF, (h + 1) * HALF)
                            mm = three(pe, y[:, h, 0:HALF], (Rh[:, k, j * P:(j + 1) * P], Rl[:, k, j * P:(j + 1) * P]),
                                       (l0["W23h"][:, k, w], l0["W23l"][:, k, w]), k == 0, k == KH - 1)
                        mm.then_inc(y_ready[h], 1)

                def sum_runs(r, t):
                    pe.wait_ge(row_ready, r * 8 + (t + 1))
                    pe.wait_ge(match_ready, r * 2 + (t // 4 + 1))
                    pe.wait_ge(sum_scaled, r * 16 + 2 * t)
                    pe.wait_ge(carry_ready, r * 16 + 2 * t)
                    for h in range(2):
                        mm = pe.matmul(s[:, h, 0:SW[h]], match[:, t % 4, :], Y[:, t % 2, h * HALF:h * HALF + SW[h]],
                                       start=True, stop=True)
                    mm.then_inc(sum_ready, 1)

                pe.sem_inc(tp_free, 2)
                with pe.Fori(0, ER) as r:
                    transpose(r, 0)
                    for m in range(KH):
                        first(r, 0, m)
                    transpose(r, 1)
                    for j in range(GROUP):
                        second(r, 0, j)
                        if j:
                            sum_runs(r, j - 1)
                    for m in range(KH):
                        first(r, 1, m)
                        if m == 2:
                            sum_runs(r, 3)
                    for j in range(GROUP):
                        second(r, 1, j)
                        if j:
                            sum_runs(r, 4 + j - 1)
                    sum_runs(r, 7)


def layer0_nodes(nc, core, a, keep, T0, x1):
    sem = core.sem
    w_loaded, w_hi, w_lo, init = sem("c_w"), sem("c_whi"), sem("c_wlo"), sem("c_init")
    x_loaded = [sem("c_x0"), sem("c_x1")]
    res_loaded = [sem("c_r0"), sem("c_r1")]
    run_loaded = [sem("c_g0"), sem("c_g1")]
    idx_staged, go, res_ready = sem("c_idx"), sem("c_go"), sem("c_res")
    ln_step, var_ready, std_ready, norm_ready, h_ready = (sem("c_" + n) for n in ("lnstep", "var", "std", "norm", "h"))
    tp_ready, tp_free, hT_hi = sem("c_tp"), sem("c_tpfree"), sem("c_hThi")
    u_ready, u_out, z_hi = sem("c_u"), sem("c_uout"), sem("c_zhi")
    o_ready, o_out = sem("c_o"), sem("c_oout")
    stored = [sem("c_st0"), sem("c_st1")]
    TPR = 2 * (KF + KI)
    GT = 2 * GROUP

    with ExitStack() as st:
        sb = lambda n, s, d=F32: core.sb(st, "c_" + n, s, d)
        X = sb("X", [P, 2, GROUP, F])
        XB = sb("XB", [P, 2, GROUP, F])
        G = sb("G", [P, 2, GROUP, IN])
        idx = sb("idx", [P, GT], I32)
        stt = core.stats(st, "c")
        hTh, hTl = sb("hTh", [P, 2, KF, GROUP * P], F32R), sb("hTl", [P, 2, KF, GROUP * P], F32R)
        U = sb("U", [P, 2, GROUP, IN])
        R = sb("R", [P, 2, GROUP * P])
        zh, zl = sb("zh", [P, 2, KI, GROUP * P], F32R), sb("zl", [P, 2, KI, GROUP * P], F32R)
        W3h, W3l = sb("W3h", [P, KF, IN], F32R), sb("W3l", [P, KF, IN], F32R)
        W4h, W4l = sb("W4h", [P, KI, F], F32R), sb("W4l", [P, KI, F], F32R)
        b3, b4 = sb("b3", [P, KI]), sb("b4", [P, F])
        tp = core.ps(st, "c_tp_ps", [P, 2, 512])
        u = core.ps(st, "c_u_ps", [P, 4, 512])
        o = core.ps(st, "c_o_ps", [P, 2, 512])
        W3raw = U[:, 0, :, :]
        W4raw = U[:, 1, :, :].rearrange("p j n -> p (j n)").rearrange("p (k n) -> p k n", k=KI)

        with nc.Block() as block:
            @block.sync
            def _(sp):
                def load(g, b):
                    sp.dma_start(X[:, b, :, :], group_rows(a["x"], g, F)).then_inc(x_loaded[b], 16)

                def load_last(buf, b, sems):
                    at = (NG - 1) * GROUP * P
                    left = NODES - at
                    for j in range((left + P - 1) // P):
                        n = min(P, left - j * P)
                        sp.dma_start(buf[0:n, b, j, :], a["x"][at + j * P:at + j * P + n, :]).then_inc(sems[b], 16)

                def residual(g, b):
                    sp.dma_start(XB[:, b, :, :], group_rows(a["x"], g, F)).then_inc(res_loaded[b], 16)

                def store(r, g, b):
                    sp.wait_ge(o_out, r * GT + (4 * b + 4 + 2))
                    sp.dma_start(group_rows(x1, g, F), XB[:, b, :, :]).then_inc(stored[b], 16)

                for b in range(2):
                    load(b, b)
                sp.dma_start(W3raw, a["L0_gnn_W3"][0:F, :].rearrange("(k p) n -> p k n", p=P)).then_inc(w_loaded, 16)
                sp.dma_start(W4raw, a["L0_gnn_W4"].rearrange("(k p) n -> p k n", p=P)).then_inc(w_loaded, 16)
                sp.dma_start(b3[:, :], a["L0_gnn_b3"].rearrange("(k p) -> p k", p=P),
                             allow_slow_non_contiguous=True).then_inc(w_loaded, 16)
                sp.dma_start(b4[:, :], a["L0_gnn_b4"].rearrange("(o n) -> o n", o=1).broadcast_to([P, F])).then_inc(w_loaded, 16)
                sp.wait_ge(init, 2)
                with sp.Fori(0, NR - 2) as r:
                    for b in range(2):
                        sp.wait_ge(stored[b], r * 16)
                        residual(r * 2 + b, b)
                    sp.wait_ge(tp_ready, r * TPR + 2 * KF)
                    for b in range(2):
                        load(r * 2 + (2 + b), b)
                    for b in range(2):
                        store(r, r * 2 + b, b)
                for r in (NR - 2, NR - 1):
                    for b in range(2):
                        sp.wait_ge(stored[b], 16 * r)
                        if r == NR - 1 and b:
                            load_last(XB, b, res_loaded)
                        else:
                            residual(2 * r + b, b)
                    sp.wait_ge(tp_ready, r * TPR + 2 * KF)
                    for b in range(2):
                        if r == NR - 1:
                            load(b, b)
                        elif b:
                            load_last(X, b, x_loaded)
                        else:
                            load(2 * r + 2, b)
                    for b in range(2):
                        store(r, 2 * r + b, b)
                for b in range(2):
                    sp.wait_ge(stored[b], 16 * NR)
                    sp.wait_ge(x_loaded[b], 16 * (NR + 1) + 32 * b)

            @block.gpsimd
            def _(pool):
                pool.memset(G[:, :, :, :], 0.0).then_inc(init, 1)
                pool.memset(XB[:, 1, :, :], 0.0).then_inc(init, 1)
                pool.wait_ge(w_loaded, 64)
                pool.wait_ge(init, 2)

                def round_(r, late):
                    pool.tensor_copy(idx[:, :], keep["slot"][:, bass.ds(r * GT, GT)]).then_inc(idx_staged, 1)
                    pool.wait_ge(idx_staged, r + 1)
                    pool.wait_ge(u_out, r * (2 * GT) + 4)
                    pool.sem_inc(go, 1)
                    for i in range(GT):
                        pool.indirect_dma_start(G[:, i // GROUP, i % GROUP, :], None, T0[:, :],
                                                bass.IndirectOffsetOnAxis(idx[:, i:i + 1], 0),
                                                bounds_check=ROWS_E - 1, oob_is_err=False).then_inc(run_loaded[i // GROUP], 16)
                    for b in range(2):
                        pool.wait_ge(res_loaded[b], r * 16 + (16 + late * b))
                        pool.tensor_tensor(XB[:, b, :, :], XB[:, b, :, :], over(b4[:, :].unsqueeze(1), [P, GROUP, F]),
                                           ALU.add).then_inc(res_ready, 1)
                    for b in range(2):
                        pool.wait_ge(run_loaded[b], r * 64 + 64)
                    pool.sem_inc(go, 1)

                with pool.Fori(0, NR - 1) as r:
                    round_(r, 0)
                round_(NR - 1, 32)

            @block.scalar
            def _(act):
                def norm(r):
                    act.wait_ge(var_ready, r * GT + GT)
                    layer_norm_std(act, stt, keep["eps"]).then_inc(std_ready, 1)
                    act.wait_ge(norm_ready, r + 1)
                    for i, x in enumerate(tiles(X)):
                        relu_norm(act, x, x, stt, i).then_inc(h_ready, 1)

                def transposed(r, b):
                    for c in range(KF):
                        act.wait_ge(tp_ready, r * TPR + (KF * b + c + 1))
                        act.copy(hTh[:, b, c, :], tp[:, (KF * b + c) % 2, :]).then_inc(hT_hi, 1)

                def hidden(r, b):
                    act.wait_ge(o_ready, r * GT)
                    for c in range(KI):
                        k = 2 * KF + KI * b + c
                        act.wait_ge(tp_ready, r * TPR + (k + 1))
                        act.activation(R[:, k % 2, :], tp[:, k % 2, :], ACT.Relu, bias=b3[:, c:c + 1]).then_inc(z_hi, 1)
                        act.activation(zh[:, b, c, :], tp[:, k % 2, :], ACT.Relu, bias=b3[:, c:c + 1]).then_inc(z_hi, 1)

                norm(0)
                for n, (raw, hi) in enumerate(((W3raw, W3h), (W4raw, W4h))):
                    split_on_act(act, raw, hi[:, :, :], w_loaded, 64, w_hi)
                with act.Fori(0, NR) as r:
                    for b in range(2):
                        transposed(r, b)
                    norm(r + 1)
                    for b in range(2):
                        hidden(r, b)

            @block.vector
            def _(dve):
                def norm(r, late=0):
                    for b in range(2):
                        dve.wait_ge(x_loaded[b], r * 16 + (16 + late * b))
                    layer_norm_stats(dve, tiles(X), stt, ln_step, r * 9, var_ready)
                    dve.wait_ge(std_ready, r + 1)
                    layer_norm_scale(dve, stt, ln_step, r * 9 + 9, norm_ready)

                def add_runs(r, b):
                    for j in range(GROUP):
                        t = GROUP * b + j
                        if j == 0:
                            dve.wait_ge(run_loaded[b], r * 64 + 64)
                        dve.wait_ge(u_ready, r * GT + (t + 1))
                        for h in range(2):
                            w = slice(h * HALF, (h + 1) * HALF)
                            dve.scalar_tensor_tensor(out=U[:, b, j, w], in0=G[:, b, j, w],
                                                     scalar=keep["has"][:, bass.ds(r * GT + t, 1)],
                                                     in1=u[:, 2 * (t % 2) + h, 0:HALF], op0=ALU.mult, op1=ALU.add
                                                     ).then_inc(u_out, 1)

                def round_(r, late):
                    for b in range(2):
                        for c in range(KF):
                            k = KF * b + c
                            dve.wait_ge(hT_hi, r * (2 * KF) + (k + 1))
                            dve.tensor_tensor(hTl[:, b, c, :], tp[:, k % 2, :], hTh[:, b, c, :].bitcast(F32),
                                              ALU.subtract).then_inc(tp_free, 1)
                    add_runs(r, 0)
                    norm(r + 1, late)
                    add_runs(r, 1)
                    for b in range(2):
                        for c in range(KI):
                            k = KI * b + c
                            dve.wait_ge(z_hi, r * (4 * KI) + (2 * k + 2))
                            dve.tensor_tensor(zl[:, b, c, :], R[:, k % 2, :], zh[:, b, c, :].bitcast(F32),
                                              ALU.subtract).then_inc(tp_free, 1)
                    for b in range(2):
                        dve.wait_ge(res_ready, r * 2 + (b + 1))
                        for j in range(GROUP):
                            t = GROUP * b + j
                            dve.wait_ge(o_ready, r * GT + (t + 1))
                            dve.tensor_tensor(XB[:, b, j, :], o[:, t % 2, :], XB[:, b, j, :], ALU.add).then_inc(o_out, 1)

                norm(0)
                for n, (raw, hi, lo) in enumerate(((W3raw, W3h, W3l), (W4raw, W4h, W4l))):
                    split_on_dve(dve, raw, hi[:, :, :], lo[:, :, :], w_hi, n + 1, w_lo)
                with dve.Fori(0, NR - 2) as r:
                    round_(r, 0)
                for r in (NR - 2, NR - 1):
                    round_(r, 32)

            @block.tensor
            def _(pe):
                def transpose(r, k, source):
                    pe.wait_ge(tp_free, r * TPR + (k + 1))
                    for j in range(GROUP):
                        mm = pe.transpose(tp[:, k % 2, j * P:(j + 1) * P], source(j), keep["ident"][:, :])
                    mm.then_inc(tp_ready, 1)

                def first(r, b):
                    pe.wait_ge(tp_free, r * TPR + (KF * b + KF + 2))
                    for j in range(GROUP):
                        t = GROUP * b + j
                        pe.wait_ge(u_out, r * (2 * GT) + (2 * t + 2))
                        for h in range(2):
                            w = slice(h * HALF, (h + 1) * HALF)
                            for c in range(KF):
                                mm = three(pe, u[:, 2 * (t % 2) + h, 0:HALF],
                                           (hTh[:, b, c, j * P:(j + 1) * P], hTl[:, b, c, j * P:(j + 1) * P]),
                                           (W3h[:, c, w], W3l[:, c, w]), c == 0, c == KF - 1)
                        mm.then_inc(u_ready, 1)

                def second(r, b):
                    pe.wait_ge(tp_free, r * TPR + (2 * KF + KI * b + KI + 2))
                    for j in range(GROUP):
                        t = GROUP * b + j
                        pe.wait_ge(o_out, r * GT + (t + 1))
                        for c in range(KI):
                            mm = three(pe, o[:, t % 2, :], (zh[:, b, c, j * P:(j + 1) * P], zl[:, b, c, j * P:(j + 1) * P]),
                                       (W4h[:, c, :], W4l[:, c, :]), c == 0, c == KI - 1)
                        mm.then_inc(o_ready, 1)

                pe.sem_inc(tp_free, 2)
                pe.sem_inc(u_out, 4)
                pe.sem_inc(o_out, 2)
                pe.wait_ge(w_lo, 2)
                with pe.Fori(0, NR) as r:
                    for b in range(2):
                        pe.wait_ge(h_ready, r * GT + (GROUP * b + GROUP))
                        for c in range(KF):
                            transpose(r, KF * b + c, lambda j: X[:, b, j, c * P:(c + 1) * P])
                    for b in range(2):
                        first(r, b)
                    for b in range(2):
                        pe.wait_ge(u_out, r * (2 * GT) + (2 * GROUP * (b + 1) + 4))
                        for c in range(KI):
                            transpose(r, 2 * KF + KI * b + c, lambda j: U[:, b, j, c * P:(c + 1) * P])
                    for b in range(2):
                        second(r, b)


def layer1_messages(nc, core, a, keep, x1, msg, logit):
    sem = core.sem
    w_loaded, w_hi, w_lo, diag_set = sem("d_w"), sem("d_whi"), sem("d_wlo"), sem("d_diag")
    proj_ready = sem("d_proj")
    idx_staged, go = sem("d_idx"), sem("d_go")
    x_loaded = [sem("d_x0"), sem("d_x1")]
    ln_step, var_ready, std_ready, norm_ready, h_ready = (sem("d_" + n) for n in ("lnstep", "var", "std", "norm", "h"))
    tp_ready, tp_free, hT_hi = sem("d_tp"), sem("d_tpfree"), sem("d_hThi")
    m_ready, m_out = sem("d_m"), [sem("d_mo0"), sem("d_mo1")]
    dot_ready, dot_step, dot_read = sem("d_dot"), sem("d_dotstep"), sem("d_dotread")
    LW = (GW, GW + HEADS)

    with ExitStack() as st:
        sb = lambda n, s, d=F32: core.sb(st, "d_" + n, s, d)
        X = sb("X", [P, 2, 2, GROUP, F])
        idx = sb("idx", [P, 2 * GROUP], I32)
        stt = core.stats(st, "d")
        hTh, hTl = sb("hTh", [P, 2, KF, GROUP * P], F32R), sb("hTl", [P, 2, KF, GROUP * P], F32R)
        Wh, Wl = sb("Wh", [P, KF, F + HEADS], F32R), sb("Wl", [P, KF, F + HEADS], F32R)
        Ah, Al = sb("Ah", [P, KF, HEADS], F32R), sb("Al", [P, KF, HEADS], F32R)
        Wraw = sb("Wraw", [P, KF, F])
        Wrow = sb("Wrow", [P, KF, F])
        diag = sb("diag", [P, 2, KF, HEADS])
        dots = sb("dots", [P, GROUP, HEADS])
        tp = core.ps(st, "d_tp_ps", [P, 2, 512])
        m = core.ps(st, "d_m_ps", [P, 4, 512])
        dot = core.ps(st, "d_dot_ps", [P, 512])
        proj = core.ps(st, "d_proj_ps", [P, 512])
        dotv = dot[:, 0:GROUP * HEADS].rearrange("p (j h) -> p j h", h=HEADS)
        projv = proj[:, 0:2 * KF * HEADS].rearrange("p (a k h) -> p a k h", a=2, h=HEADS)

        with nc.Block() as block:
            @block.sync
            def _(sp):
                sp.dma_start(Wraw[:, :, :], a["W1T"].rearrange("(k p) n -> p k n", p=P)).then_inc(w_loaded, 16)
                sp.dma_start(Wrow[:, :, :], a["L1_gnn_W"].rearrange("(k p) n -> p k n", p=P)).then_inc(w_loaded, 16)
                sp.wait_ge(diag_set, 1)
                for q, n in enumerate(("L1_gnn_a_src", "L1_gnn_a_dst")):
                    for h in range(HEADS):
                        sp.dma_start(diag[HD * (h % 2):HD * (h % 2) + HD, q, h // 2, h:h + 1],
                                     a[n][h:h + 1, :].rearrange("o d -> d o"), allow_slow_non_contiguous=True
                                     ).then_inc(w_loaded, 16)

            @block.gpsimd
            def _(pool):
                pool.memset(diag[:, :, :, :], 0.0).then_inc(diag_set, 1)
                with pool.Fori(0, ER) as r:
                    for b in range(2):
                        g = r * 2 + b
                        for q, n in enumerate(("src", "dst")):
                            pool.tensor_copy(idx[:, q * GROUP:(q + 1) * GROUP],
                                             keep[n][:, bass.ds(g * GROUP, GROUP)]).then_inc(idx_staged, 1)
                        pool.wait_ge(idx_staged, r * 4 + (2 * b + 2))
                        pool.wait_ge(tp_ready, r * 16 + 8 * b + (0 if b == 0 else 0))
                        pool.sem_inc(go, 1)
                        for i in range(2 * GROUP):
                            pool.indirect_dma_start(X[:, b, i // GROUP, i % GROUP, :], None, x1[:, :],
                                                    bass.IndirectOffsetOnAxis(idx[:, i:i + 1], 0),
                                                    bounds_check=ROWS_N - 1, oob_is_err=False).then_inc(x_loaded[b], 16)
                        pool.wait_ge(x_loaded[b], r * 128 + 128)
                        pool.sem_inc(go, 1)

            @block.scalar
            def _(act):
                def norm(r, b):
                    act.wait_ge(var_ready, r * 16 + (8 * b + 8))
                    layer_norm_std(act, stt, keep["eps"]).then_inc(std_ready, 1)
                    act.wait_ge(norm_ready, r * 2 + (b + 1))
                    for i, x in enumerate(tiles(X[:, b, :, :, :])):
                        relu_norm(act, x, x, stt, i).then_inc(h_ready, 1)

                split_on_act(act, Wraw[:, :, :], Wh[:, :, 0:F], w_loaded, 16 * 18, w_hi)
                split_on_act(act, projv[:, 0, :, :], Wh[:, :, F:F + HEADS], proj_ready, 1, w_hi)
                split_on_act(act, projv[:, 1, :, :], Ah[:, :, :], proj_ready, 1, w_hi)
                with act.Fori(0, ER) as r:
                    for b in range(2):
                        norm(r, b)
                        act.wait_ge(dot_ready, r * 2 + b)
                        for q in range(2):
                            for c in range(KF):
                                k = 8 * b + KF * q + c
                                act.wait_ge(tp_ready, r * 16 + (k + 1))
                                act.copy(hTh[:, q, c, :], tp[:, k % 2, :]).then_inc(hT_hi, 1)
                        for j in range(GROUP):
                            act.wait_ge(m_ready, r * 8 + (4 * b + j + 1))
                            act.copy(msg[:, bass.ds(r * 8 + (4 * b + j), 1), 0:GW],
                                     m[:, 2 * (j % 2):2 * (j % 2) + 1, 0:GW]).then_inc(m_out[0], 1)

            @block.vector
            def _(dve):
                split_on_dve(dve, Wraw[:, :, :], Wh[:, :, 0:F], Wl[:, :, 0:F], w_hi, 1, w_lo)
                split_on_dve(dve, projv[:, 0, :, :], Wh[:, :, F:F + HEADS], Wl[:, :, F:F + HEADS], w_hi, 3, w_lo)
                split_on_dve(dve, projv[:, 1, :, :], Ah[:, :, :], Al[:, :, :], w_hi, 3, w_lo)
                with dve.Fori(0, ER) as r:
                    for b in range(2):
                        dve.wait_ge(x_loaded[b], r * 128 + 128)
                        layer_norm_stats(dve, tiles(X[:, b, :, :, :]), stt, ln_step, r * 18 + 9 * b, var_ready)
                        dve.wait_ge(std_ready, r * 2 + (b + 1))
                        layer_norm_scale(dve, stt, ln_step, r * 18 + (9 * b + 9), norm_ready)
                        for q in range(2):
                            for c in range(KF):
                                k = 8 * b + KF * q + c
                                dve.wait_ge(hT_hi, r * 16 + (k + 1))
                                dve.tensor_tensor(hTl[:, q, c, :], tp[:, k % 2, :], hTh[:, q, c, :].bitcast(F32),
                                                  ALU.subtract).then_inc(tp_free, 1)
                        for j in range(GROUP):
                            dve.wait_ge(m_ready, r * 8 + (4 * b + j + 1))
                            dve.tensor_copy(msg[:, bass.ds(r * 8 + (4 * b + j), 1), GW:F + HEADS],
                                            m[:, 2 * (j % 2) + 1:2 * (j % 2) + 2, 0:GW + HEADS]).then_inc(m_out[1], 1)
                        dve.wait_ge(dot_ready, r * 2 + (b + 1))
                        dve.wait_ge(m_out[1], r * 8 + (4 * b + 4 + 2))
                        g = r * 8 + 4 * b
                        dve.tensor_tensor(dots[:, :, :], dotv, msg[:, bass.ds(g, GROUP), F:F + HEADS], ALU.add
                                          ).then_inc(dot_step, 1)
                        dve.wait_ge(dot_step, r * 4 + (2 * b + 1))
                        dve.scalar_tensor_tensor(out=dots[:, :, :], in0=dots[:, :, :], scalar=0.2, in1=dots[:, :, :],
                                                 op0=ALU.mult, op1=ALU.max).then_inc(dot_step, 1)
                        dve.wait_ge(dot_step, r * 4 + (2 * b + 2))
                        dve.tensor_tensor(logit[:, bass.ds(g, GROUP), :], dots[:, :, :], keep["fac"][:, bass.ds(g, GROUP), :],
                                          ALU.mult).then_inc(dot_read, 1)

            @block.tensor
            def _(pe):
                pe.wait_ge(w_loaded, 16 * 18)
                for q in range(2):
                    for k in range(KF):
                        for c in range(KF):
                            mm = pe.matmul(projv[:, q, k, :], Wrow[:, c, k * P:(k + 1) * P], diag[:, q, c, :],
                                           start=(c == 0), stop=(c == KF - 1))
                mm.then_inc(proj_ready, 1)
                pe.sem_inc(tp_free, 2)
                pe.sem_inc(m_out[0], 2)
                pe.sem_inc(m_out[1], 2)
                pe.wait_ge(w_lo, 3)
                with pe.Fori(0, ER) as r:
                    for b in range(2):
                        pe.wait_ge(h_ready, r * 16 + (8 * b + 8))
                        for q in range(2):
                            for c in range(KF):
                                k = 8 * b + KF * q + c
                                pe.wait_ge(tp_free, r * 16 + (k + 1))
                                for j in range(GROUP):
                                    mm = pe.transpose(tp[:, k % 2, j * P:(j + 1) * P],
                                                      X[:, b, q, j, c * P:(c + 1) * P], keep["ident"][:, :])
                                mm.then_inc(tp_ready, 1)
                        pe.wait_ge(tp_free, r * 16 + (8 * b + 8 + 2))
                        for j in range(GROUP):
                            t = 4 * b + j
                            for h in range(2):
                                pe.wait_ge(m_out[h], r * 8 + (t + 1))
                                for c in range(KF):
                                    mm = three(pe, m[:, 2 * (j % 2) + h, 0:LW[h]],
                                               (hTh[:, 0, c, j * P:(j + 1) * P], hTl[:, 0, c, j * P:(j + 1) * P]),
                                               (Wh[:, c, GW * h:GW * h + LW[h]], Wl[:, c, GW * h:GW * h + LW[h]]),
                                               c == 0, c == KF - 1)
                            mm.then_inc(m_ready, 1)
                        pe.wait_ge(dot_read, r * 2 + b)
                        for j in range(GROUP):
                            for c in range(KF):
                                mm = three(pe, dotv[:, j, :], (hTh[:, 1, c, j * P:(j + 1) * P], hTl[:, 1, c, j * P:(j + 1) * P]),
                                           (Ah[:, c, :], Al[:, c, :]), c == 0, c == KF - 1)
                        mm.then_inc(dot_ready, 1)


def layer1_softmax(nc, core, a, keep, logit):
    sem = core.sem
    loaded, same_ready, turned, flat, fwd_done, bwd_done, shifted, exped, back, out_done = (
        sem("s_" + n) for n in ("loaded", "same", "turned", "flat", "fwd", "bwd", "shift", "exp", "back", "out"))
    with ExitStack() as st:
        sb = lambda n, s, d=F32: core.sb(st, "s_" + n, s, d)
        L = sb("L", [HEADS, ROWS_E])
        top = sb("top", [HEADS, ROWS_E])
        ids = sb("ids", [HEADS, ROWS_E], I32)
        same = sb("same", [HEADS, ROWS_E + 1], U16)
        turn = core.ps(st, "s_turn_ps", [P, 4, 512])
        rows = core.ps(st, "s_rows_ps", [P, 512])
        rowsv = rows[:, 0:ET * HEADS].rearrange("p (t h) -> p t h", h=HEADS)
        with nc.Block() as block:
            @block.sync
            def _(sp):
                sp.dma_start(ids[:, :], a["dst_flat"].broadcast_to([HEADS, ROWS_E])).then_inc(loaded, 16)

            @block.tensor
            def _(pe):
                for g in range(EG):
                    if g >= 4:
                        pe.wait_ge(flat, g - 3)
                    for j in range(GROUP):
                        mm = pe.transpose(turn[0:HEADS, g % 4, j * P:(j + 1) * P], logit[:, GROUP * g + j, :], keep["ident"][:, :])
                    mm.then_inc(turned, 1)
                pe.wait_ge(exped, 1)
                for t in range(ET):
                    mm = pe.transpose(rowsv[:, t, :], L[:, t * P:(t + 1) * P], keep["ident"][0:HEADS, 0:HEADS])
                mm.then_inc(back, 1)

            @block.scalar
            def _(act):
                for g in range(EG):
                    act.wait_ge(turned, g + 1)
                    act.copy(L[:, g * 512:(g + 1) * 512], turn[0:HEADS, g % 4, :]).then_inc(flat, 1)
                act.wait_ge(shifted, 1)
                act.activation(L[:, :], L[:, :], ACT.Exp).then_inc(exped, 1)

            @block.vector
            def _(dve):
                dve.memset(same[:, 0:1], 0).then_inc(same_ready, 1)
                dve.memset(same[:, ROWS_E:ROWS_E + 1], 0).then_inc(same_ready, 1)
                dve.wait_ge(loaded, 16)
                dve.tensor_tensor(same[:, 1:ROWS_E], ids[:, 1:ROWS_E], ids[:, 0:ROWS_E - 1], ALU.is_equal).then_inc(same_ready, 1)
                dve.wait_ge(same_ready, 3)
                dve.wait_ge(flat, EG)
                dve.tensor_tensor_scan(top[:, :], same[:, 0:ROWS_E], L[:, :], 0.0, ALU.mult, ALU.max).then_inc(fwd_done, 1)
                dve.wait_ge(fwd_done, 1)
                dve.tensor_tensor_scan(top[:, ::-1], same[:, ROWS_E:0:-1], top[:, ::-1], 0.0, ALU.mult, ALU.max).then_inc(bwd_done, 1)
                dve.wait_ge(bwd_done, 1)
                dve.tensor_tensor(L[:, :], L[:, :], top[:, :], ALU.subtract).then_inc(shifted, 1)
                dve.wait_ge(back, 1)
                dve.tensor_copy(logit[:, :, :], rowsv).then_inc(out_done, 1)


def layer1_sums(nc, core, a, keep, msg, prob, T1):
    sem = core.sem
    init, weighed, row_ready, carry_ready, match_ready = (sem("e_" + n) for n in ("init", "weighed", "row", "carry", "match"))
    sum_ready, den_step, den_ready, scaled, stored = (sem("e_" + n) for n in ("sum", "denstep", "den", "scaled", "stored"))
    st_sem = [sem("e_st0"), sem("e_st1")]
    LW = (GW, GW + HEADS)
    with ExitStack() as st:
        sb = lambda n, s, d=F32: core.sb(st, "e_" + n, s, d)
        Y = sb("Y", [P, 2, 1, F + HEADS])
        carry = sb("carry", [1, F + HEADS])
        match = sb("match", [P, 2, GROUP, P])
        den, inv = sb("den", [P, HEADS]), sb("inv", [P, HEADS])
        T = sb("T", [P, 2, F])
        s = core.ps(st, "e_s_ps", [P, 4, 512])
        half = HEADS // 2
        with nc.Block() as block:
            @block.sync
            def _(sp):
                with sp.Fori(0, ET // 2) as r:
                    for b in range(2):
                        sp.wait_ge(scaled, r * 4 + (2 * b + 2))
                        sp.dma_start(T1[bass.ds((r * 2 + b) * P, P), :], T[:, b, :]).then_inc(st_sem[b], 16)
                for b in range(2):
                    sp.wait_ge(st_sem[b], 16 * (ET // 2))

            @block.scalar
            def _(act):
                act.wait_ge(init, 1)
                with act.Fori(0, ET // 2) as r:
                    for b in range(2):
                        t = r * 2 + b
                        act.wait_ge(weighed, r * 4 + (2 * b + 2))
                        act.wait_ge(carry_ready, r * 4 + 2 * b)
                        act.copy(Y[0:1, b, 0, :], carry[0:1, :]).then_inc(row_ready, 1)
                        act.wait_ge(sum_ready, t + 1)
                        act.wait_ge(row_ready, t + 1)
                        for h in range(2):
                            act.copy(carry[0:1, GW * h:GW * h + LW[h]], s[0:1, 2 * b + h, 0:LW[h]]).then_inc(carry_ready, 1)

            @block.vector
            def _(dve):
                dve.memset(carry[:, :], 0.0).then_inc(init, 1)

                def weigh(r, b):
                    t = r * 2 + b
                    dve.tensor_tensor(Y[:, b, :, 0:F].rearrange("p o (h d) -> p (o h) d", d=HD),
                                      msg[:, bass.ds(t, 1), 0:F].rearrange("p o (h d) -> p (o h) d", d=HD),
                                      over(prob[:, bass.ds(t, 1), :].rearrange("p o h -> p (o h)").unsqueeze(2), [P, HEADS, HD]),
                                      ALU.mult).then_inc(weighed, 1)
                    dve.tensor_copy(Y[:, b, :, F:F + HEADS], prob[:, bass.ds(t, 1), :]).then_inc(weighed, 1)

                def sums(r, b):
                    dve.wait_ge(carry_ready, r * 4 + (2 * b + 2))
                    dve.tensor_scalar(den[:, :], s[:, 2 * b + 1, GW:GW + HEADS], 1e-10, None, ALU.add).then_inc(den_step, 1)
                    dve.wait_ge(den_step, r * 4 + (2 * b + 1))
                    dve.reciprocal(inv[:, :], den[:, :]).then_inc(den_step, 1)
                    dve.wait_ge(den_step, r * 4 + (2 * b + 2))
                    dve.wait_ge(st_sem[b], r * 16)
                    for h in range(2):
                        dve.tensor_tensor(T[:, b, GW * h:GW * (h + 1)].rearrange("p (h d) -> p h d", d=HD),
                                          s[:, 2 * b + h, 0:GW].rearrange("p (h d) -> p h d", d=HD),
                                          over(inv[:, half * h:half * (h + 1)].unsqueeze(2), [P, half, HD]),
                                          ALU.mult).then_inc(scaled, 1)

                with dve.Fori(0, EG // 2) as q:
                    for gb in range(2):
                        g = (q * 2 + gb) * GROUP
                        dve.tensor_tensor(match[:, gb, :, :], keep["rows"][:, bass.ds(g * P, GROUP * P)].rearrange("p (j q) -> p j q", q=P),
                                          over(keep["dst"][:, bass.ds(g, GROUP)].unsqueeze(2), [P, GROUP, P]),
                                          ALU.is_equal).then_inc(match_ready, 1)
                        for jj in range(2):
                            r = q * 4 + (2 * gb + jj)
                            weigh(r, 0)
                            weigh(r, 1)
                            sums(r, 0)
                            sums(r, 1)

            @block.tensor
            def _(pe):
                with pe.Fori(0, EG // 2) as q:
                    for gb in range(2):
                        pe.wait_ge(match_ready, q * 2 + (gb + 1))
                        for j in range(GROUP):
                            t = q * 8 + (4 * gb + j)
                            pe.wait_ge(row_ready, t + 1)
                            for h in range(2):
                                mm = pe.matmul(s[:, 2 * (j % 2) + h, 0:LW[h]], match[:, gb, j, :],
                                               Y[:, j % 2, 0, GW * h:GW * h + LW[h]], start=True, stop=True)
                            mm.then_inc(sum_ready, 1)


def layer1_nodes(nc, core, a, keep, x1, T1, x2):
    sem = core.sem
    w_loaded, init, idx_staged, go = sem("n_w"), sem("n_init"), sem("n_idx"), sem("n_go")
    x_loaded = [sem("n_x0"), sem("n_x1")]
    run_loaded = [sem("n_g0"), sem("n_g1")]
    ln_step, var_ready, std_ready, norm_ready, h_ready = (sem("n_" + n) for n in ("lnstep", "var", "std", "norm", "h"))
    ln2_step, var2_ready, std2_ready, norm2_ready, n_ready = (sem("n2_" + n) for n in ("lnstep", "var", "std", "norm", "n"))
    res_ready, added, times_gamma, out_ready = sem("n_res"), sem("n_added"), sem("n_gamma"), sem("n_out")
    stored = sem("n_stored")
    GT = 2 * GROUP

    with ExitStack() as st:
        sb = lambda n, s, d=F32: core.sb(st, "n_" + n, s, d)
        X = sb("X", [P, 2, 2, GROUP, F])
        G = sb("G", [P, 2, 2, GROUP, F])
        H = sb("H", [P, 2, GROUP, F])
        O = sb("O", [P, 2, GROUP, XW])
        idx = sb("idx", [P, GT], I32)
        one, two = core.stats(st, "n1"), core.stats(st, "n2")
        gamma, beta = sb("gamma", [P, F]), sb("beta", [P, F])

        with nc.Block() as block:
            @block.sync
            def _(sp):
                sp.dma_start(gamma[:, :], a["L1_gnn_ln_gamma"].rearrange("(o n) -> o n", o=1).broadcast_to([P, F])).then_inc(w_loaded, 16)
                sp.dma_start(beta[:, :], a["L1_gnn_ln_beta"].rearrange("(o n) -> o n", o=1).broadcast_to([P, F])).then_inc(w_loaded, 16)
                with sp.Fori(0, NR // 2) as q:
                    for rb in range(2):
                        sp.wait_ge(out_ready, q * 32 + 16 * rb)
                        for b in range(2):
                            sp.dma_start(X[:, rb, b, :, :], group_rows(x1, q * 4 + (2 * rb + b), F)).then_inc(x_loaded[rb], 16)
                        if rb:
                            for k in range(2):
                                sp.wait_ge(out_ready, q * 32 + 16 * (k + 1))
                                for b in range(2):
                                    sp.dma_start(group_rows(x2, q * 4 + (2 * k + b), XW), O[:, b, :, :]).then_inc(stored, 16)
                sp.wait_ge(stored, 16 * NG)

            @block.gpsimd
            def _(pool):
                pool.memset(G[:, :, :, :, :], 0.0).then_inc(init, 1)
                pool.wait_ge(w_loaded, 32)
                pool.wait_ge(init, 1)
                with pool.Fori(0, NR // 2) as q:
                    for rb in range(2):
                        r = q * 2 + rb
                        pool.tensor_copy(idx[:, :], keep["slot"][:, bass.ds(r * GT, GT)]).then_inc(idx_staged, 1)
                        pool.wait_ge(idx_staged, r + 1)
                        pool.wait_ge(out_ready, q * 32 + 16 * rb)
                        pool.sem_inc(go, 1)
                        for i in range(GT):
                            pool.indirect_dma_start(G[:, rb, i // GROUP, i % GROUP, :], None, T1[:, :],
                                                    bass.IndirectOffsetOnAxis(idx[:, i:i + 1], 0),
                                                    bounds_check=ROWS_E - 1, oob_is_err=False).then_inc(run_loaded[rb], 16)
                        pool.wait_ge(run_loaded[rb], q * 128 + 128)
                        pool.wait_ge(h_ready, r * GT + GT)
                        for b in range(2):
                            pool.tensor_tensor(X[:, rb, b, :, :], X[:, rb, b, :, :], over(beta[:, :].unsqueeze(1), [P, GROUP, F]),
                                               ALU.add).then_inc(res_ready, 1)

            @block.scalar
            def _(act):
                with act.Fori(0, NR // 2) as q:
                    for rb in range(2):
                        r = q * 2 + rb
                        act.wait_ge(var_ready, r * GT + GT)
                        layer_norm_std(act, one, keep["eps"]).then_inc(std_ready, 1)
                        act.wait_ge(norm_ready, r + 1)
                        act.wait_ge(added, r * GT)
                        for i in range(GT):
                            relu_norm(act, H[:, i // GROUP, i % GROUP, :], X[:, rb, i // GROUP, i % GROUP, :], one, i).then_inc(h_ready, 1)
                        act.wait_ge(var2_ready, r * GT + GT)
                        layer_norm_std(act, two, keep["eps"]).then_inc(std2_ready, 1)
                        act.wait_ge(norm2_ready, r + 1)
                        for i in range(GT):
                            g = G[:, rb, i // GROUP, i % GROUP, :]
                            act.activation(g, g, ACT.Identity, bias=two["shift"][:, i:i + 1],
                                           scale=two["rstd"][:, i:i + 1]).then_inc(n_ready, 1)

            @block.vector
            def _(dve):
                dve.wait_ge(w_loaded, 32)
                with dve.Fori(0, NR // 2) as q:
                    for rb in range(2):
                        r = q * 2 + rb
                        dve.wait_ge(x_loaded[rb], q * 32 + 32)
                        layer_norm_stats(dve, tiles(X[:, rb, :, :, :]), one, ln_step, r * 9, var_ready)
                        dve.wait_ge(std_ready, r + 1)
                        layer_norm_scale(dve, one, ln_step, r * 9 + 9, norm_ready)
                        dve.wait_ge(run_loaded[rb], q * 128 + 128)
                        for i in range(GT):
                            g = G[:, rb, i // GROUP, i % GROUP, :]
                            dve.wait_ge(h_ready, r * GT + (i + 1))
                            dve.scalar_tensor_tensor(out=g, in0=g, scalar=keep["has"][:, bass.ds(r * GT + i, 1)],
                                                     in1=H[:, i // GROUP, i % GROUP, :], op0=ALU.mult, op1=ALU.add
                                                     ).then_inc(added, 1)
                        dve.wait_ge(added, r * GT + GT)
                        layer_norm_stats(dve, tiles(G[:, rb, :, :, :]), two, ln2_step, r * 9, var2_ready)
                        dve.wait_ge(std2_ready, r + 1)
                        layer_norm_scale(dve, two, ln2_step, r * 9 + 9, norm2_ready)
                        dve.wait_ge(stored, r * 32)
                        dve.tensor_copy(O[:, :, :, F:XW].rearrange("p b j c -> p (b j) c"),
                                        over(keep["dis"][:, bass.ds(r * GT, GT)].unsqueeze(2), [P, GT, XW - F])).then_inc(times_gamma, 1)
                        for i in range(GT):
                            g = G[:, rb, i // GROUP, i % GROUP, :]
                            dve.wait_ge(n_ready, r * GT + (i + 1))
                            dve.tensor_tensor(g, g, gamma[:, :], ALU.mult).then_inc(times_gamma, 1)
                        for i in range(GT):
                            g = G[:, rb, i // GROUP, i % GROUP, :]
                            if i % GROUP == 0:
                                dve.wait_ge(res_ready, r * 2 + (i // GROUP + 1))
                            dve.wait_ge(times_gamma, r * 9 + (i + 2))
                            dve.tensor_tensor(O[:, i // GROUP, i % GROUP, 0:F], g, X[:, rb, i // GROUP, i % GROUP, :],
                                              ALU.add).then_inc(out_ready, 2)


def layer2_edges(nc, core, a, keep, x2, T2):
    sem = core.sem
    idx_staged, go = sem("f_idx"), sem("f_go")
    x_loaded = [sem("f_x0"), sem("f_x1")]
    ln_step, var_ready, std_ready, norm_ready = (sem("f_" + n) for n in ("lnstep", "var", "std", "norm"))
    init, filled, row_ready, carry_ready, match_ready, sum_ready = (sem("f_" + n) for n in ("init", "fill", "row", "carry", "match", "sum"))
    out0, out1, stored = sem("f_out0"), sem("f_out1"), [sem("f_st0"), sem("f_st1")]
    GT = 2 * GROUP
    W = F + 2
    LW = (GW, GW + 2)
    with ExitStack() as st:
        sb = lambda n, s, d=F32: core.sb(st, "f_" + n, s, d)
        X = sb("X", [P, 2, 2, GROUP, XW])
        idx = sb("idx", [P, GT], I32)
        stt = core.stats(st, "f")
        Y = sb("Y", [P, 2, W])
        carry = sb("carry", [1, W])
        match = sb("match", [P, GT, P])
        T = sb("T", [P, 2, W])
        s = core.ps(st, "f_s_ps", [P, 4, 512])
        with nc.Block() as block:
            @block.sync
            def _(sp):
                with sp.Fori(0, ET // 2) as r:
                    for b in range(2):
                        sp.wait_ge(out0, r * 2 + (b + 1))
                        sp.wait_ge(out1, r * 2 + (b + 1))
                        sp.dma_start(T2[bass.ds((r * 2 + b) * P, P), :], T[:, b, :]).then_inc(stored[b], 16)
                for b in range(2):
                    sp.wait_ge(stored[b], 16 * (ET // 2))

            @block.gpsimd
            def _(pool):
                def gather(r, rb, before):
                    pool.tensor_copy(idx[:, :], keep["src"][:, bass.ds(r * GT, GT)]).then_inc(idx_staged, 1)
                    pool.wait_ge(idx_staged, r + 1)
                    pool.wait_ge(sum_ready, before)
                    pool.sem_inc(go, 1)
                    for i in range(GT):
                        pool.indirect_dma_start(X[:, rb, i // GROUP, i % GROUP, :], None, x2[:, :],
                                                bass.IndirectOffsetOnAxis(idx[:, i:i + 1], 0),
                                                bounds_check=ROWS_N - 1, oob_is_err=False).then_inc(x_loaded[rb], 16)

                gather(0, 0, 0)
                pool.wait_ge(x_loaded[0], 128)
                with pool.Fori(0, 2) as q:
                    for k in range(2):
                        rb = 1 - k
                        gather(q * 2 + (k + 1), rb, q * 16 + 8 * k)
                        pool.wait_ge(x_loaded[rb], q * 128 + (128 if rb else 256))
                        pool.sem_inc(go, 1)

            @block.scalar
            def _(act):
                act.wait_ge(init, 1)

                def round_(r, rb, n):
                    act.wait_ge(var_ready, r * GT + GT)
                    layer_norm_std(act, stt, keep["eps"]).then_inc(std_ready, 1)
                    act.wait_ge(norm_ready, r + 1)
                    for i in range(GT):
                        b = i % 2
                        t = r * GT + i
                        x = X[:, rb, i // GROUP, i % GROUP, :]
                        act.wait_ge(out1, t)
                        relu_norm(act, Y[:, b, 0:F], x[:, 0:F], stt, i).then_inc(filled, 1)
                        act.copy(Y[:, b, F:W], x[:, F:W]).then_inc(filled, 1)
                        act.wait_ge(filled, t * 2 + 2)
                        act.wait_ge(carry_ready, t * 2)
                        act.copy(Y[0:1, b, :], carry[0:1, :]).then_inc(row_ready, 1)
                        act.wait_ge(sum_ready, t + 1)
                        act.wait_ge(row_ready, t + 1)
                        for h in range(2):
                            act.copy(carry[0:1, GW * h:GW * h + LW[h]], s[0:1, 2 * b + h, 0:LW[h]]).then_inc(carry_ready, 1)
                        act.wait_ge(stored[b], r * 64 + 16 * (i // 2))
                        act.copy(T[:, b, 0:GW], s[:, 2 * b, 0:GW]).then_inc(out0, 1)

                with act.Fori(0, 2) as q:
                    for rb in range(2):
                        round_(q * 2 + rb, rb, 0)
                round_(ER - 1, 0, 0)

            @block.vector
            def _(dve):
                dve.memset(carry[:, :], 0.0).then_inc(init, 1)

                def round_(r, rb, q):
                    dve.wait_ge(x_loaded[rb], q * 128 + 128)
                    layer_norm_stats(dve, tiles(X[:, rb, :, :, :]), stt, ln_step, r * 10, var_ready)
                    dve.wait_ge(std_ready, r + 1)
                    layer_norm_scale(dve, stt, ln_step, r * 10 + 9, norm_ready,
                                     X[:, rb, :, :, F:F + 1].rearrange("p b j c -> p (b j c)"))
                    dve.tensor_tensor(match[:, :, :], keep["rows"][:, bass.ds(r * (GT * P), GT * P)].rearrange("p (j q) -> p j q", q=P),
                                      over(keep["dst"][:, bass.ds(r * GT, GT)].unsqueeze(2), [P, GT, P]),
                                      ALU.is_equal).then_inc(match_ready, 1)
                    for i in range(GT):
                        t = r * GT + i
                        dve.wait_ge(carry_ready, t * 2 + 2)
                        dve.wait_ge(stored[i % 2], r * 64 + 16 * (i // 2))
                        dve.tensor_copy(T[:, i % 2, GW:W], s[:, 2 * (i % 2) + 1, 0:GW + 2]).then_inc(out1, 1)

                with dve.Fori(0, 2) as q:
                    for rb in range(2):
                        round_(q * 2 + rb, rb, q)
                round_(ER - 1, 0, 2)

            @block.tensor
            def _(pe):
                with pe.Fori(0, ER) as r:
                    pe.wait_ge(match_ready, r + 1)
                    for i in range(GT):
                        b = i % 2
                        t = r * GT + i
                        pe.wait_ge(row_ready, t + 1)
                        for h in range(2):
                            mm = pe.matmul(s[:, 2 * b + h, 0:LW[h]], match[:, i, :], Y[:, b, GW * h:GW * h + LW[h]],
                                           start=True, stop=True)
                        mm.then_inc(sum_ready, 1)


def layer2_nodes(nc, core, a, keep, x2, T2, x3):
    sem = core.sem
    w_loaded, w_hi, w_lo, init = sem("g_w"), sem("g_whi"), sem("g_wlo"), sem("g_init")
    idx_staged, go = sem("g_idx"), sem("g_go")
    x_loaded = [sem("g_x0"), sem("g_x1")]
    run_loaded = sem("g_run")
    ln_step, var_ready, std_ready, norm_ready, h_ready = (sem("g_" + n) for n in ("lnstep", "var", "std", "norm", "h"))
    a_ready, ns_step = sem("g_a"), sem("g_ns")
    tp_ready, tp_free, hT_hi = sem("g_tp"), sem("g_tpfree"), sem("g_hThi")
    o_ready, biased, out_ready, stored = sem("g_o"), sem("g_biased"), sem("g_out"), [sem("g_st0"), sem("g_st1")]
    GT = 2 * GROUP
    TW = F + 2
    with ExitStack() as st:
        sb = lambda n, s, d=F32: core.sb(st, "g_" + n, s, d)
        X = sb("X", [P, 2, 2, GROUP, XW])
        G = sb("G", [P, 2, GROUP, TW])
        H = sb("H", [P, 2, GROUP, F])
        V = sb("V", [P, 2, F])
        idx = sb("idx", [P, GT], I32)
        stt = core.stats(st, "g")
        ns = sb("ns", [P, 2, GT])
        hTh, hTl = sb("hTh", [P, 2, KF, GROUP * P], F32R), sb("hTl", [P, 2, KF, GROUP * P], F32R)
        Wraw = sb("Wraw", [P, KF, F])
        Wh, Wl = sb("Wh", [P, KF, F], F32R), sb("Wl", [P, KF, F], F32R)
        bias = sb("bias", [P, F])
        tp = core.ps(st, "g_tp_ps", [P, 2, 512])
        o = core.ps(st, "g_o_ps", [P, 4, 512])
        with nc.Block() as block:
            @block.sync
            def _(sp):
                def load(q, rb):
                    for b in range(2):
                        sp.dma_start(X[:, rb, b, :, :], group_rows(x2, q * 4 + (2 * rb + b), XW)).then_inc(x_loaded[rb], 16)

                load(0, 0)
                sp.dma_start(Wraw[:, :, :], a["W2nT"].rearrange("(k p) n -> p k n", p=P)).then_inc(w_loaded, 16)
                sp.dma_start(bias[:, :], a["L2_gnn_b"].rearrange("(o n) -> o n", o=1).broadcast_to([P, F])).then_inc(w_loaded, 16)
                load(0, 1)

                def store(q, rb):
                    for b in range(2):
                        sp.wait_ge(out_ready, q * 16 + (8 * rb + 4 * b + 4))
                        sp.dma_start(group_rows(x3, q * 4 + (2 * rb + b), F), X[:, rb, b, :, 0:F]).then_inc(stored[rb], 16)

                with sp.Fori(0, NR // 2 - 1) as q:
                    for rb in range(2):
                        store(q, rb)
                        sp.wait_ge(stored[rb], q * 32 + 32)
                        load(q + 1, rb)
                for rb in range(2):
                    store(NR // 2 - 1, rb)
                    if rb == 0:
                        sp.wait_ge(stored[0], 16 * NR)
                        load(0, 0)
                sp.wait_ge(stored[0], 16 * NR)
                sp.wait_ge(stored[1], 16 * NR)
                sp.wait_ge(x_loaded[0], 16 * NR + 32)

            @block.gpsimd
            def _(pool):
                pool.memset(G[:, :, :, :], 0.0).then_inc(init, 1)
                pool.wait_ge(init, 1)
                with pool.Fori(0, NR) as r:
                    pool.tensor_copy(idx[:, :], keep["slot"][:, bass.ds(r * GT, GT)]).then_inc(idx_staged, 1)
                    pool.wait_ge(idx_staged, r + 1)
                    pool.wait_ge(a_ready, r * GT)
                    pool.wait_ge(ns_step, r * 2)
                    pool.sem_inc(go, 1)
                    for i in range(GT):
                        pool.indirect_dma_start(G[:, i // GROUP, i % GROUP, :], None, T2[:, :],
                                                bass.IndirectOffsetOnAxis(idx[:, i:i + 1], 0),
                                                bounds_check=ROWS_E - 1, oob_is_err=False).then_inc(run_loaded, 16)
                    pool.wait_ge(run_loaded, r * 128 + 128)
                    pool.sem_inc(go, 1)

            @block.scalar
            def _(act):
                def norm(r, rb):
                    act.wait_ge(var_ready, r * GT + GT)
                    layer_norm_std(act, stt, keep["eps"]).then_inc(std_ready, 1)
                    act.wait_ge(norm_ready, r + 1)
                    act.wait_ge(a_ready, r * GT)
                    act.wait_ge(tp_ready, r * GT)
                    for i, x in enumerate(tiles(X[:, rb, :, :, :])):
                        relu_norm(act, H[:, i // GROUP, i % GROUP, :], x, stt, i).then_inc(h_ready, 1)

                norm(0, 0)
                split_on_act(act, Wraw[:, :, :], Wh[:, :, :], w_loaded, 32, w_hi)
                with act.Fori(0, NR // 2) as q:
                    for rb in range(2):
                        r = q * 2 + rb
                        for b in range(2):
                            for c in range(KF):
                                k = KF * b + c
                                act.wait_ge(tp_ready, r * GT + (k + 1))
                                act.copy(hTh[:, b, c, :], tp[:, k % 2, :]).then_inc(hT_hi, 1)
                        norm(r + 1, 1 - rb)

            @block.vector
            def _(dve):
                def norm(r, rb, loaded):
                    dve.wait_ge(x_loaded[rb], loaded)
                    layer_norm_stats(dve, tiles(X[:, rb, :, :, :]), stt, ln_step, r * 10, var_ready)
                    dve.wait_ge(std_ready, r + 1)
                    layer_norm_scale(dve, stt, ln_step, r * 10 + 9, norm_ready,
                                     keep["dis2"][:, bass.ds(r * GT, GT)])

                norm(0, 0, 32)
                split_on_dve(dve, Wraw[:, :, :], Wh[:, :, :], Wl[:, :, :], w_hi, 1, w_lo)
                with dve.Fori(0, NR // 2) as q:
                    for rb in range(2):
                        r = q * 2 + rb
                        dve.wait_ge(run_loaded, r * 128 + 128)
                        nsr = ns[:, rb, :]
                        dve.tensor_tensor(nsr, G[:, :, :, F:F + 1].rearrange("p b j c -> p (b j c)"),
                                          keep["dish"][:, bass.ds(r * GT, GT)], ALU.mult).then_inc(ns_step, 1)
                        dve.wait_ge(ns_step, r * 2 + 1)
                        dve.tensor_tensor(nsr, nsr, keep["dis2"][:, bass.ds(r * GT, GT)], ALU.add).then_inc(ns_step, 1)
                        for i in range(GT):
                            h = H[:, i // GROUP, i % GROUP, :]
                            dve.wait_ge(h_ready, r * GT + (i + 1))
                            dve.scalar_tensor_tensor(out=h, in0=G[:, i // GROUP, i % GROUP, 0:F],
                                                     scalar=keep["dish"][:, bass.ds(r * GT + i, 1)], in1=h,
                                                     op0=ALU.mult, op1=ALU.add).then_inc(a_ready, 1)
                        for b in range(2):
                            for c in range(KF):
                                k = KF * b + c
                                dve.wait_ge(hT_hi, r * GT + (k + 1))
                                dve.tensor_tensor(hTl[:, b, c, :], tp[:, k % 2, :], hTh[:, b, c, :].bitcast(F32),
                                                  ALU.subtract).then_inc(tp_free, 1)
                        norm(r + 1, 1 - rb, q * 32 + (64 if rb else 32))
                        dve.wait_ge(ns_step, r * 2 + 2)
                        for i in range(GT):
                            x = X[:, rb, i // GROUP, i % GROUP, 0:F]
                            dve.wait_ge(o_ready, r * GT + (i + 1))
                            if i >= 2:
                                dve.wait_ge(out_ready, r * GT + (i - 1))
                            dve.scalar_tensor_tensor(out=V[:, i % 2, :], in0=bias[:, :], scalar=ns[:, rb, i:i + 1],
                                                     in1=o[:, i % 4, :], op0=ALU.mult, op1=ALU.add).then_inc(biased, 1)
                            dve.wait_ge(biased, r * GT + (i + 1))
                            dve.scalar_tensor_tensor(out=x, in0=V[:, i % 2, :], scalar=0.0, in1=x, op0=ALU.max, op1=ALU.add
                                                     ).then_inc(out_ready, 1)

            @block.tensor
            def _(pe):
                pe.sem_inc(tp_free, 2)
                pe.wait_ge(w_lo, 1)
                with pe.Fori(0, NR) as r:
                    for b in range(2):
                        pe.wait_ge(a_ready, r * GT + (GROUP * b + GROUP))
                        for c in range(KF):
                            k = KF * b + c
                            pe.wait_ge(tp_free, r * GT + (k + 1))
                            for j in range(GROUP):
                                mm = pe.transpose(tp[:, k % 2, j * P:(j + 1) * P], H[:, b, j, c * P:(c + 1) * P], keep["ident"][:, :])
                            mm.then_inc(tp_ready, 1)
                    for b in range(2):
                        pe.wait_ge(tp_free, r * GT + (KF * b + KF + 2))
                        for j in range(GROUP):
                            i = GROUP * b + j
                            if i < 4:
                                pe.wait_ge(biased, r * GT)
                            else:
                                pe.wait_ge(biased, r * GT + (i - 3))
                            for c in range(KF):
                                mm = three(pe, o[:, i % 4, :], (hTh[:, b, c, j * P:(j + 1) * P], hTl[:, b, c, j * P:(j + 1) * P]),
                                           (Wh[:, c, :], Wl[:, c, :]), c == 0, c == KF - 1)
                            mm.then_inc(o_ready, 1)


def layer3_edges(nc, core, a, keep, x3, T3):
    sem = core.sem
    w_loaded, w_hi, w_lo, const_ready, const_out, init = (sem("h_" + n) for n in ("w", "whi", "wlo", "const", "constout", "init"))
    idx_staged, go = sem("h_idx"), sem("h_go")
    x_loaded = [sem("h_x0"), sem("h_x1")]
    ln_step, var_ready, std_ready, norm_ready, h_ready = (sem("h_" + n) for n in ("lnstep", "var", "std", "norm", "h"))
    tp_ready, tp_free, hT_hi = sem("h_tp"), sem("h_tpfree"), sem("h_hThi")
    m_ready, m_out, match_ready = sem("h_m"), sem("h_mout"), sem("h_match")
    row_ready, next_ready, carry_ready, sum_ready, sum_out = (sem("h_" + n) for n in ("row", "next", "carry", "sum", "sumout"))
    z_ready, z_out, stored = sem("h_z"), sem("h_zout"), [sem("h_st0"), sem("h_st1")]
    D = FE
    with ExitStack() as st:
        sb = lambda n, s, d=F32: core.sb(st, "h_" + n, s, d)
        X = sb("X", [P, 2, GROUP, F])
        idx = sb("idx", [P, GROUP], I32)
        stt = core.stats(st, "h")
        hTh, hTl = sb("hTh", [P, KF, GROUP * P], F32R), sb("hTl", [P, KF, GROUP * P], F32R)
        Wraw, Wh, Wl = sb("Wraw", [P, KF, D]), sb("Wh", [P, KF, D], F32R), sb("Wl", [P, KF, D], F32R)
        Wf = sb("Wf", [P, F])
        bg, bgw = sb("bg", [P, 1]), sb("bgw", [P, P])
        bf, const = sb("bf", [P, F]), sb("const", [P, F])
        Y = sb("Y", [P, GROUP, D])
        carry = sb("carry", [1, D])
        match = sb("match", [P, GROUP, P])
        S = sb("S", [P, GROUP * P])
        Z = sb("Z", [P, 2, F])
        tp = core.ps(st, "h_tp_ps", [P, 2, 512])
        m = core.ps(st, "h_m_ps", [P, 512])
        sT = core.ps(st, "h_s_ps", [P, 512])
        nx = core.ps(st, "h_nx_ps", [P, 512])
        z = core.ps(st, "h_z_ps", [P, 2, 512])
        with nc.Block() as block:
            @block.sync
            def _(sp):
                sp.dma_start(Wraw[:, :, :], a["L3_gnn_W_gcn"].rearrange("(k p) n -> p k n", p=P)).then_inc(w_loaded, 16)
                sp.dma_start(Wf[:, :], a["WfT"]).then_inc(w_loaded, 16)
                sp.dma_start(bg[:, :], a["L3_gnn_b_gcn"].rearrange("(p o) -> p o", o=1)).then_inc(w_loaded, 16)
                sp.dma_start(bf[:, :], a["L3_gnn_b_fc"].rearrange("(o n) -> o n", o=1).broadcast_to([P, F])).then_inc(w_loaded, 16)
                with sp.Fori(0, ET // 2) as r:
                    for b in range(2):
                        sp.wait_ge(z_out, r * 2 + (b + 1))
                        sp.dma_start(T3[bass.ds((r * 2 + b) * P, P), :], Z[:, b, :]).then_inc(stored[b], 16)
                for b in range(2):
                    sp.wait_ge(stored[b], 16 * (ET // 2))

            @block.gpsimd
            def _(pool):
                with pool.Fori(0, ER) as r:
                    for b in range(2):
                        g = r * 2 + b
                        pool.tensor_copy(idx[:, :], keep["src"][:, bass.ds(g * GROUP, GROUP)]).then_inc(idx_staged, 1)
                        pool.wait_ge(idx_staged, g + 1)
                        pool.wait_ge(tp_ready, r * 8 + (4 * b))
                        pool.sem_inc(go, 1)
                        for i in range(GROUP):
                            pool.indirect_dma_start(X[:, b, i, :], None, x3[:, :], bass.IndirectOffsetOnAxis(idx[:, i:i + 1], 0),
                                                    bounds_check=ROWS_N - 1, oob_is_err=False).then_inc(x_loaded[b], 16)
                        pool.wait_ge(x_loaded[b], r * 64 + 64)
                        pool.sem_inc(go, 1)

            @block.scalar
            def _(act):
                split_on_act(act, Wraw[:, :, :], Wh[:, :, :], w_loaded, 64, w_hi)
                act.wait_ge(init, 1)
                with act.Fori(0, ER) as r:
                    for b in range(2):
                        g = r * 2 + b
                        act.wait_ge(var_ready, r * 8 + (4 * b + 4))
                        act.activation(stt["std"][:, 0:GROUP], stt["mv"][:, 0:GROUP, 1], ACT.Sqrt, bias=keep["eps"][:, 0:1]).then_inc(std_ready, 1)
                        act.wait_ge(norm_ready, g + 1)
                        for i in range(GROUP):
                            relu_norm(act, X[:, b, i, :], X[:, b, i, :], stt, i).then_inc(h_ready, 1)
                        act.wait_ge(m_ready, g)
                        for c in range(KF):
                            act.wait_ge(tp_ready, r * 8 + (4 * b + c + 1))
                            act.copy(hTh[:, c, :], tp[:, c % 2, :]).then_inc(hT_hi, 1)
                        act.wait_ge(m_out, g + 1)
                        for j in range(GROUP):
                            t = r * 8 + (4 * b + j)
                            act.wait_ge(carry_ready, t)
                            act.copy(Y[0:1, j, :], carry[0:1, :]).then_inc(row_ready, 1)
                            act.wait_ge(next_ready, t + 1)
                            act.wait_ge(row_ready, t + 1)
                            act.copy(carry[0:1, :], nx[0:1, 0:D]).then_inc(carry_ready, 1)
                        act.wait_ge(sum_ready, g + 1)
                        act.wait_ge(z_ready, r * 8 + 4 * b)
                        act.copy(S[:, :], sT[:, :]).then_inc(sum_out, 1)

            @block.vector
            def _(dve):
                dve.memset(carry[:, :], 0.0).then_inc(init, 1)
                split_on_dve(dve, Wraw[:, :, :], Wh[:, :, :], Wl[:, :, :], w_hi, 1, w_lo)
                dve.tensor_copy(bgw[:, :], over(bg[:, 0:1], [P, P])).then_inc(w_lo, 1)
                dve.wait_ge(const_ready, 1)
                dve.tensor_tensor(const[:, :], z[:, 0, :], bf[:, :], ALU.add).then_inc(const_out, 1)
                with dve.Fori(0, ER) as r:
                    for b in range(2):
                        g = r * 2 + b
                        dve.wait_ge(x_loaded[b], r * 64 + 64)
                        for i in range(GROUP):
                            dve.bn_stats(stt["raw"][:, i, :], X[:, b, i, :]).then_inc(ln_step, 1)
                        dve.wait_ge(ln_step, r * 10 + (5 * b + 4))
                        dve.sem_inc(stt["go"], 1)
                        for i in range(GROUP):
                            dve.bn_aggr(stt["mv"][:, i, :], stt["raw"][:, i, :]).then_inc(var_ready, 1)
                        dve.wait_ge(std_ready, g + 1)
                        dve.reciprocal(stt["rstd"][:, 0:GROUP], stt["std"][:, 0:GROUP]).then_inc(ln_step, 1)
                        dve.wait_ge(ln_step, r * 10 + (5 * b + 5))
                        dve.scalar_tensor_tensor(out=stt["shift"][:, 0:GROUP], in0=stt["mv"][:, 0:GROUP, 0], scalar=-1.0,
                                                 in1=stt["rstd"][:, 0:GROUP], op0=ALU.mult, op1=ALU.mult).then_inc(norm_ready, 1)
                        for c in range(KF):
                            dve.wait_ge(hT_hi, r * 8 + (4 * b + c + 1))
                            dve.tensor_tensor(hTl[:, c, :], tp[:, c % 2, :], hTh[:, c, :].bitcast(F32), ALU.subtract).then_inc(tp_free, 1)
                        dve.wait_ge(sum_ready, g)
                        t = r * 8 + 4 * b
                        dve.tensor_tensor(match[:, :, :], keep["rows"][:, bass.ds(t * P, GROUP * P)].rearrange("p (j q) -> p j q", q=P),
                                          over(keep["dst"][:, bass.ds(t, GROUP)].unsqueeze(2), [P, GROUP, P]),
                                          ALU.is_equal).then_inc(match_ready, 1)
                        dve.wait_ge(m_ready, g + 1)
                        dve.tensor_tensor(Y[:, :, :], m[:, :].rearrange("p (j d) -> p j d", d=D),
                                          over(keep["wgt"][:, bass.ds(t, GROUP)].unsqueeze(2), [P, GROUP, D]),
                                          ALU.mult).then_inc(m_out, 1)
                        for j in range(GROUP):
                            dve.wait_ge(z_ready, t + (j + 1))
                            dve.wait_ge(stored[j % 2], r * 64 + 32 * b + 16 * (j // 2))
                            dve.tensor_tensor(Z[:, j % 2, :], z[:, j % 2, :], const[:, :], ALU.add).then_inc(z_out, 1)

            @block.tensor
            def _(pe):
                pe.wait_ge(w_lo, 2)
                pe.matmul(z[:, 0, :], bgw[:, :], Wf[:, :], start=True, stop=True).then_inc(const_ready, 1)
                pe.wait_ge(const_out, 1)
                pe.sem_inc(tp_free, 2)
                with pe.Fori(0, ER) as r:
                    for b in range(2):
                        g = r * 2 + b
                        pe.wait_ge(h_ready, r * 8 + (4 * b + 4))
                        for c in range(KF):
                            pe.wait_ge(tp_free, r * 8 + (4 * b + c + 1))
                            for j in range(GROUP):
                                mm = pe.transpose(tp[:, c % 2, j * P:(j + 1) * P], X[:, b, j, c * P:(c + 1) * P], keep["ident"][:, :])
                            mm.then_inc(tp_ready, 1)
                        pe.wait_ge(tp_free, r * 8 + (4 * b + 4 + 2))
                        pe.wait_ge(m_out, g)
                        for j in range(GROUP):
                            for c in range(KF):
                                mm = three(pe, m[:, j * D:(j + 1) * D], (hTh[:, c, j * P:(j + 1) * P], hTl[:, c, j * P:(j + 1) * P]),
                                           (Wh[:, c, :], Wl[:, c, :]), c == 0, c == KF - 1)
                        mm.then_inc(m_ready, 1)
                        pe.wait_ge(match_ready, g + 1)
                        for j in range(GROUP):
                            t = r * 8 + (4 * b + j)
                            pe.wait_ge(row_ready, t + 1)
                            pe.wait_ge(carry_ready, t)
                            pe.matmul(nx[0:1, 0:D], match[:, j, 0:1], Y[:, j, :], start=True, stop=True).then_inc(next_ready, 1)
                            if j == 0:
                                pe.wait_ge(sum_out, g)
                            mm = pe.matmul(sT[:, j * P:(j + 1) * P], Y[:, j, :], match[:, j, :], start=True, stop=True)
                        mm.then_inc(sum_ready, 1)
                        pe.wait_ge(sum_out, g + 1)
                        for j in range(GROUP):
                            t = r * 8 + (4 * b + j)
                            if j >= 2:
                                pe.wait_ge(z_out, t - 1)
                            else:
                                pe.wait_ge(z_out, r * 8 + 4 * b)
                            pe.matmul(z[:, j % 2, :], S[:, j * P:(j + 1) * P], Wf[:, :], start=True, stop=True).then_inc(z_ready, 1)


def layer3_nodes(nc, core, a, keep, x3, T3, out):
    sem = core.sem
    w_loaded, wide, const_ready, const_out = sem("i_w"), sem("i_wide"), sem("i_const"), sem("i_constout")
    idx_staged, go, filled = sem("i_idx"), sem("i_go"), sem("i_fill")
    x_loaded, run_loaded, stored = ([sem(f"i_{n}{b}") for b in range(2)] for n in ("x", "g", "st"))
    out_ready = sem("i_out")
    with ExitStack() as st:
        sb = lambda n, s, d=F32: core.sb(st, "i_" + n, s, d)
        X = sb("X", [P, 2, GROUP, F])
        G = sb("G", [P, 2, GROUP, F])
        idx = sb("idx", [P, 2, GROUP], I32)
        Wf, bf, const = sb("Wf", [P, F]), sb("bf", [P, F]), sb("const", [P, F])
        bg, bgw = sb("bg", [P, 1]), sb("bgw", [P, P])
        z = core.ps(st, "i_z_ps", [P, 512])
        with nc.Block() as block:
            @block.sync
            def _(sp):
                sp.dma_start(Wf[:, :], a["WfT"]).then_inc(w_loaded, 16)
                sp.dma_start(bg[:, :], a["L3_gnn_b_gcn"].rearrange("(p o) -> p o", o=1)).then_inc(w_loaded, 16)
                sp.dma_start(bf[:, :], a["L3_gnn_b_fc"].rearrange("(o n) -> o n", o=1).broadcast_to([P, F])).then_inc(w_loaded, 16)
                with sp.Fori(0, NR) as r:
                    for b in range(2):
                        sp.wait_ge(stored[b], r * 16)
                        sp.dma_start(X[:, b, :, :], group_rows(x3, r * 2 + b, F)).then_inc(x_loaded[b], 16)

            @block.gpsimd
            def _(pool):
                with pool.Fori(0, NR) as r:
                    for b in range(2):
                        g = r * 2 + b
                        pool.wait_ge(run_loaded[b], r * 64)
                        pool.sem_inc(go, 1)
                        pool.tensor_copy(idx[:, b, :], keep["slot"][:, bass.ds(g * GROUP, GROUP)]).then_inc(idx_staged, 1)
                        pool.wait_ge(idx_staged, g + 1)
                        pool.wait_ge(filled, g + 1)
                        pool.sem_inc(go, 1)
                        for i in range(GROUP):
                            pool.indirect_dma_start(G[:, b, i, :], None, T3[:, :], bass.IndirectOffsetOnAxis(idx[:, b, i:i + 1], 0),
                                                    bounds_check=ROWS_E - 1, oob_is_err=False).then_inc(run_loaded[b], 16)

            @block.scalar
            def _(act):
                def fill(b):
                    act.copy(G[:, b, :, :], over(const[:, :].unsqueeze(1), [P, GROUP, F])).then_inc(filled, 1)

                act.wait_ge(const_out, 1)
                fill(0)
                fill(1)
                with act.Fori(0, NR - 1) as r:
                    for b in range(2):
                        act.wait_ge(out_ready, r * 2 + (b + 1))
                        act.dma_start(group_rows(out, r * 2 + b, F), X[:, b, :, :]).then_inc(stored[b], 16)
                        fill(b)
                act.wait_ge(out_ready, NG - 1)
                act.dma_start(group_rows(out, NG - 2, F), X[:, 0, :, :]).then_inc(stored[0], 16)
                act.wait_ge(out_ready, NG)
                at = (NG - 1) * GROUP * P
                for j in range((NODES - at + P - 1) // P):
                    n = min(P, NODES - at - j * P)
                    act.dma_start(out[at + j * P:at + j * P + n, :], X[0:n, 1, j, :]).then_inc(stored[1], 16)
                act.wait_ge(stored[0], 16 * NR)
                act.wait_ge(stored[1], 16 * (NR - 1) + 48)

            @block.vector
            def _(dve):
                dve.wait_ge(w_loaded, 48)
                dve.tensor_copy(bgw[:, :], over(bg[:, 0:1], [P, P])).then_inc(wide, 1)
                dve.wait_ge(const_ready, 1)
                dve.tensor_tensor(const[:, :], z[:, :], bf[:, :], ALU.add).then_inc(const_out, 1)
                with dve.Fori(0, NR) as r:
                    for b in range(2):
                        dve.wait_ge(x_loaded[b], r * 16 + 16)
                        dve.wait_ge(run_loaded[b], r * 64 + 64)
                        dve.tensor_tensor(X[:, b, :, :], X[:, b, :, :], G[:, b, :, :], ALU.add).then_inc(out_ready, 1)

            @block.tensor
            def _(pe):
                pe.wait_ge(wide, 1)
                pe.matmul(z[:, :], bgw[:, :], Wf[:, :], start=True, stop=True).then_inc(const_ready, 1)


def program(nc, a, out, stop_after=9):
    core = Core(nc)
    with core.whole:
        outer = core.whole
        keep = {
            "src": core.sb(outer, "src", [P, ET + 2 * GROUP], I32), "dst": core.sb(outer, "dstk", [P, ET + 2 * GROUP], I32),
            "rows": core.sb(outer, "rows", [P, ROWS_E], U16), "fac": core.sb(outer, "fac", [P, ET, HEADS]),
            "wgt": core.sb(outer, "wgt", [P, ET]), "ident": core.sb(outer, "ident", [P, P]), "eps": core.sb(outer, "eps", [P, 1]),
            "slot": core.sb(outer, "slot", [P, NT + 8], I32),
        }
        for n in ("dis", "dis2", "has", "dish"):
            keep[n] = core.sb(outer, n, [P, NT + 8])

        def table(name, rows, width, last):
            return out if last == stop_after else nc.dram_tensor(name, (rows, width), F32).ap()

        T0 = table("T0", ROWS_E, IN, 1)
        x1 = table("x1", ROWS_N, F, 2)
        T1 = table("T1", ROWS_E, F, 3)
        x2 = table("x2", ROWS_N, XW, 4)
        T2 = table("T2", ROWS_E, F + 2, 5)
        x3 = table("x3", ROWS_N, F, 6)
        T3 = table("T3", ROWS_E, F, 7)
        with ExitStack() as w:
            l0 = {"W1h": core.sb(w, "W1h", [P, KI, HID], F32R), "W1l": core.sb(w, "W1l", [P, KI, HID], F32R),
                  "W23h": core.sb(w, "W23h", [P, KH, IN], F32R), "W23l": core.sb(w, "W23l", [P, KH, IN], F32R),
                  "b1": core.sb(w, "b1", [P, KH]), "c2": core.sb(w, "c2", [P, IN])}
            core.run(prepare, a, keep, l0)
            core.run(spread_rows, a, keep)
            core.run(layer0_edges, a, keep, l0, T0)
        if stop_after >= 2:
            core.run(layer0_nodes, a, keep, T0, x1)
        if stop_after >= 3:
            with ExitStack() as w:
                msg = core.sb(w, "msg", [P, ET, F + HEADS])
                logit = core.sb(w, "logit", [P, ET, HEADS])
                core.run(layer1_messages, a, keep, x1, msg, logit)
                core.run(layer1_softmax, a, keep, logit)
                core.run(layer1_sums, a, keep, msg, logit, T1)
        if stop_after >= 4:
            core.run(layer1_nodes, a, keep, x1, T1, x2)
        if stop_after >= 5:
            core.run(layer2_edges, a, keep, x2, T2)
        if stop_after >= 6:
            core.run(layer2_nodes, a, keep, x2, T2, x3)
        if stop_after >= 7:
            core.run(layer3_edges, a, keep, x3, T3)
        if stop_after >= 8:
            core.run(layer3_nodes, a, keep, x3, T3, out)


def spread_rows(nc, core, a, keep):
    loaded, packed = core.sem("r_loaded"), core.sem("r_packed")
    with ExitStack() as st:
        raw = core.sb(st, "r_raw", [P, ROWS_E // 4], I32)
        with nc.Block() as block:
            @block.sync
            def _(sp):
                for q in range(4):
                    if q:
                        sp.wait_ge(packed, q)
                    sp.dma_start(raw[:, :], a["dst_row"][:, q * 1280:(q + 1) * 1280].broadcast_to([P, 1280])).then_inc(loaded, 16)

            @block.vector
            def _(dve):
                for q in range(4):
                    dve.wait_ge(loaded, 16 * (q + 1))
                    dve.tensor_copy(keep["rows"][:, q * 1280:(q + 1) * 1280], raw[:, :]).then_inc(packed, 1)


def windows(v, np, tiles, front, back):
    at = NEW * np.arange(tiles)[None, :] - 1 + np.arange(P)[:, None]
    w = np.concatenate([np.full((1,) + v.shape[1:], front, v.dtype), v,
                        np.full((tiles * P,) + v.shape[1:], back, v.dtype)])
    return np.ascontiguousarray(w[at + 1])


def lay_out(inputs, np):
    a = {}
    for n in ("x", "L1_gnn_et_emb", "L0_gnn_W1", "L0_gnn_b1", "L0_gnn_b2", "L0_gnn_W3", "L0_gnn_b3", "L0_gnn_W4", "L0_gnn_b4",
              "L1_gnn_W", "L1_gnn_a_src", "L1_gnn_a_dst", "L1_gnn_ln_gamma", "L1_gnn_ln_beta", "L2_gnn_b",
              "L3_gnn_W_gcn", "L3_gnn_b_gcn", "L3_gnn_b_fc"):
        a[n] = np.ascontiguousarray(inputs[n])
    a["W2T"] = np.ascontiguousarray(np.asarray(inputs["L0_gnn_W2"]).T)
    a["W1T"] = np.ascontiguousarray(np.asarray(inputs["L1_gnn_W"]).T)
    a["W2nT"] = np.ascontiguousarray(np.asarray(inputs["L2_gnn_W"]).T)
    a["WfT"] = np.ascontiguousarray(np.asarray(inputs["L3_gnn_W_fc"]).T)
    dst, src = np.asarray(inputs["dst"]), np.asarray(inputs["src"])
    dw = windows(dst, np, ET, NODES + 1, NODES)
    a["dst_win"] = dw
    a["dst_wide"] = windows(dst, np, ET + 2 * GROUP, NODES + 1, NODES)
    nxt = windows(dst, np, ET + 1, NODES + 1, NODES)
    after = np.concatenate([nxt[1:, :ET], nxt[1:2, 1:]])
    after[0] = dw[0]
    a["dst_next"] = np.ascontiguousarray(after)
    sw = windows(src, np, ET + 2 * GROUP, 0, 0)
    a["src_win"] = sw
    count = windows(src, np, ET, ROWS_N, ROWS_N)
    count[0] = ROWS_N
    a["src_count"] = count
    row = dw.T.copy()
    a["dst_flat"] = row.reshape(1, -1).copy()
    row[:, 0] = row[:, P - 1]
    a["dst_row"] = np.ascontiguousarray(row.reshape(1, -1))
    a["type_win"] = windows(np.asarray(inputs["edge_type_8"]), np, ET, 0, 0)
    a["weight_win"] = windows(np.asarray(inputs["edge_weight"]), np, ET, 0, 0)
    at = windows(np.asarray(inputs["edge_attr_128"]), np, ET + 2 * GROUP, 0, 0)
    a["attr_win"] = np.ascontiguousarray(at.reshape(P, EG + 2, GROUP, FE))
    return a


def kernel(**inputs):
    import numpy as _np
    import concourse.bacc as _bacc
    from concourse import mybir as _mybir
    from concourse.bass_utils import run_bass_kernel_spmd as _run

    nc = _bacc.Bacc("TRN2", target_bir_lowering=False, num_devices=1, dynamic_dma_scratch_size=8192)
    arrays = lay_out(inputs, _np)
    args = {n: nc.dram_tensor("in_" + n, v.shape, _mybir.dt.from_np(v.dtype), kind="ExternalInput").ap()
            for n, v in arrays.items()}
    out = nc.dram_tensor("out_0", (NODES, F), _mybir.dt.float32, kind="ExternalOutput").ap()
    program(nc, args, out)
    r = _run(nc, [{"in_" + n: v for n, v in arrays.items()}], core_ids=[0])
    return r.results[0]["out_0"]
```

```python
import concourse.bass as bass
from concourse import mybir
from contextlib import ExitStack

F32 = mybir.dt.float32
F32R = mybir.dt.float32r
I32 = mybir.dt.int32
U32 = mybir.dt.uint32
U16 = mybir.dt.uint16
ALU = mybir.AluOpType
ACT = mybir.ActivationFunctionType

P = 128
NODES = 10000
EDGES = 5000
F = 512
FE = 128
IN = F + FE
HID = 2 * IN
KF = F // P
KI = IN // P
KH = HID // P
HEADS = 8
HD = F // HEADS
GW = F // 2
HALF = IN // 2
GROUP = 4
NEW = P - 1
ET = 40
EG = ET // GROUP
ER = EG // 2
NT = 80
NG = NT // GROUP
NR = NG // 2
ROWS_E = ET * P
ROWS_N = NT * P
EPS = 1e-5
XW = F + 4
FAR = 1.0e6
assert ET * NEW >= EDGES and NT * P >= NODES and (ET - 1) * NEW < EDGES


def group_rows(table, g, cols):
    return table[bass.ds(g * (GROUP * P), GROUP * P), 0:cols].rearrange("(j p) f -> p j f", p=P)


def tiles(x, width=F):
    return [x[:, i // GROUP, i % GROUP, 0:width] for i in range(2 * GROUP)]


def over(ap, shape):
    return ap.broadcast_to(shape)


def layer_norm_stats(dve, rows, st, steps, base, var_ready):
    for i, row in enumerate(rows):
        dve.bn_stats(st["raw"][:, i, :], row).then_inc(steps, 1)
    dve.wait_ge(steps, base + len(rows))
    dve.sem_inc(st["go"], 1)
    for i in range(len(rows)):
        dve.bn_aggr(st["mv"][:, i, :], st["raw"][:, i, :]).then_inc(var_ready, 1)


def layer_norm_std(act, st, eps):
    return act.activation(st["std"][:, :], st["mv"][:, :, 1], ACT.Sqrt, bias=eps[:, 0:1])


def layer_norm_scale(dve, st, steps, base, norm_ready, times=None):
    dve.reciprocal(st["rstd"][:, :], st["std"][:, :]).then_inc(steps, 1)
    dve.wait_ge(steps, base)
    if times is not None:
        dve.tensor_tensor(st["rstd"][:, :], st["rstd"][:, :], times, ALU.mult).then_inc(steps, 1)
        dve.wait_ge(steps, base + 1)
    dve.scalar_tensor_tensor(out=st["shift"][:, :], in0=st["mv"][:, :, 0], scalar=-1.0, in1=st["rstd"][:, :],
                             op0=ALU.mult, op1=ALU.mult).then_inc(norm_ready, 1)


def relu_norm(act, out, x, st, i):
    return act.activation(out, x, ACT.Relu, bias=st["shift"][:, i:i + 1], scale=st["rstd"][:, i:i + 1])


class Core:

    def __init__(self, nc):
        self.nc = nc
        self.whole = ExitStack()
        self.sems = []

    def run(self, build, *args):
        self.sems = []
        build(self.nc, self, *args)
        self.nc.clear_and_free_semaphores(self.sems)
        self.nc.all_engine_barrier()

    def sem(self, name):
        self.sems.append(self.nc.alloc_semaphore(name))
        return self.sems[-1]

    def sb(self, stack, name, shape, dt=F32):
        return stack.enter_context(self.nc.sbuf_tensor(name, shape, dt))

    def ps(self, stack, name, shape):
        return stack.enter_context(self.nc.psum_tensor(name, shape, F32))

    def stats(self, stack, name):
        return {"go": self.sem(name + "_lngo"), "raw": self.sb(stack, name + "_raw", [P, 2 * GROUP, 6]),
                "mv": self.sb(stack, name + "_mv", [P, 2 * GROUP, 2]),
                "std": self.sb(stack, name + "_std", [P, 2 * GROUP]),
                "rstd": self.sb(stack, name + "_rstd", [P, 2 * GROUP]),
                "shift": self.sb(stack, name + "_shift", [P, 2 * GROUP])}


def split_on_act(act, raw, hi, loaded, count, hi_done):
    act.wait_ge(loaded, count)
    act.copy(hi, raw).then_inc(hi_done, 1)


def split_on_dve(dve, raw, hi, lo, hi_done, count, lo_done):
    dve.wait_ge(hi_done, count)
    dve.tensor_tensor(lo, raw, hi.bitcast(F32), ALU.subtract).then_inc(lo_done, 1)


def three(pe, out, a, b, first, last):
    (ah, al), (bh, bl) = a, b
    pe.matmul(out, ah, bh, start=first, stop=False)
    pe.matmul(out, ah, bl, start=False, stop=False)
    return pe.matmul(out, al, bh, start=False, stop=last)


def prepare(nc, core, a, keep, l0):
    sem = core.sem
    idx_loaded, rows_loaded, small_loaded = sem("a_idx"), sem("a_rows"), sem("a_small")
    w1_loaded = [sem("a_w1l0"), sem("a_w1l1")]
    w2_loaded = [sem("a_w2l0"), sem("a_w2l1")]
    w3b_loaded = sem("a_w3b")
    iota_ready, zero_ready = sem("a_iota"), sem("a_zero")
    dve_step = sem("a_dve")
    onehot_ready, hist_read, hist_done = sem("a_onehot"), sem("a_hist_read"), sem("a_hist")
    count_ready, root_ready, = sem("a_count"), sem("a_root")
    w1_hi, w1_lo = sem("a_w1hi"), sem("a_w1lo")
    fold_ready, fold_hi, fold_lo = sem("a_fold"), sem("a_fold_hi"), sem("a_fold_lo")
    c2_ready, ident_ready = sem("a_c2"), sem("a_ident")
    FAC_K = HEADS

    with ExitStack() as st:
        sb = lambda n, s, d=F32: core.sb(st, "a_" + n, s, d)
        dst_i, nxt_i, src_i, typ_i = (sb(n, [P, ET], I32) for n in ("dst", "nxt", "src", "typ"))
        row_i = sb("rowi", [P, 2, GROUP * P], I32)
        wgt = sb("wgt", [P, ET])
        emb = sb("emb", [P, 8 * HEADS])
        hl = sb("hl", [P, 4, ET], I32)
        last = sb("last", [P, ET])
        val = sb("val", [P, ET])
        iota_i = sb("iotai", [P, P], I32)
        iota_f = sb("iotaf", [P, P])
        slot_i = sb("sloti", [P, ET], I32)
        pick = sb("pick", [P, ET])
        term = sb("term", [P, ET, HEADS])
        onehot = sb("onehot", [P, 4, GROUP, P])
        zeros = sb("zeros", [P, P])
        found = sb("found", [P, NT])
        W1raw = sb("W1raw", [P, 2, HID])
        W3b = sb("W3b", [P, KH, IN])
        W2m = sb("W2m", [P, 2, KH, P])
        b2c = sb("b2c", [P, KH])
        b2w = sb("b2w", [P, KH, P])
        root = sb("root", [P, NT])
        hist = core.ps(st, "a_hist_ps", [P, 2, 512])
        fold = core.ps(st, "a_fold_ps", [P, 4, 512])
        c2p = core.ps(st, "a_c2_ps", [P, 2, 512])

        with nc.Block() as block:
            @block.sync
            def _(sp):
                sp.dma_start(dst_i[:, :], a["dst_win"]).then_inc(idx_loaded, 16)
                sp.dma_start(nxt_i[:, :], a["dst_next"]).then_inc(idx_loaded, 16)
                sp.dma_start(src_i[:, :], a["src_count"]).then_inc(idx_loaded, 16)
                sp.dma_start(typ_i[:, :], a["type_win"]).then_inc(idx_loaded, 16)
                sp.dma_start(keep["src"][:, :], a["src_win"]).then_inc(idx_loaded, 16)
                sp.dma_start(keep["dst"][:, :], a["dst_wide"]).then_inc(idx_loaded, 16)
                sp.dma_start(wgt[:, :], a["weight_win"]).then_inc(small_loaded, 16)
                sp.dma_start(emb[:, :], a["L1_gnn_et_emb"].rearrange("(o k) h -> o (k h)", o=1).broadcast_to([P, 8 * HEADS])
                             ).then_inc(small_loaded, 16)
                sp.dma_start(b2c[:, :], a["L0_gnn_b2"].rearrange("(k p) -> p k", p=P),
                             allow_slow_non_contiguous=True).then_inc(small_loaded, 16)
                sp.dma_start(l0["b1"][:, :], a["L0_gnn_b1"].rearrange("(k p) -> p k", p=P),
                             allow_slow_non_contiguous=True).then_inc(small_loaded, 16)
                sp.dma_start(W3b[:, :, :], a["L0_gnn_W3"][F:F + HID, :].rearrange("(k p) n -> p k n", p=P)
                             ).then_inc(w3b_loaded, 16)
                for k in range(KI):
                    if k >= 2:
                        sp.wait_ge(w1_lo, k - 1)
                    sp.dma_start(W1raw[:, k % 2, :], a["L0_gnn_W1"][k * P:(k + 1) * P, :]).then_inc(w1_loaded[k % 2], 16)
                for k in range(2, KH):
                    sp.wait_ge(fold_ready, k - 1)
                    sp.dma_start(W2m[:, k % 2, :, :], a["W2T"][:, k * P:(k + 1) * P].rearrange("(k p) m -> p k m", p=P)
                                   ).then_inc(w2_loaded[k % 2], 16)

            @block.scalar
            def _(act):
                for k in range(2):
                    act.dma_start(W2m[:, k, :, :], a["W2T"][:, k * P:(k + 1) * P].rearrange("(k p) m -> p k m", p=P)
                                  ).then_inc(w2_loaded[k], 16)
                for k in range(KI):
                    act.wait_ge(w1_loaded[k % 2], 16 * (k // 2 + 1))
                    act.copy(l0["W1h"][:, k, :], W1raw[:, k % 2, :]).then_inc(w1_hi, 1)
                act.wait_ge(count_ready, 1)
                act.activation(root[:, :], found[:, :], ACT.Sqrt).then_inc(root_ready, 1)
                with act.Fori(0, KH // 2) as it:
                    for b in range(2):
                        act.wait_ge(fold_ready, it * 2 + (b + 1))
                        for h in range(2):
                            act.copy(l0["W23h"][:, it * 2 + b, h * HALF:(h + 1) * HALF],
                                     fold[:, 2 * b + h, 0:HALF]).then_inc(fold_hi, 1)

            @block.gpsimd
            def _(pool):
                pool.iota(iota_i[:, :], [[1, P]], base=0, channel_multiplier=0).then_inc(iota_ready, 1)
                pool.iota(slot_i[:, :], [[P, ET]], base=1, channel_multiplier=1).then_inc(iota_ready, 1)
                pool.memset(zeros[:, :], 0.0).then_inc(zero_ready, 1)
                pool.memset(keep["ident"][:, :], 1.0).then_inc(ident_ready, 1)
                pool.wait_ge(ident_ready, 1)
                pool.affine_select(out=keep["ident"][:, :], in_=keep["ident"][:, :], compare_op=ALU.is_equal, fill=0.0,
                                   base=0, pattern=[[-1, P]], channel_multiplier=1).then_inc(ident_ready, 1)

            @block.vector
            def _(dve):
                n = 0

                def step(ins):
                    nonlocal n
                    n += 1
                    ins.then_inc(dve_step, 1)
                    dve.wait_ge(dve_step, n)

                step(dve.memset(keep["eps"][:, :], EPS))
                dve.wait_ge(iota_ready, 2)
                dve.wait_ge(idx_loaded, 16 * 6)
                step(dve.tensor_copy(iota_f[:, :], iota_i[:, :]))
                for k, ids in enumerate((src_i, dst_i)):
                    step(dve.tensor_scalar(hl[:, 2 * k, :], ids[:, :], 127, None, ALU.bitwise_and))
                    step(dve.tensor_scalar(hl[:, 2 * k + 1, :], ids[:, :], 7, None, ALU.logical_shift_right))
                step(dve.tensor_tensor(last[:, :], dst_i[:, :], nxt_i[:, :], ALU.not_equal))
                step(dve.tensor_tensor(val[:, :], last[:, :], slot_i[:, :], ALU.mult))
                dve.wait_ge(small_loaded, 16 * 4)
                fac = keep["fac"][:, :, :]
                step(dve.memset(fac, 1.0))
                for k in range(FAC_K):
                    step(dve.tensor_scalar(pick[:, :], typ_i[:, :], float(k), None, ALU.is_equal))
                    step(dve.tensor_tensor(term[:, :, :], over(pick[:, :].unsqueeze(2), [P, ET, HEADS]),
                                           over(emb[:, k * HEADS:(k + 1) * HEADS].unsqueeze(1), [P, ET, HEADS]), ALU.mult))
                    step(dve.tensor_tensor(fac, fac, term[:, :, :], ALU.add))
                step(dve.tensor_tensor(fac, fac, over(wgt[:, :].unsqueeze(2), [P, ET, HEADS]), ALU.mult))
                step(dve.tensor_copy(keep["wgt"][:, :], wgt[:, :]))
                step(dve.tensor_copy(b2w[:, :, :], over(b2c[:, :].unsqueeze(2), [P, KH, P])))
                c2 = n
                assert c2 == B2W_STEP
                for k in range(KI):
                    dve.wait_ge(w1_hi, k + 1)
                    dve.tensor_tensor(l0["W1l"][:, k, :], W1raw[:, k % 2, :], l0["W1h"][:, k, :].bitcast(F32),
                                      ALU.subtract).then_inc(w1_lo, 1)
                with dve.Fori(0, EG) as g:
                    dve.wait_ge(hist_read, g)
                    for q, (part, width) in enumerate(((0, P), (1, NT), (2, P), (3, NT))):
                        cols = over(hl[:, part, bass.ds(g * GROUP, GROUP)].unsqueeze(2), [P, GROUP, width])
                        dve.tensor_tensor(onehot[:, q, :, 0:width], over(iota_f[:, 0:width].unsqueeze(1), [P, GROUP, width]),
                                          cols, ALU.is_equal).then_inc(onehot_ready, 1)
                    dve.wait_ge(onehot_ready, g * 5 + 4)
                    dve.tensor_tensor(onehot[:, 3, :, 0:NT], onehot[:, 3, :, 0:NT],
                                      over(val[:, bass.ds(g * GROUP, GROUP)].unsqueeze(2), [P, GROUP, NT]),
                                      ALU.mult).then_inc(onehot_ready, 1)
                dve.wait_ge(hist_done, 1)
                dve.tensor_scalar(found[:, :], hist[:, 0, 0:NT], 1.0, None, ALU.add).then_inc(count_ready, 1)
                dve.wait_ge(root_ready, 1)
                step(dve.reciprocal(keep["dis"][:, 0:NT], root[:, :]))
                step(dve.tensor_scalar(keep["has"][:, 0:NT], hist[:, 1, 0:NT], 0.0, None, ALU.is_gt))
                step(dve.tensor_scalar(found[:, :], keep["has"][:, 0:NT], -FAR, FAR - 1.0, ALU.mult, ALU.add))
                step(dve.memset(keep["slot"][:, :], 1 << 20))
                step(dve.memset(keep["dis"][:, NT:NT + 8], 0.0))
                step(dve.memset(keep["has"][:, NT:NT + 8], 0.0))
                step(dve.tensor_tensor(keep["dis2"][:, :], keep["dis"][:, :], keep["dis"][:, :], ALU.mult))
                step(dve.tensor_tensor(keep["dish"][:, :], keep["dis"][:, :], keep["has"][:, :], ALU.mult))
                step(dve.tensor_tensor(keep["slot"][:, 0:NT], hist[:, 1, 0:NT], found[:, :], ALU.add))
                with dve.Fori(0, KH // 2) as it:
                    for b in range(2):
                        for h in range(2):
                            dve.wait_ge(fold_hi, it * 4 + (2 * b + h + 1))
                            dve.tensor_tensor(l0["W23l"][:, it * 2 + b, h * HALF:(h + 1) * HALF], fold[:, 2 * b + h, 0:HALF],
                                              l0["W23h"][:, it * 2 + b, h * HALF:(h + 1) * HALF].bitcast(F32),
                                              ALU.subtract).then_inc(fold_lo, 1)
                dve.wait_ge(c2_ready, 1)
                for h in range(2):
                    step(dve.tensor_copy(l0["c2"][:, h * HALF:(h + 1) * HALF], c2p[:, h, 0:HALF]))

            @block.tensor
            def _(pe):
                pe.wait_ge(zero_ready, 1)
                for q in range(2):
                    pe.matmul(hist[:, q, 0:NT], zeros[:, :], zeros[:, 0:NT], start=True, stop=False)
                with pe.Fori(0, EG) as g:
                    pe.wait_ge(onehot_ready, g * 5 + 5)
                    for j in range(GROUP):
                        for q in range(2):
                            mm = pe.matmul(hist[:, q, 0:NT], onehot[:, 2 * q, j, :], onehot[:, 2 * q + 1, j, 0:NT],
                                           start=False, stop=False)
                    mm.then_inc(hist_read, 1)
                for q in range(2):
                    mm = pe.matmul(hist[:, q, 0:NT], zeros[:, :], zeros[:, 0:NT], start=False, stop=True)
                mm.then_inc(hist_done, 1)
                pe.wait_ge(w3b_loaded, 16)
                with pe.Fori(0, KH // 2) as it:
                    for b in range(2):
                        pe.wait_ge(w2_loaded[b], it * 16 + 16)
                        pe.wait_ge(fold_lo, it * 4)
                        for h in range(2):
                            for k in range(KH):
                                mm = pe.matmul(fold[:, 2 * b + h, 0:HALF], W2m[:, b, k, :], W3b[:, k, h * HALF:(h + 1) * HALF],
                                               start=(k == 0), stop=(k == KH - 1))
                        mm.then_inc(fold_ready, 1)
                pe.wait_ge(dve_step, B2W_STEP)
                for h in range(2):
                    for k in range(KH):
                        mm = pe.matmul(c2p[:, h, 0:HALF], b2w[:, k, :], W3b[:, k, h * HALF:(h + 1) * HALF],
                                       start=(k == 0), stop=(k == KH - 1))
                mm.then_inc(c2_ready, 1)


B2W_STEP = 1 + 1 + 4 + 2 + 1 + 3 * HEADS + 1 + 1 + 1


def turn_plan(r, t):
    if t < GROUP:
        return r, 1, ((0, 1), (2, 3), (4,), ())[t], ()
    return r + 1, 0, ((0,), (1,), (2,), ())[t - GROUP], (3, 4) if t == 2 * GROUP - 1 else ()


def layer0_edges(nc, core, a, keep, l0, T0):
    sem = core.sem
    idx_staged, go = sem("b_idx"), sem("b_go")
    x_loaded = [sem("b_x0"), sem("b_x1")]
    attr_loaded = [sem("b_attr0"), sem("b_attr1")]
    rows_loaded = sem("b_rows")
    dve_init = sem("b_init")
    ln_step, var_ready, std_ready, norm_ready, h_ready = (sem("b_" + n) for n in ("lnstep", "var", "std", "norm", "h"))
    tp_ready, tp_free, hT_hi = sem("b_tp"), sem("b_tpfree"), sem("b_hThi")
    hid_ready, relu_ready, hid_hi, hid_lo = sem("b_hid"), sem("b_relu"), sem("b_hidhi"), sem("b_hidlo")
    y_ready = [sem("b_y0"), sem("b_y1")]
    y_out = [sem("b_yo0"), sem("b_yo1")]
    row_ready, carry_ready, match_ready = sem("b_row"), sem("b_carry"), sem("b_match")
    sum_ready, cnt_inv, sum_scaled = sem("b_sum"), sem("b_cnt"), sem("b_scaled")
    sum_stored = sem("b_stored")

    with ExitStack() as st:
        sb = lambda n, s, d=F32: core.sb(st, "b_" + n, s, d)
        X = sb("X", [P, 2, GROUP, F])
        attr = sb("attr", [P, 2, GROUP, FE])
        idx = sb("idx", [P, 2 * GROUP], I32)
        stt = core.stats(st, "b")
        hTh, hTl = sb("hTh", [P, KI, GROUP * P], F32R), sb("hTl", [P, KI, GROUP * P], F32R)
        R = sb("R", [P, 2, GROUP * P])
        Rh, Rl = sb("Rh", [P, KH, GROUP * P], F32R), sb("Rl", [P, KH, GROUP * P], F32R)
        Y = sb("Y", [P, 2, IN + 2])
        carry = sb("carry", [1, IN + 2])
        match = sb("match", [P, GROUP, P])
        inv = sb("inv", [P, 1])
        T = sb("T", [P, IN])
        tp = core.ps(st, "b_tp_ps", [P, 2, 512])
        hid = core.ps(st, "b_hid_ps", [P, 2, 512])
        y = core.ps(st, "b_y_ps", [P, 2, 512])
        s = core.ps(st, "b_s_ps", [P, 2, 512])
        rows16 = keep["rows"]
        SW = (HALF, HALF + 2)

        with nc.Block() as block:
            @block.gpsimd
            def _(pool):
                with pool.Fori(0, ER + 1) as r:
                    pool.tensor_copy(idx[:, :], keep["src"][:, bass.ds(r * (2 * GROUP), 2 * GROUP)]).then_inc(idx_staged, 1)
                    pool.wait_ge(idx_staged, r + 1)
                    pool.wait_ge(tp_ready, r * (2 * KI))
                    pool.sem_inc(go, 1)
                    for i in range(2 * GROUP):
                        pool.indirect_dma_start(X[:, i // GROUP, i % GROUP, :], None, a["x"][:, :],
                                                bass.IndirectOffsetOnAxis(idx[:, i:i + 1], 0),
                                                bounds_check=NODES - 1, oob_is_err=False).then_inc(x_loaded[i // GROUP], 16)
                    pool.wait_ge(x_loaded[0], r * 64 + 64)
                    pool.wait_ge(x_loaded[1], r * 64 + 64)
                    pool.sem_inc(go, 1)

            @block.sync
            def _(sp):
                for b in range(2):
                    sp.dma_start(attr[:, b, :, :], a["attr_win"][:, b, :, :]).then_inc(attr_loaded[b], 16)
                with sp.Fori(0, ER) as r:
                    for t in range(2 * GROUP):
                        sp.wait_ge(sum_scaled, (r * (2 * GROUP) + t) * 2 + 2)
                        sp.dma_start(T0[bass.ds((r * (2 * GROUP) + t) * P, P), :], T[:, :]).then_inc(sum_stored, 16)
                        if t in (4, 5):
                            b = t - 4
                            sp.wait_ge(tp_ready, r * (2 * KI) + 2 * KI)
                            sp.dma_start(attr[:, b, :, :], a["attr_win"][:, r * 2 + (2 + b), :, :]).then_inc(attr_loaded[b], 16)
                sp.wait_ge(sum_stored, 16 * ET)
                for b in range(2):
                    sp.wait_ge(attr_loaded[b], 16 * (ER + 1))

            @block.scalar
            def _(act):
                def root(r):
                    act.wait_ge(var_ready, r * 8 + 8)
                    layer_norm_std(act, stt, keep["eps"]).then_inc(std_ready, 1)
                    act.wait_ge(norm_ready, r + 1)

                def norm_rows(r, first):
                    for i in (first, first + 1):
                        xi = X[:, i // GROUP, i % GROUP, :]
                        relu_norm(act, xi, xi, stt, i).then_inc(h_ready, 1)

                def norm(r):
                    root(r)
                    for i in range(0, 8, 2):
                        norm_rows(r, i)

                def transposed(r, b, chunks):
                    for c in chunks:
                        if c == 0:
                            act.wait_ge(hid_ready, r * 20 + 10 * b)
                        act.wait_ge(tp_ready, r * 10 + (5 * b + c + 1))
                        act.copy(hTh[:, c, :], tp[:, (5 * b + c) % 2, :]).then_inc(hT_hi, 1)

                def hidden(r, b, m):
                    k = 10 * b + m
                    if m == 0:
                        act.wait_ge(y_ready[1], r * 8 + 4 * b)
                    act.wait_ge(hid_ready, r * 20 + (k + 1))
                    act.wait_ge(hid_lo, r * 20 + max(k - 1, 0))
                    act.activation(R[:, m % 2, :], hid[:, m % 2, :], ACT.Relu, bias=l0["b1"][:, m:m + 1]).then_inc(relu_ready, 1)
                    act.activation(Rh[:, m, :], hid[:, m % 2, :], ACT.Relu, bias=l0["b1"][:, m:m + 1]).then_inc(hid_hi, 1)

                def carry_out(r, t):
                    act.wait_ge(sum_ready, r * 8 + (t + 1))
                    act.wait_ge(row_ready, r * 8 + (t + 1))
                    act.copy(carry[0:1, 0:HALF], s[0:1, 0, 0:HALF]).then_inc(carry_ready, 1)
                    act.copy(carry[0:1, HALF:IN + 2], s[0:1, 1, 0:HALF + 2]).then_inc(carry_ready, 1)

                def edge_rows(r, t):
                    nr, nb, during, last = turn_plan(r, t)
                    act.wait_ge(y_ready[0], r * 8 + (t + 1))
                    act.copy(Y[:, t % 2, 0:HALF], y[:, 0, 0:HALF]).then_inc(y_out[0], 1)
                    transposed(nr, nb, during[:1])
                    if t % 4:
                        carry_out(r, t - 1)
                    act.wait_ge(y_out[0], r * 8 + (t + 1))
                    act.wait_ge(y_out[1], r * 8 + (t + 1))
                    act.wait_ge(carry_ready, r * 16 + 2 * t)
                    act.copy(Y[0:1, t % 2, :], carry[0:1, :]).then_inc(row_ready, 1)
                    transposed(nr, nb, during[1:])
                    transposed(nr, nb, last)

                act.wait_ge(dve_init, 2)
                norm(0)
                transposed(0, 0, range(KI))
                with act.Fori(0, ER) as r:
                    for m in range(KH):
                        hidden(r, 0, m)
                    for t in range(4):
                        edge_rows(r, t)
                    for m in range(KH):
                        hidden(r, 1, m)
                        if m == 2:
                            carry_out(r, 3)
                        if m == 5:
                            root(r + 1)
                        if m >= 6:
                            norm_rows(r + 1, 2 * (m - 6))
                    for t in range(4, 8):
                        edge_rows(r, t)
                    carry_out(r, 7)

            @block.vector
            def _(dve):
                dve.memset(Y[:, :, IN:IN + 2], 1.0).then_inc(dve_init, 1)
                dve.memset(carry[:, :], 0.0).then_inc(dve_init, 1)

                def norm(r):
                    dve.wait_ge(x_loaded[0], r * 64 + 64)
                    dve.wait_ge(x_loaded[1], r * 64 + 64)
                    layer_norm_stats(dve, tiles(X), stt, ln_step, r * 9, var_ready)
                    dve.wait_ge(std_ready, r + 1)
                    layer_norm_scale(dve, stt, ln_step, r * 9 + 9, norm_ready)

                def transposed(r, b, chunks):
                    for c in chunks:
                        dve.wait_ge(hT_hi, r * 10 + (5 * b + c + 1))
                        dve.tensor_tensor(hTl[:, c, :], tp[:, (5 * b + c) % 2, :], hTh[:, c, :].bitcast(F32),
                                          ALU.subtract).then_inc(tp_free, 1)

                def hidden(r, b, m):
                    dve.wait_ge(hid_hi, r * 20 + (10 * b + m + 1))
                    dve.tensor_tensor(Rl[:, m, :], R[:, m % 2, :], Rh[:, m, :].bitcast(F32), ALU.subtract).then_inc(hid_lo, 1)

                def build_match(r, b):
                    dve.wait_ge(sum_ready, r * 8 + 4 * b)
                    g = r * 8 + 4 * b
                    dve.tensor_tensor(match[:, :, :], rows16[:, bass.ds(g * P, GROUP * P)].rearrange("p (j q) -> p j q", q=P),
                                      over(keep["dst"][:, bass.ds(g, GROUP)].unsqueeze(2), [P, GROUP, P]),
                                      ALU.is_equal).then_inc(match_ready, 1)

                def sums(r, t):
                    dve.wait_ge(carry_ready, r * 16 + (2 * t + 2))
                    dve.reciprocal(inv[:, :], s[:, 1, HALF:HALF + 1]).then_inc(cnt_inv, 1)
                    dve.wait_ge(cnt_inv, r * 8 + (t + 1))
                    dve.wait_ge(sum_stored, r * 128 + 16 * t)
                    for h in range(2):
                        dve.scalar_tensor_tensor(out=T[:, h * HALF:(h + 1) * HALF], in0=s[:, h, 0:HALF], scalar=inv[:, 0:1],
                                                 in1=l0["c2"][:, h * HALF:(h + 1) * HALF], op0=ALU.mult, op1=ALU.add
                                                 ).then_inc(sum_scaled, 1)

                def edge_rows(r, t):
                    nr, nb, during, last = turn_plan(r, t)
                    transposed(nr, nb, during[:1])
                    dve.wait_ge(y_ready[1], r * 8 + (t + 1))
                    dve.tensor_copy(Y[:, t % 2, HALF:IN], y[:, 1, 0:HALF]).then_inc(y_out[1], 1)
                    if t % 4:
                        sums(r, t - 1)
                    transposed(nr, nb, during[1:])
                    transposed(nr, nb, last)

                norm(0)
                transposed(0, 0, range(KI))
                with dve.Fori(0, ER) as r:
                    build_match(r, 0)
                    for m in range(KH):
                        hidden(r, 0, m)
                    for t in range(4):
                        edge_rows(r, t)
                    for m in range(KH):
                        hidden(r, 1, m)
                        if m == 2:
                            sums(r, 3)
                            build_match(r, 1)
                        if m == 4:
                            norm(r + 1)
                    for t in range(4, 8):
                        edge_rows(r, t)
                    sums(r, 7)

            @block.tensor
            def _(pe):
                def transpose(r, b, chunks):
                    for c in chunks:
                        k = 5 * b + c
                        if c == 0:
                            pe.wait_ge(h_ready, r * 8 + (4 * b + 4))
                        if c == KF:
                            pe.wait_ge(attr_loaded[b], r * 16 + 16)
                        pe.wait_ge(tp_free, r * 10 + (k + 1))
                        for j in range(GROUP):
                            rows = X[:, b, j, c * P:(c + 1) * P] if c < KF else attr[:, b, j, :]
                            mm = pe.transpose(tp[:, k % 2, j * P:(j + 1) * P], rows, keep["ident"][:, :])
                        mm.then_inc(tp_ready, 1)

                def first(r, b, m):
                    k = 10 * b + m
                    pe.wait_ge(hid_hi, r * 20 + max(k - 1, 0))
                    for c in range(KI):
                        if m == 0:
                            pe.wait_ge(tp_free, r * 10 + (5 * b + c + 1 + 2))
                        mm = three(pe, hid[:, m % 2, :],
                                   (l0["W1h"][:, c, m * P:(m + 1) * P], l0["W1l"][:, c, m * P:(m + 1) * P]),
                                   (hTh[:, c, :], hTl[:, c, :]), c == 0, c == KI - 1)
                    mm.then_inc(hid_ready, 1)

                def second(r, b, j):
                    t = 4 * b + j
                    nr, nb, during, last = turn_plan(r, t)
                    for h in range(2):
                        pe.wait_ge(y_out[h], r * 8 + t)
                        for k in range(KH):
                            if j == 0 and h == 0:
                                pe.wait_ge(hid_lo, r * 20 + (10 * b + k + 1))
                            w = slice(h * HALF, (h + 1) * HALF)
                            mm = three(pe, y[:, h, 0:HALF], (Rh[:, k, j * P:(j + 1) * P], Rl[:, k, j * P:(j + 1) * P]),
                                       (l0["W23h"][:, k, w], l0["W23l"][:, k, w]), k == 0, k == KH - 1)
                        mm.then_inc(y_ready[h], 1)
                        transpose(nr, nb, during[h:h + 1])
                    if j:
                        sum_runs(r, t - 1)
                    transpose(nr, nb, last)

                def sum_runs(r, t):
                    pe.wait_ge(row_ready, r * 8 + (t + 1))
                    pe.wait_ge(match_ready, r * 2 + (t // 4 + 1))
                    pe.wait_ge(sum_scaled, r * 16 + 2 * t)
                    pe.wait_ge(carry_ready, r * 16 + 2 * t)
                    for h in range(2):
                        mm = pe.matmul(s[:, h, 0:SW[h]], match[:, t % 4, :], Y[:, t % 2, h * HALF:h * HALF + SW[h]],
                                       start=True, stop=True)
                    mm.then_inc(sum_ready, 1)

                pe.sem_inc(tp_free, 2)
                transpose(0, 0, range(KI))
                with pe.Fori(0, ER) as r:
                    for m in range(KH):
                        first(r, 0, m)
                    for j in range(GROUP):
                        second(r, 0, j)
                    for m in range(KH):
                        first(r, 1, m)
                        if m == 1:
                            sum_runs(r, 3)
                    for j in range(GROUP):
                        second(r, 1, j)
                    sum_runs(r, 7)


Z_SLOT = ((0, 1), (2, 3), (4,), ())


def layer0_nodes(nc, core, a, keep, T0, x1):
    sem = core.sem
    w_loaded, w_hi, w_lo, init = sem("c_w"), sem("c_whi"), sem("c_wlo"), sem("c_init")
    x_loaded = [sem("c_x0"), sem("c_x1")]
    res_loaded = [sem("c_r0"), sem("c_r1")]
    run_loaded = [sem("c_g0"), sem("c_g1")]
    idx_staged, go, res_ready = sem("c_idx"), sem("c_go"), sem("c_res")
    ln_step, var_ready, std_ready, norm_ready, h_ready = (sem("c_" + n) for n in ("lnstep", "var", "std", "norm", "h"))
    tp_ready, tp_free, hT_hi = sem("c_tp"), sem("c_tpfree"), sem("c_hThi")
    u_ready, u_out, z_hi = sem("c_u"), sem("c_uout"), sem("c_zhi")
    o_ready, o_out = sem("c_o"), sem("c_oout")
    stored = [sem("c_st0"), sem("c_st1")]
    TPR = 2 * (KF + KI)
    GT = 2 * GROUP

    with ExitStack() as st:
        sb = lambda n, s, d=F32: core.sb(st, "c_" + n, s, d)
        X = sb("X", [P, 2, GROUP, F])
        XB = sb("XB", [P, 2, GROUP, F])
        G = sb("G", [P, 2, GROUP, IN])
        idx = sb("idx", [P, GT], I32)
        stt = core.stats(st, "c")
        hTh, hTl = sb("hTh", [P, 2, KF, GROUP * P], F32R), sb("hTl", [P, 2, KF, GROUP * P], F32R)
        U = sb("U", [P, 2, GROUP, IN])
        R = sb("R", [P, 2, GROUP * P])
        zh, zl = sb("zh", [P, 2, KI, GROUP * P], F32R), sb("zl", [P, 2, KI, GROUP * P], F32R)
        W3h, W3l = sb("W3h", [P, KF, IN], F32R), sb("W3l", [P, KF, IN], F32R)
        W4h, W4l = sb("W4h", [P, KI, F], F32R), sb("W4l", [P, KI, F], F32R)
        b3, b4 = sb("b3", [P, KI]), sb("b4", [P, F])
        tp = core.ps(st, "c_tp_ps", [P, 2, 512])
        u = core.ps(st, "c_u_ps", [P, 4, 512])
        o = core.ps(st, "c_o_ps", [P, 2, 512])
        W3raw = U[:, 0, :, :]
        W4raw = U[:, 1, :, :].rearrange("p j n -> p (j n)").rearrange("p (k n) -> p k n", k=KI)

        with nc.Block() as block:
            @block.sync
            def _(sp):
                def load(g, b):
                    sp.dma_start(X[:, b, :, :], group_rows(a["x"], g, F)).then_inc(x_loaded[b], 16)

                def load_last(buf, b, sems):
                    at = (NG - 1) * GROUP * P
                    left = NODES - at
                    for j in range((left + P - 1) // P):
                        n = min(P, left - j * P)
                        sp.dma_start(buf[0:n, b, j, :], a["x"][at + j * P:at + j * P + n, :]).then_inc(sems[b], 16)

                def residual(g, b):
                    sp.dma_start(XB[:, b, :, :], group_rows(a["x"], g, F)).then_inc(res_loaded[b], 16)

                def store(r, g, b):
                    sp.wait_ge(o_out, r * GT + (4 * b + 4 + 2))
                    sp.dma_start(group_rows(x1, g, F), XB[:, b, :, :]).then_inc(stored[b], 16)

                for b in range(2):
                    load(b, b)
                sp.dma_start(W3raw, a["L0_gnn_W3"][0:F, :].rearrange("(k p) n -> p k n", p=P)).then_inc(w_loaded, 16)
                sp.dma_start(W4raw, a["L0_gnn_W4"].rearrange("(k p) n -> p k n", p=P)).then_inc(w_loaded, 16)
                sp.dma_start(b3[:, :], a["L0_gnn_b3"].rearrange("(k p) -> p k", p=P),
                             allow_slow_non_contiguous=True).then_inc(w_loaded, 16)
                sp.dma_start(b4[:, :], a["L0_gnn_b4"].rearrange("(o n) -> o n", o=1).broadcast_to([P, F])).then_inc(w_loaded, 16)
                sp.wait_ge(init, 2)
                with sp.Fori(0, NR - 2) as r:
                    sp.wait_ge(tp_ready, r * TPR + 2 * KF)
                    for b in range(2):
                        load(r * 2 + (2 + b), b)
                    for b in range(2):
                        sp.wait_ge(stored[b], r * 16)
                        residual(r * 2 + b, b)
                    for b in range(2):
                        store(r, r * 2 + b, b)
                for r in (NR - 2, NR - 1):
                    sp.wait_ge(tp_ready, r * TPR + 2 * KF)
                    for b in range(2):
                        if r == NR - 1:
                            load(b, b)
                        elif b:
                            load_last(X, b, x_loaded)
                        else:
                            load(2 * r + 2, b)
                    for b in range(2):
                        sp.wait_ge(stored[b], 16 * r)
                        if r == NR - 1 and b:
                            load_last(XB, b, res_loaded)
                        else:
                            residual(2 * r + b, b)
                    for b in range(2):
                        store(r, 2 * r + b, b)
                for b in range(2):
                    sp.wait_ge(stored[b], 16 * NR)
                    sp.wait_ge(x_loaded[b], 16 * (NR + 1) + 32 * b)

            @block.gpsimd
            def _(pool):
                pool.memset(G[:, :, :, :], 0.0).then_inc(init, 1)
                pool.memset(XB[:, 1, :, :], 0.0).then_inc(init, 1)
                pool.wait_ge(w_loaded, 64)
                pool.wait_ge(init, 2)

                def round_(r, late):
                    pool.tensor_copy(idx[:, :], keep["slot"][:, bass.ds(r * GT, GT)]).then_inc(idx_staged, 1)
                    pool.wait_ge(idx_staged, r + 1)
                    pool.wait_ge(u_out, r * (2 * GT) + 4)
                    pool.sem_inc(go, 1)
                    for i in range(GT):
                        pool.indirect_dma_start(G[:, i // GROUP, i % GROUP, :], None, T0[:, :],
                                                bass.IndirectOffsetOnAxis(idx[:, i:i + 1], 0),
                                                bounds_check=ROWS_E - 1, oob_is_err=False).then_inc(run_loaded[i // GROUP], 16)
                    for b in range(2):
                        pool.wait_ge(res_loaded[b], r * 16 + (16 + late * b))
                        pool.tensor_tensor(XB[:, b, :, :], XB[:, b, :, :], over(b4[:, :].unsqueeze(1), [P, GROUP, F]),
                                           ALU.add).then_inc(res_ready, 1)
                    for b in range(2):
                        pool.wait_ge(run_loaded[b], r * 64 + 64)
                    pool.sem_inc(go, 1)

                with pool.Fori(0, NR - 1) as r:
                    round_(r, 0)
                round_(NR - 1, 32)

            @block.scalar
            def _(act):
                def root(r):
                    act.wait_ge(var_ready, r * GT + GT)
                    layer_norm_std(act, stt, keep["eps"]).then_inc(std_ready, 1)
                    act.wait_ge(norm_ready, r + 1)

                def norm_rows(r, first):
                    for i in (first, first + 1):
                        x = X[:, i // GROUP, i % GROUP, :]
                        relu_norm(act, x, x, stt, i).then_inc(h_ready, 1)

                def turned_rows(r, chunks):
                    for k in chunks:
                        act.wait_ge(tp_ready, r * TPR + (k + 1))
                        act.copy(hTh[:, k // KF, k % KF, :], tp[:, k % 2, :]).then_inc(hT_hi, 1)

                def hidden(r, b, chunks):
                    for c in chunks:
                        k = 2 * KF + KI * b + c
                        act.wait_ge(o_ready, r * GT)
                        act.wait_ge(tp_ready, r * TPR + (k + 1))
                        act.activation(R[:, k % 2, :], tp[:, k % 2, :], ACT.Relu, bias=b3[:, c:c + 1]).then_inc(z_hi, 1)
                        act.activation(zh[:, b, c, :], tp[:, k % 2, :], ACT.Relu, bias=b3[:, c:c + 1]).then_inc(z_hi, 1)

                root(0)
                for i in range(GROUP):
                    norm_rows(0, 2 * i)
                for n, (raw, hi) in enumerate(((W3raw, W3h), (W4raw, W4h))):
                    split_on_act(act, raw, hi[:, :, :], w_loaded, 64, w_hi)
                turned_rows(0, range(2 * KF))
                with act.Fori(0, NR) as r:
                    for j in range(GROUP):
                        hidden(r, 0, Z_SLOT[j])
                    for j in range(GROUP):
                        hidden(r, 1, Z_SLOT[j])
                        if j == 0:
                            root(r + 1)
                        norm_rows(r + 1, 2 * j)
                    for j in range(GROUP):
                        turned_rows(r + 1, (2 * j, 2 * j + 1))

            @block.vector
            def _(dve):
                def stats(r, late, first):
                    if first % GROUP == 0:
                        b = first // GROUP
                        dve.wait_ge(x_loaded[b], r * 16 + (16 + late * b))
                    for i in (first, first + 1):
                        dve.bn_stats(stt["raw"][:, i, :], X[:, i // GROUP, i % GROUP, :]).then_inc(ln_step, 1)

                def scale(r):
                    dve.wait_ge(ln_step, r * 9 + GT)
                    dve.sem_inc(stt["go"], 1)
                    for i in range(GT):
                        dve.bn_aggr(stt["mv"][:, i, :], stt["raw"][:, i, :]).then_inc(var_ready, 1)
                    dve.wait_ge(std_ready, r + 1)
                    layer_norm_scale(dve, stt, ln_step, r * 9 + 9, norm_ready)

                def turned_rows(r, chunks):
                    for k in chunks:
                        dve.wait_ge(hT_hi, r * (2 * KF) + (k + 1))
                        dve.tensor_tensor(hTl[:, k // KF, k % KF, :], tp[:, k % 2, :], hTh[:, k // KF, k % KF, :].bitcast(F32),
                                          ALU.subtract).then_inc(tp_free, 1)

                def hidden(r, b, chunks):
                    for c in chunks:
                        k = KI * b + c
                        dve.wait_ge(z_hi, r * (4 * KI) + (2 * k + 2))
                        dve.tensor_tensor(zl[:, b, c, :], R[:, k % 2, :], zh[:, b, c, :].bitcast(F32),
                                          ALU.subtract).then_inc(tp_free, 1)

                def add_run(r, b, j):
                    t = GROUP * b + j
                    if j == 0:
                        dve.wait_ge(run_loaded[b], r * 64 + 64)
                    dve.wait_ge(u_ready, r * GT + (t + 1))
                    for h in range(2):
                        w = slice(h * HALF, (h + 1) * HALF)
                        dve.scalar_tensor_tensor(out=U[:, b, j, w], in0=G[:, b, j, w],
                                                 scalar=keep["has"][:, bass.ds(r * GT + t, 1)],
                                                 in1=u[:, 2 * (t % 2) + h, 0:HALF], op0=ALU.mult, op1=ALU.add
                                                 ).then_inc(u_out, 1)

                def add_residual(r, b, j):
                    t = GROUP * b + j
                    if j == 0:
                        dve.wait_ge(res_ready, r * 2 + (b + 1))
                    dve.wait_ge(o_ready, r * GT + (t + 1))
                    dve.tensor_tensor(XB[:, b, j, :], o[:, t % 2, :], XB[:, b, j, :], ALU.add).then_inc(o_out, 1)

                def round_(r, late):
                    for j in range(GROUP):
                        add_run(r, 0, j)
                    for j in range(GROUP):
                        add_run(r, 1, j)
                        hidden(r, 0, Z_SLOT[j])
                        stats(r + 1, late, 2 * j)
                    for j in range(GROUP):
                        if j == 0:
                            scale(r + 1)
                        add_residual(r, 0, j)
                        hidden(r, 1, Z_SLOT[j])
                    for j in range(GROUP):
                        add_residual(r, 1, j)
                        turned_rows(r + 1, (2 * j, 2 * j + 1))

                for i in range(GROUP):
                    stats(0, 0, 2 * i)
                scale(0)
                for n, (raw, hi, lo) in enumerate(((W3raw, W3h, W3l), (W4raw, W4h, W4l))):
                    split_on_dve(dve, raw, hi[:, :, :], lo[:, :, :], w_hi, n + 1, w_lo)
                turned_rows(0, range(2 * KF))
                with dve.Fori(0, NR - 2) as r:
                    round_(r, 0)
                for r in (NR - 2, NR - 1):
                    round_(r, 32)

            @block.tensor
            def _(pe):
                def transpose(r, k, source):
                    pe.wait_ge(tp_free, r * TPR + (k + 1))
                    for j in range(GROUP):
                        mm = pe.transpose(tp[:, k % 2, j * P:(j + 1) * P], source(j), keep["ident"][:, :])
                    mm.then_inc(tp_ready, 1)

                def turn_rows(r, chunks):
                    for k in chunks:
                        b, c = k // KF, k % KF
                        if c == 0:
                            pe.wait_ge(h_ready, r * GT + (GROUP * b + GROUP))
                        transpose(r, k, lambda j: X[:, b, j, c * P:(c + 1) * P])

                def turn_sums(r, b, chunks):
                    for c in chunks:
                        pe.wait_ge(u_out, r * (2 * GT) + (2 * GROUP * (b + 1) + 4))
                        transpose(r, 2 * KF + KI * b + c, lambda j: U[:, b, j, c * P:(c + 1) * P])

                def first(r, b, j):
                    t = GROUP * b + j
                    if j == 0:
                        pe.wait_ge(tp_free, r * TPR + (KF * b + KF + 2))
                    pe.wait_ge(u_out, r * (2 * GT) + (2 * t + 2))
                    for h in range(2):
                        w = slice(h * HALF, (h + 1) * HALF)
                        for c in range(KF):
                            mm = three(pe, u[:, 2 * (t % 2) + h, 0:HALF],
                                       (hTh[:, b, c, j * P:(j + 1) * P], hTl[:, b, c, j * P:(j + 1) * P]),
                                       (W3h[:, c, w], W3l[:, c, w]), c == 0, c == KF - 1)
                    mm.then_inc(u_ready, 1)

                def second(r, b, j):
                    t = GROUP * b + j
                    if j == 0:
                        pe.wait_ge(tp_free, r * TPR + (2 * KF + KI * b + KI + 2))
                    pe.wait_ge(o_out, r * GT + (t + 1))
                    for c in range(KI):
                        mm = three(pe, o[:, t % 2, :], (zh[:, b, c, j * P:(j + 1) * P], zl[:, b, c, j * P:(j + 1) * P]),
                                   (W4h[:, c, :], W4l[:, c, :]), c == 0, c == KI - 1)
                    mm.then_inc(o_ready, 1)

                pe.sem_inc(tp_free, 2)
                pe.sem_inc(u_out, 4)
                pe.sem_inc(o_out, 2)
                turn_rows(0, range(2 * KF))
                pe.wait_ge(w_lo, 2)
                with pe.Fori(0, NR) as r:
                    for j in range(GROUP):
                        first(r, 0, j)
                    for j in range(GROUP):
                        first(r, 1, j)
                        turn_sums(r, 0, Z_SLOT[j])
                    for j in range(GROUP):
                        second(r, 0, j)
                        turn_sums(r, 1, Z_SLOT[j])
                    for j in range(GROUP):
                        second(r, 1, j)
                        turn_rows(r + 1, (2 * j, 2 * j + 1))


def layer1_messages(nc, core, a, keep, x1, msg, logit):
    sem = core.sem
    w_loaded, w_hi, w_lo, diag_set = sem("d_w"), sem("d_whi"), sem("d_wlo"), sem("d_diag")
    proj_ready = sem("d_proj")
    idx_staged, go = sem("d_idx"), sem("d_go")
    x_loaded = [sem("d_x0"), sem("d_x1")]
    ln_step, var_ready, std_ready, norm_ready, h_ready = (sem("d_" + n) for n in ("lnstep", "var", "std", "norm", "h"))
    tp_ready, tp_free, hT_hi = sem("d_tp"), sem("d_tpfree"), sem("d_hThi")
    m_ready, m_out = sem("d_m"), [sem("d_mo0"), sem("d_mo1")]
    dot_ready, dot_step, dot_read = sem("d_dot"), sem("d_dotstep"), sem("d_dotread")
    flat_ready, flat_out, go_pe = sem("d_flat"), sem("d_flatout"), sem("d_gope")
    MW = (F + HEADS) // 2

    with ExitStack() as st:
        sb = lambda n, s, d=F32: core.sb(st, "d_" + n, s, d)
        X = sb("X", [P, 2, 2, GROUP, F])
        idx = sb("idx", [P, 2, 2 * GROUP], I32)
        stt = core.stats(st, "d")
        hTh, hTl = sb("hTh", [P, 3, KF, GROUP * P], F32R), sb("hTl", [P, 3, KF, GROUP * P], F32R)
        Wh, Wl = sb("Wh", [P, KF, F + HEADS], F32R), sb("Wl", [P, KF, F + HEADS], F32R)
        Ah, Al = sb("Ah", [P, KF, HEADS], F32R), sb("Al", [P, KF, HEADS], F32R)
        Wraw = sb("Wraw", [P, KF, F])
        Wrow = sb("Wrow", [P, KF, F])
        diag = sb("diag", [P, 2, KF, HEADS])
        dots = sb("dots", [P, GROUP, HEADS])
        flat = sb("flat", [HEADS, GROUP * P])
        tp = core.ps(st, "d_tp_ps", [P, 2, 512])
        m = core.ps(st, "d_m_ps", [P, 4, 512])
        dot = core.ps(st, "d_dot_ps", [P, 512])
        proj = core.ps(st, "d_proj_ps", [P, 512])
        dotv = dot[:, 0:GROUP * HEADS].rearrange("p (j h) -> p j h", h=HEADS)
        projv = proj[:, 0:2 * KF * HEADS].rearrange("p (a k h) -> p a k h", a=2, h=HEADS)

        with nc.Block() as block:
            @block.sync
            def _(sp):
                sp.dma_start(Wraw[:, :, :], a["W1T"].rearrange("(k p) n -> p k n", p=P)).then_inc(w_loaded, 16)
                sp.dma_start(Wrow[:, :, :], a["L1_gnn_W"].rearrange("(k p) n -> p k n", p=P)).then_inc(w_loaded, 16)
                sp.wait_ge(diag_set, 1)
                for q, n in enumerate(("L1_gnn_a_src", "L1_gnn_a_dst")):
                    for h in range(HEADS):
                        sp.dma_start(diag[HD * (h % 2):HD * (h % 2) + HD, q, h // 2, h:h + 1],
                                     a[n][h:h + 1, :].rearrange("o d -> d o"), allow_slow_non_contiguous=True
                                     ).then_inc(w_loaded, 16)

            @block.gpsimd
            def _(pool):
                pool.memset(diag[:, :, :, :], 0.0).then_inc(diag_set, 1)

                def gather(g, b, before, turned):
                    pool.wait_ge(x_loaded[b], before)
                    pool.sem_inc(go, 1)
                    for q, n in enumerate(("src", "dst")):
                        pool.tensor_copy(idx[:, b, q * GROUP:(q + 1) * GROUP],
                                         keep[n][:, bass.ds(g * GROUP, GROUP)]).then_inc(idx_staged, 1)
                    pool.wait_ge(idx_staged, g * 2 + 2)
                    pool.wait_ge(tp_ready, turned)
                    pool.sem_inc(go, 1)
                    for i in range(2 * GROUP):
                        pool.indirect_dma_start(X[:, b, i // GROUP, i % GROUP, :], None, x1[:, :],
                                                bass.IndirectOffsetOnAxis(idx[:, b, i:i + 1], 0),
                                                bounds_check=ROWS_N - 1, oob_is_err=False).then_inc(x_loaded[b], 16)

                gather(0, 0, 0, 0)
                with pool.Fori(0, ER) as r:
                    gather(r * 2 + 1, 1, r * 128, r * 16)
                    gather(r * 2 + 2, 0, r * 128 + 128, r * 16 + 8)
                pool.wait_ge(x_loaded[0], 128 * (ER + 1))
                pool.wait_ge(x_loaded[1], 128 * ER)
                pool.sem_inc(go, 1)

            @block.scalar
            def _(act):
                def root(g, q):
                    n = slice(GROUP * q, GROUP * q + GROUP)
                    act.wait_ge(var_ready, g * 8 + (4 * q + 4))
                    act.activation(stt["std"][:, n], stt["mv"][:, n, 1], ACT.Sqrt, bias=keep["eps"][:, 0:1]).then_inc(std_ready, 1)

                def norm_rows(g, b, q):
                    act.wait_ge(norm_ready, g * 2 + (q + 1))
                    for j in range(GROUP):
                        x = X[:, b, q, j, :]
                        relu_norm(act, x, x, stt, GROUP * q + j).then_inc(h_ready, 1)

                def turned(g, b, q, chunks, used):
                    if q == 0:
                        act.wait_ge(m_ready, used)
                    else:
                        act.wait_ge(flat_ready, used)
                    for c in chunks:
                        k = KF * q + c
                        act.wait_ge(tp_ready, g * 8 + (k + 1))
                        act.copy(hTh[:, 2 if q else b, c, :], tp[:, k % 2, :]).then_inc(hT_hi, 1)

                def message(g, j):
                    act.wait_ge(m_ready, g * 4 + (j + 1))
                    act.copy(msg[:, bass.ds(g * 4 + j, 1), 0:MW],
                             m[:, 2 * (j % 2):2 * (j % 2) + 1, 0:MW]).then_inc(m_out[0], 1)

                split_on_act(act, Wraw[:, :, :], Wh[:, :, 0:F], w_loaded, 16 * 18, w_hi)
                split_on_act(act, projv[:, 0, :, :], Wh[:, :, F:F + HEADS], proj_ready, 1, w_hi)
                split_on_act(act, projv[:, 1, :, :], Ah[:, :, :], proj_ready, 1, w_hi)
                for q in range(2):
                    root(0, q)
                    norm_rows(0, 0, q)
                turned(0, 0, 0, range(KF), 0)
                with act.Fori(0, ER) as r:
                    for b in range(2):
                        g = r * 2 + b
                        message(g, 0)
                        turned(g, b, 1, (0, 1), g)
                        root(g + 1, 0)
                        norm_rows(g + 1, 1 - b, 0)
                        message(g, 1)
                        turned(g, b, 1, (2, 3), g)
                        message(g, 2)
                        act.wait_ge(flat_ready, g + 1)
                        act.wait_ge(dot_ready, g)
                        act.copy(flat[:, :], proj[0:HEADS, :]).then_inc(flat_out, 1)
                        turned(g + 1, 1 - b, 0, (0, 1), g * 4)
                        root(g + 1, 1)
                        message(g, 3)
                        turned(g + 1, 1 - b, 0, (2, 3), g * 4)
                        norm_rows(g + 1, 1 - b, 1)

            @block.vector
            def _(dve):
                split_on_dve(dve, Wraw[:, :, :], Wh[:, :, 0:F], Wl[:, :, 0:F], w_hi, 1, w_lo)
                split_on_dve(dve, projv[:, 0, :, :], Wh[:, :, F:F + HEADS], Wl[:, :, F:F + HEADS], w_hi, 3, w_lo)
                split_on_dve(dve, projv[:, 1, :, :], Ah[:, :, :], Al[:, :, :], w_hi, 3, w_lo)

                def stats(g, b, q, loaded):
                    if q == 0:
                        dve.wait_ge(x_loaded[b], loaded)
                    for j in range(GROUP):
                        dve.bn_stats(stt["raw"][:, GROUP * q + j, :], X[:, b, q, j, :]).then_inc(ln_step, 1)

                def scale(g, q):
                    n = slice(GROUP * q, GROUP * q + GROUP)
                    dve.wait_ge(ln_step, g * 10 + (5 * q + 4))
                    dve.sem_inc(stt["go"], 1)
                    for i in range(GROUP * q, GROUP * q + GROUP):
                        dve.bn_aggr(stt["mv"][:, i, :], stt["raw"][:, i, :]).then_inc(var_ready, 1)
                    dve.wait_ge(std_ready, g * 2 + (q + 1))
                    dve.reciprocal(stt["rstd"][:, n], stt["std"][:, n]).then_inc(ln_step, 1)
                    dve.wait_ge(ln_step, g * 10 + (5 * q + 5))
                    dve.scalar_tensor_tensor(out=stt["shift"][:, n], in0=stt["mv"][:, n, 0], scalar=-1.0, in1=stt["rstd"][:, n],
                                             op0=ALU.mult, op1=ALU.mult).then_inc(norm_ready, 1)

                def turned(g, b, q, chunks):
                    for c in chunks:
                        k = KF * q + c
                        at = 2 if q else b
                        dve.wait_ge(hT_hi, g * 8 + (k + 1))
                        dve.tensor_tensor(hTl[:, at, c, :], tp[:, k % 2, :], hTh[:, at, c, :].bitcast(F32),
                                          ALU.subtract).then_inc(tp_free, 1)

                def message(g, j):
                    dve.wait_ge(m_ready, g * 4 + (j + 1))
                    dve.tensor_copy(msg[:, bass.ds(g * 4 + j, 1), MW:2 * MW],
                                    m[:, 2 * (j % 2) + 1:2 * (j % 2) + 2, 0:MW]).then_inc(m_out[1], 1)

                def logits(g):
                    dve.wait_ge(dot_ready, g + 1)
                    dve.wait_ge(m_out[1], g * 4 + (4 + 2))
                    dve.tensor_tensor(dots[:, :, :], dotv, msg[:, bass.ds(g * 4, GROUP), F:F + HEADS], ALU.add
                                      ).then_inc(dot_step, 1)
                    dve.wait_ge(dot_step, g * 2 + 1)
                    dve.scalar_tensor_tensor(out=dots[:, :, :], in0=dots[:, :, :], scalar=0.2, in1=dots[:, :, :],
                                             op0=ALU.mult, op1=ALU.max).then_inc(dot_step, 1)
                    dve.wait_ge(dot_step, g * 2 + 2)
                    dve.tensor_tensor(logit[:, bass.ds(g * 4, GROUP), :], dots[:, :, :], keep["fac"][:, bass.ds(g * 4, GROUP), :],
                                      ALU.mult).then_inc(dot_read, 1)

                for q in range(2):
                    stats(0, 0, q, 128)
                    scale(0, q)
                turned(0, 0, 0, range(KF))
                with dve.Fori(0, ER) as r:
                    for b in range(2):
                        g = r * 2 + b
                        stats(g + 1, 1 - b, 0, r * 128 + 128 * (b + 1))
                        message(g, 0)
                        turned(g, b, 1, (0, 1))
                        scale(g + 1, 0)
                        message(g, 1)
                        turned(g, b, 1, (2, 3))
                        stats(g + 1, 1 - b, 1, None)
                        message(g, 2)
                        turned(g + 1, 1 - b, 0, (0, 1))
                        scale(g + 1, 1)
                        message(g, 3)
                        turned(g + 1, 1 - b, 0, (2, 3))
                        logits(g)

            @block.tensor
            def _(pe):
                pe.wait_ge(w_loaded, 16 * 18)
                for q in range(2):
                    for k in range(KF):
                        for c in range(KF):
                            mm = pe.matmul(projv[:, q, k, :], Wrow[:, c, k * P:(k + 1) * P], diag[:, q, c, :],
                                           start=(c == 0), stop=(c == KF - 1))
                mm.then_inc(proj_ready, 1)
                pe.sem_inc(tp_free, 2)
                pe.sem_inc(m_out[0], 2)
                pe.sem_inc(m_out[1], 2)

                def turn(g, b, q, chunks):
                    pe.wait_ge(h_ready, g * 8 + (GROUP * q + GROUP))
                    for c in chunks:
                        k = KF * q + c
                        pe.wait_ge(tp_free, g * 8 + (k + 1))
                        for j in range(GROUP):
                            mm = pe.transpose(tp[:, k % 2, j * P:(j + 1) * P],
                                              X[:, b, q, j, c * P:(c + 1) * P], keep["ident"][:, :])
                        mm.then_inc(tp_ready, 1)

                def message(g, b, j):
                    for h in range(2):
                        pe.wait_ge(m_out[h], g * 4 + (j + 1))
                        for c in range(KF):
                            if j == 0 and h == 0:
                                pe.wait_ge(tp_free, g * 8 + (c + 1 + 2))
                            mm = three(pe, m[:, 2 * (j % 2) + h, 0:MW],
                                       (hTh[:, b, c, j * P:(j + 1) * P], hTl[:, b, c, j * P:(j + 1) * P]),
                                       (Wh[:, c, MW * h:MW * h + MW], Wl[:, c, MW * h:MW * h + MW]),
                                       c == 0, c == KF - 1)
                    mm.then_inc(m_ready, 1)

                turn(0, 0, 0, range(KF))
                pe.wait_ge(w_lo, 3)
                with pe.Fori(0, ER) as r:
                    for b in range(2):
                        g = r * 2 + b
                        message(g, b, 0)
                        turn(g, b, 1, (0, 1))
                        message(g, b, 1)
                        turn(g, b, 1, (2, 3))
                        message(g, b, 2)
                        pe.wait_ge(tp_free, g * 8 + (8 + 2))
                        pe.wait_ge(flat_out, g)
                        for c in range(KF):
                            mm = three(pe, proj[0:HEADS, :], (Ah[:, c, :], Al[:, c, :]), (hTh[:, 2, c, :], hTl[:, 2, c, :]),
                                       c == 0, c == KF - 1)
                        mm.then_inc(flat_ready, 1)
                        turn(g + 1, 1 - b, 0, (0, 1))
                        message(g, b, 3)
                        turn(g + 1, 1 - b, 0, (2, 3))
                        pe.wait_ge(flat_out, g + 1)
                        pe.wait_ge(dot_read, g)
                        pe.sem_inc(go_pe, 1)
                        for j in range(GROUP):
                            mm = pe.transpose(dotv[:, j, :], flat[:, j * P:(j + 1) * P], keep["ident"][0:HEADS, 0:HEADS])
                        mm.then_inc(dot_ready, 1)


def layer1_softmax(nc, core, a, keep, logit):
    sem = core.sem
    loaded, same_ready, turned, flat, fwd_done, bwd_done, shifted, exped, back, out_done = (
        sem("s_" + n) for n in ("loaded", "same", "turned", "flat", "fwd", "bwd", "shift", "exp", "back", "out"))
    with ExitStack() as st:
        sb = lambda n, s, d=F32: core.sb(st, "s_" + n, s, d)
        L = sb("L", [HEADS, ROWS_E])
        top = sb("top", [HEADS, ROWS_E])
        ids = sb("ids", [HEADS, ROWS_E], I32)
        same = sb("same", [HEADS, ROWS_E + 1], U16)
        turn = core.ps(st, "s_turn_ps", [P, 4, 512])
        rows = core.ps(st, "s_rows_ps", [P, 512])
        rowsv = rows[:, 0:ET * HEADS].rearrange("p (t h) -> p t h", h=HEADS)
        with nc.Block() as block:
            @block.sync
            def _(sp):
                sp.dma_start(ids[:, :], a["dst_flat"].broadcast_to([HEADS, ROWS_E])).then_inc(loaded, 16)

            @block.tensor
            def _(pe):
                for g in range(EG):
                    if g >= 4:
                        pe.wait_ge(flat, g - 3)
                    for j in range(GROUP):
                        mm = pe.transpose(turn[0:HEADS, g % 4, j * P:(j + 1) * P], logit[:, GROUP * g + j, :], keep["ident"][:, :])
                    mm.then_inc(turned, 1)
                pe.wait_ge(exped, 1)
                for t in range(ET):
                    mm = pe.transpose(rowsv[:, t, :], L[:, t * P:(t + 1) * P], keep["ident"][0:HEADS, 0:HEADS])
                mm.then_inc(back, 1)

            @block.scalar
            def _(act):
                for g in range(EG):
                    act.wait_ge(turned, g + 1)
                    act.copy(L[:, g * 512:(g + 1) * 512], turn[0:HEADS, g % 4, :]).then_inc(flat, 1)
                act.wait_ge(shifted, 1)
                act.activation(L[:, :], L[:, :], ACT.Exp).then_inc(exped, 1)

            @block.vector
            def _(dve):
                dve.memset(same[:, 0:1], 0).then_inc(same_ready, 1)
                dve.memset(same[:, ROWS_E:ROWS_E + 1], 0).then_inc(same_ready, 1)
                dve.wait_ge(loaded, 16)
                dve.tensor_tensor(same[:, 1:ROWS_E], ids[:, 1:ROWS_E], ids[:, 0:ROWS_E - 1], ALU.is_equal).then_inc(same_ready, 1)
                dve.wait_ge(same_ready, 3)
                dve.wait_ge(flat, EG)
                dve.tensor_tensor_scan(top[:, :], same[:, 0:ROWS_E], L[:, :], 0.0, ALU.mult, ALU.max).then_inc(fwd_done, 1)
                dve.wait_ge(fwd_done, 1)
                dve.tensor_tensor_scan(top[:, ::-1], same[:, ROWS_E:0:-1], top[:, ::-1], 0.0, ALU.mult, ALU.max).then_inc(bwd_done, 1)
                dve.wait_ge(bwd_done, 1)
                dve.tensor_tensor(L[:, :], L[:, :], top[:, :], ALU.subtract).then_inc(shifted, 1)
                dve.wait_ge(back, 1)
                dve.tensor_copy(logit[:, :, :], rowsv).then_inc(out_done, 1)


def layer1_sums(nc, core, a, keep, msg, prob, T1):
    sem = core.sem
    init, weighed, match_ready, carry_ready = (sem("e_" + n) for n in ("init", "weighed", "match", "carry"))
    y_hi, y_lo, bulk_ready = sem("e_yhi"), sem("e_ylo"), sem("e_bulk")
    sum_ready, den_step, scaled, go = (sem("e_" + n) for n in ("sum", "denstep", "scaled", "go"))
    stored = [sem(f"e_st{b}") for b in range(GROUP)]
    LW = (GW, GW + HEADS)
    with ExitStack() as st:
        sb = lambda n, s, d=F32: core.sb(st, "e_" + n, s, d)
        Y = sb("Y", [P, GROUP, 1, F + HEADS])
        Yh, Yl = sb("Yh", [P, GROUP, F + HEADS], F32R), sb("Yl", [P, GROUP, F + HEADS], F32R)
        carry = sb("carry", [1, 2, GW + HEADS])
        match = sb("match", [P, 2, GROUP, P], F32R)
        den, inv = sb("den", [P, HEADS]), sb("inv", [P, HEADS])
        T = sb("T", [P, GROUP, F])
        s = core.ps(st, "e_s_ps", [P, 2 * GROUP, 512])
        half = HEADS // 2
        with nc.Block() as block:
            @block.sync
            def _(sp):
                with sp.Fori(0, EG) as g:
                    for j in range(GROUP):
                        sp.wait_ge(scaled, g * GROUP + (j + 1 + GROUP))
                        sp.dma_start(T1[bass.ds((g * GROUP + j) * P, P), :], T[:, j, :]).then_inc(stored[j], 16)
                for j in range(GROUP):
                    sp.wait_ge(stored[j], 16 * EG)

            @block.scalar
            def _(act):
                def split(g, j):
                    t = g * GROUP + j
                    act.wait_ge(weighed, t * 2 + 2)
                    act.wait_ge(bulk_ready, t + 1)
                    act.copy(Yh[:, j % GROUP, :], Y[:, j % GROUP, 0, :]).then_inc(y_hi, 1)

                def group(g, last):
                    for j in range(GROUP):
                        for h in range(2):
                            act.wait_ge(sum_ready, g * (2 * GROUP) + (2 * j + h + 1))
                            act.copy(carry[0:1, h, 0:LW[h]], s[0:1, 2 * j + h, 0:LW[h]]).then_inc(carry_ready, 1)
                        if not (last and j >= 2):
                            split(g, j + 2)

                split(0, 0)
                split(0, 1)
                with act.Fori(0, EG - 1) as g:
                    group(g, False)
                group(EG - 1, True)

            @block.gpsimd
            def _(pool):
                pool.wait_ge(init, 2)

                with pool.Fori(0, EG) as g:
                    for j in range(GROUP):
                        t = g * GROUP + j
                        pool.wait_ge(y_lo, t + 1)
                        pool.sem_inc(go, 1)
                        pool.tensor_tensor(Y[:, j, :, 0:F].rearrange("p o (h d) -> p (o h) d", d=HD),
                                           msg[:, bass.ds(t, 1), 0:F].rearrange("p o (h d) -> p (o h) d", d=HD),
                                           over(prob[:, bass.ds(t, 1), :].rearrange("p o h -> p (o h)").unsqueeze(2), [P, HEADS, HD]),
                                           ALU.mult).then_inc(weighed, 1)
                        pool.tensor_copy(Y[:, j, :, F:F + HEADS], prob[:, bass.ds(t, 1), :]).then_inc(weighed, 1)

            @block.vector
            def _(dve):
                dve.memset(carry[:, :, :], 0.0).then_inc(init, 1)
                dve.memset(prob[0:1, :, :], 0.0).then_inc(init, 1)

                def build_match(g, b):
                    dve.tensor_tensor(match[:, b, :, :], keep["rows"][:, bass.ds(g * (GROUP * P), GROUP * P)].rearrange("p (j q) -> p j q", q=P),
                                      over(keep["dst"][:, bass.ds(g * GROUP, GROUP)].unsqueeze(2), [P, GROUP, P]),
                                      ALU.is_equal).then_inc(match_ready, 1)

                def sums(g, j):
                    t = g * GROUP + j
                    dve.wait_ge(carry_ready, t * 2 + 3)
                    dve.tensor_scalar(den[:, :], s[:, 2 * j + 1, GW:GW + HEADS], 1e-10, None, ALU.add).then_inc(den_step, 1)
                    dve.wait_ge(den_step, t * 2 + 1)
                    dve.reciprocal(inv[:, :], den[:, :]).then_inc(den_step, 1)
                    dve.wait_ge(den_step, t * 2 + 2)
                    dve.wait_ge(stored[j], g * 16)
                    dve.tensor_tensor(T[:, j, :].rearrange("p (a h d) -> p a h d", a=2, d=HD),
                                      s[:, 2 * j:2 * j + 2, 0:GW].rearrange("p a (h d) -> p a h d", d=HD),
                                      over(inv[:, :].rearrange("p (a h) -> p a h", a=2).unsqueeze(3), [P, 2, half, HD]),
                                      ALU.mult).then_inc(scaled, 1)

                def split(g, j):
                    dve.wait_ge(y_hi, g * GROUP + (j + 1))
                    dve.tensor_tensor(Yl[:, j % GROUP, :], Y[:, j % GROUP, 0, :], Yh[:, j % GROUP, :].bitcast(F32),
                                      ALU.subtract).then_inc(y_lo, 1)

                def group(g, b, last):
                    if not last:
                        build_match(g + 1, 1 - b)
                    for j in range(GROUP):
                        if not (last and j >= 2):
                            split(g, j + 2)
                        sums(g, j)

                build_match(0, 0)
                split(0, 0)
                split(0, 1)
                with dve.Fori(0, EG // 2 - 1) as q:
                    for b in range(2):
                        group(q * 2 + b, b, False)
                group(EG - 2, 0, False)
                group(EG - 1, 1, True)

            @block.tensor
            def _(pe):
                pe.sem_inc(y_lo, GROUP)
                pe.sem_inc(carry_ready, 1)
                pe.sem_inc(bulk_ready, GROUP)
                pe.sem_inc(scaled, GROUP)
                pe.wait_ge(init, 2)
                with pe.Fori(0, EG // 2) as q:
                    for b in range(2):
                        g = q * 2 + b
                        pe.wait_ge(match_ready, g + 1)
                        for j in range(GROUP):
                            t = g * GROUP + j
                            pe.wait_ge(y_lo, t + (1 + GROUP))
                            pe.wait_ge(scaled, t + 1)
                            for h in range(2):
                                pe.matmul(s[:, 2 * j + h, 0:LW[h]], match[:, b, j, :],
                                          Yh[:, j, GW * h:GW * h + LW[h]], start=True, stop=False)
                                mm = pe.matmul(s[:, 2 * j + h, 0:LW[h]], match[:, b, j, :],
                                               Yl[:, j, GW * h:GW * h + LW[h]], start=False, stop=False)
                            mm.then_inc(bulk_ready, 1)
                            for h in range(2):
                                pe.wait_ge(carry_ready, t * 2 + h)
                                pe.matmul(s[:, 2 * j + h, 0:LW[h]], match[0:1, b, j, :].bitcast(F32), carry[0:1, h, 0:LW[h]],
                                          start=False, stop=True).then_inc(sum_ready, 1)


def layer1_nodes(nc, core, a, keep, x1, T1, x2):
    sem = core.sem
    w_loaded, init, idx_staged, go = sem("n_w"), sem("n_init"), sem("n_idx"), sem("n_go")
    x_loaded = [sem("n_x0"), sem("n_x1")]
    run_loaded = [sem("n_g0"), sem("n_g1")]
    ln_step, var_ready, std_ready, norm_ready, h_ready = (sem("n_" + n) for n in ("lnstep", "var", "std", "norm", "h"))
    ln2_step, var2_ready, std2_ready, norm2_ready, n_ready = (sem("n2_" + n) for n in ("lnstep", "var", "std", "norm", "n"))
    res_ready, added, times_gamma, out_ready = sem("n_res"), sem("n_added"), sem("n_gamma"), sem("n_out")
    stored = sem("n_stored")
    GT = 2 * GROUP

    with ExitStack() as st:
        sb = lambda n, s, d=F32: core.sb(st, "n_" + n, s, d)
        X = sb("X", [P, 2, 2, GROUP, F])
        G = sb("G", [P, 2, 2, GROUP, F])
        H = sb("H", [P, 2, GROUP, F])
        O = sb("O", [P, 2, GROUP, XW])
        idx = sb("idx", [P, GT], I32)
        one, two = core.stats(st, "n1"), core.stats(st, "n2")
        gamma, beta = sb("gamma", [P, F]), sb("beta", [P, F])

        with nc.Block() as block:
            @block.sync
            def _(sp):
                sp.dma_start(gamma[:, :], a["L1_gnn_ln_gamma"].rearrange("(o n) -> o n", o=1).broadcast_to([P, F])).then_inc(w_loaded, 16)
                sp.dma_start(beta[:, :], a["L1_gnn_ln_beta"].rearrange("(o n) -> o n", o=1).broadcast_to([P, F])).then_inc(w_loaded, 16)
                with sp.Fori(0, NR // 2) as q:
                    for rb in range(2):
                        sp.wait_ge(out_ready, q * 32 + 16 * rb)
                        for b in range(2):
                            sp.dma_start(X[:, rb, b, :, :], group_rows(x1, q * 4 + (2 * rb + b), F)).then_inc(x_loaded[rb], 16)
                        if rb:
                            for k in range(2):
                                sp.wait_ge(out_ready, q * 32 + 16 * (k + 1))
                                for b in range(2):
                                    sp.dma_start(group_rows(x2, q * 4 + (2 * k + b), XW), O[:, b, :, :]).then_inc(stored, 16)
                sp.wait_ge(stored, 16 * NG)

            @block.gpsimd
            def _(pool):
                pool.memset(G[:, :, :, :, :], 0.0).then_inc(init, 1)
                pool.wait_ge(w_loaded, 32)
                pool.wait_ge(init, 1)
                with pool.Fori(0, NR // 2) as q:
                    for rb in range(2):
                        r = q * 2 + rb
                        pool.tensor_copy(idx[:, :], keep["slot"][:, bass.ds(r * GT, GT)]).then_inc(idx_staged, 1)
                        pool.wait_ge(idx_staged, r + 1)
                        pool.wait_ge(out_ready, q * 32 + 16 * rb)
                        pool.sem_inc(go, 1)
                        for i in range(GT):
                            pool.indirect_dma_start(G[:, rb, i // GROUP, i % GROUP, :], None, T1[:, :],
                                                    bass.IndirectOffsetOnAxis(idx[:, i:i + 1], 0),
                                                    bounds_check=ROWS_E - 1, oob_is_err=False).then_inc(run_loaded[rb], 16)
                        pool.wait_ge(run_loaded[rb], q * 128 + 128)
                        pool.wait_ge(h_ready, r * GT + GT)
                        for b in range(2):
                            pool.tensor_tensor(X[:, rb, b, :, :], X[:, rb, b, :, :], over(beta[:, :].unsqueeze(1), [P, GROUP, F]),
                                               ALU.add).then_inc(res_ready, 1)

            @block.scalar
            def _(act):
                with act.Fori(0, NR // 2) as q:
                    for rb in range(2):
                        r = q * 2 + rb
                        act.wait_ge(var_ready, r * GT + GT)
                        layer_norm_std(act, one, keep["eps"]).then_inc(std_ready, 1)
                        act.wait_ge(norm_ready, r + 1)
                        act.wait_ge(added, r * GT)
                        for i in range(GT):
                            relu_norm(act, H[:, i // GROUP, i % GROUP, :], X[:, rb, i // GROUP, i % GROUP, :], one, i).then_inc(h_ready, 1)
                        act.wait_ge(var2_ready, r * GT + GT)
                        layer_norm_std(act, two, keep["eps"]).then_inc(std2_ready, 1)
                        act.wait_ge(norm2_ready, r + 1)
                        for i in range(GT):
                            g = G[:, rb, i // GROUP, i % GROUP, :]
                            act.activation(g, g, ACT.Identity, bias=two["shift"][:, i:i + 1],
                                           scale=two["rstd"][:, i:i + 1]).then_inc(n_ready, 1)

            @block.vector
            def _(dve):
                dve.wait_ge(w_loaded, 32)
                with dve.Fori(0, NR // 2) as q:
                    for rb in range(2):
                        r = q * 2 + rb
                        dve.wait_ge(x_loaded[rb], q * 32 + 32)
                        layer_norm_stats(dve, tiles(X[:, rb, :, :, :]), one, ln_step, r * 9, var_ready)
                        dve.wait_ge(std_ready, r + 1)
                        layer_norm_scale(dve, one, ln_step, r * 9 + 9, norm_ready)
                        dve.wait_ge(run_loaded[rb], q * 128 + 128)
                        for i in range(GT):
                            g = G[:, rb, i // GROUP, i % GROUP, :]
                            dve.wait_ge(h_ready, r * GT + (i + 1))
                            dve.scalar_tensor_tensor(out=g, in0=g, scalar=keep["has"][:, bass.ds(r * GT + i, 1)],
                                                     in1=H[:, i // GROUP, i % GROUP, :], op0=ALU.mult, op1=ALU.add
                                                     ).then_inc(added, 1)
                        dve.wait_ge(added, r * GT + GT)
                        layer_norm_stats(dve, tiles(G[:, rb, :, :, :]), two, ln2_step, r * 9, var2_ready)
                        dve.wait_ge(std2_ready, r + 1)
                        layer_norm_scale(dve, two, ln2_step, r * 9 + 9, norm2_ready)
                        dve.wait_ge(stored, r * 32)
                        dve.tensor_copy(O[:, :, :, F:XW].rearrange("p b j c -> p (b j) c"),
                                        over(keep["dis"][:, bass.ds(r * GT, GT)].unsqueeze(2), [P, GT, XW - F])).then_inc(times_gamma, 1)
                        for i in range(GT):
                            g = G[:, rb, i // GROUP, i % GROUP, :]
                            dve.wait_ge(n_ready, r * GT + (i + 1))
                            dve.tensor_tensor(g, g, gamma[:, :], ALU.mult).then_inc(times_gamma, 1)
                        for i in range(GT):
                            g = G[:, rb, i // GROUP, i % GROUP, :]
                            if i % GROUP == 0:
                                dve.wait_ge(res_ready, r * 2 + (i // GROUP + 1))
                            dve.wait_ge(times_gamma, r * 9 + (i + 2))
                            dve.tensor_tensor(O[:, i // GROUP, i % GROUP, 0:F], g, X[:, rb, i // GROUP, i % GROUP, :],
                                              ALU.add).then_inc(out_ready, 2)


def layer2_edges(nc, core, a, keep, x2, T2):
    sem = core.sem
    go = sem("f_go")
    x_loaded = [sem("f_x0"), sem("f_x1")]
    ln_step, var_ready, std_ready, norm_ready, h_ready = (sem("f_" + n) for n in ("lnstep", "var", "std", "norm", "h"))
    init, masked, carry_ready, match_ready, sum_ready, out_ready = (
        sem("f_" + n) for n in ("init", "masked", "carry", "match", "sum", "out"))
    y_hi, y_lo, bulk_ready = sem("f_yhi"), sem("f_ylo"), sem("f_bulk")
    stored = [sem(f"f_st{b}") for b in range(GROUP)]
    GT = 2 * GROUP
    W = XW
    HW = W // 2
    with ExitStack() as st:
        sb = lambda n, s, d=F32: core.sb(st, "f_" + n, s, d)
        X = sb("X", [P, ET, XW])
        stt = core.stats(st, "f")
        carry = sb("carry", [1, 2, HW])
        match = sb("match", [P, 2, GROUP, P], F32R)
        Yh, Yl = sb("Yh", [P, GROUP, W], F32R), sb("Yl", [P, GROUP, W], F32R)
        T = sb("T", [P, GROUP, W])
        s = core.ps(st, "f_s_ps", [P, 2 * GROUP, 512])

        def tile(r, i, width=F):
            return X[:, bass.ds(r * GT + i, 1), 0:width].rearrange("p o f -> p (o f)")

        with nc.Block() as block:
            @block.sync
            def _(sp):
                with sp.Fori(0, EG) as g:
                    for j in range(GROUP):
                        sp.wait_ge(out_ready, g * GROUP + (j + 1 + GROUP))
                        sp.dma_start(T2[bass.ds((g * GROUP + j) * P, P), :], T[:, j, 0:F + 2]).then_inc(stored[j], 16)
                for j in range(GROUP):
                    sp.wait_ge(stored[j], 16 * EG)

            @block.gpsimd
            def _(pool):
                for t in range(ET):
                    r, i = t // GT, t % GT
                    if i == 0 and r >= 2:
                        pool.wait_ge(x_loaded[r % 2], 128 * (r // 2))
                        pool.sem_inc(go, 1)
                    pool.indirect_dma_start(X[:, t, :], None, x2[:, :], bass.IndirectOffsetOnAxis(keep["src"][:, t:t + 1], 0),
                                            bounds_check=ROWS_N - 1, oob_is_err=False).then_inc(x_loaded[r % 2], 16)

            @block.scalar
            def _(act):
                def norm_row(r, i):
                    relu_norm(act, tile(r, i), tile(r, i), stt, i).then_inc(h_ready, 1)

                def root(r):
                    act.wait_ge(var_ready, r * GT + GT)
                    layer_norm_std(act, stt, keep["eps"]).then_inc(std_ready, 1)
                    act.wait_ge(norm_ready, r + 1)

                def split(r, i):
                    act.wait_ge(h_ready, r * GT + (i + 1))
                    act.wait_ge(masked, r + (i // GT + 1))
                    act.wait_ge(bulk_ready, r * GT + (i + 1))
                    act.copy(Yh[:, i % GROUP, :], tile(r, i, W)).then_inc(y_hi, 1)

                def round_(r, last):
                    for i in range(GT):
                        for h in range(2):
                            act.wait_ge(sum_ready, r * (2 * GT) + (2 * i + h + 1))
                            act.copy(carry[0:1, h, :], s[0:1, 2 * (i % GROUP) + h, 0:HW]).then_inc(carry_ready, 1)
                        if not (last and i >= GT - 2):
                            split(r, i + 2)
                        if i >= GROUP and not last:
                            if i == GROUP:
                                root(r + 1)
                            norm_row(r + 1, 2 * i - GT)
                            norm_row(r + 1, 2 * i - GT + 1)

                root(0)
                for i in range(GT):
                    norm_row(0, i)
                split(0, 0)
                split(0, 1)
                with act.Fori(0, ER - 1) as r:
                    round_(r, False)
                round_(ER - 1, True)

            @block.vector
            def _(dve):
                dve.memset(carry[:, :, :], 0.0).then_inc(init, 1)

                def stats(r, i):
                    dve.bn_stats(stt["raw"][:, i, :], tile(r, i)).then_inc(ln_step, 1)

                def scale(r):
                    ends = X[:, bass.ds(r * GT, GT), F:XW]
                    own = X[0:1, bass.ds(r * GT, GT), F:XW]
                    dve.tensor_scalar(own, own, 0.0, None, ALU.mult).then_inc(masked, 1)
                    dve.wait_ge(ln_step, r * 10 + GT)
                    dve.sem_inc(stt["go"], 1)
                    for i in range(GT):
                        dve.bn_aggr(stt["mv"][:, i, :], stt["raw"][:, i, :]).then_inc(var_ready, 1)
                    dve.wait_ge(masked, r + 1)
                    dve.wait_ge(std_ready, r + 1)
                    layer_norm_scale(dve, stt, ln_step, r * 10 + 9, norm_ready, ends[:, :, 0])

                def build_match(g, b):
                    dve.tensor_tensor(match[:, b, :, :], keep["rows"][:, bass.ds(g * (GROUP * P), GROUP * P)].rearrange("p (j q) -> p j q", q=P),
                                      over(keep["dst"][:, bass.ds(g * GROUP, GROUP)].unsqueeze(2), [P, GROUP, P]),
                                      ALU.is_equal).then_inc(match_ready, 1)

                def split(r, i):
                    dve.wait_ge(y_hi, r * GT + (i + 1))
                    dve.tensor_tensor(Yl[:, i % GROUP, :], tile(r, i, W), Yh[:, i % GROUP, :].bitcast(F32),
                                      ALU.subtract).then_inc(y_lo, 1)

                def round_(r, last, loaded):
                    for i in range(GT):
                        j = i % GROUP
                        if i == 0:
                            build_match(r * 2 + 1, 1)
                        if i == GROUP and not last:
                            build_match(r * 2 + 2, 0)
                        if i < GROUP and not last:
                            if i == 0:
                                for b in range(2):
                                    dve.wait_ge(x_loaded[b], loaded[b])
                            stats(r + 1, 2 * i)
                            stats(r + 1, 2 * i + 1)
                        if not (last and i >= GT - 2):
                            split(r, i + 2)
                        dve.wait_ge(carry_ready, r * (2 * GT) + (2 * i + 3))
                        dve.wait_ge(stored[j], r * 32 + 16 * (i // GROUP))
                        dve.tensor_copy(T[:, j, :].rearrange("p (a f) -> p a f", a=2), s[:, 2 * j:2 * j + 2, 0:HW]).then_inc(out_ready, 1)
                        if i == GROUP - 1 and not last:
                            scale(r + 1)

                dve.wait_ge(x_loaded[0], 128)
                for i in range(GT):
                    stats(0, i)
                scale(0)
                build_match(0, 0)
                split(0, 0)
                split(0, 1)
                with dve.Fori(0, 2) as q:
                    round_(q * 2, False, (q * 128 + 128, q * 128 + 128))
                    round_(q * 2 + 1, False, (q * 128 + 256, q * 128 + 128))
                round_(ER - 1, True, None)

            @block.tensor
            def _(pe):
                pe.sem_inc(out_ready, GROUP)
                pe.sem_inc(bulk_ready, GROUP)
                pe.sem_inc(carry_ready, 1)
                pe.wait_ge(init, 1)
                with pe.Fori(0, ER) as r:
                    for i in range(GT):
                        j, b = i % GROUP, i // GROUP
                        t = r * GT + i
                        if j == 0:
                            pe.wait_ge(match_ready, r * 2 + (b + 1))
                        pe.wait_ge(y_lo, t + 1)
                        pe.wait_ge(out_ready, t + 1)
                        for h in range(2):
                            w = slice(HW * h, HW * h + HW)
                            pe.matmul(s[:, 2 * j + h, 0:HW], match[:, b, j, :], Yh[:, j, w], start=True, stop=False)
                            mm = pe.matmul(s[:, 2 * j + h, 0:HW], match[:, b, j, :], Yl[:, j, w], start=False, stop=False)
                        mm.then_inc(bulk_ready, 1)
                        for h in range(2):
                            pe.wait_ge(carry_ready, t * 2 + h)
                            pe.matmul(s[:, 2 * j + h, 0:HW], match[0:1, b, j, :].bitcast(F32), carry[0:1, h, :],
                                      start=False, stop=True).then_inc(sum_ready, 1)


def layer2_nodes(nc, core, a, keep, x2, T2, x3):
    sem = core.sem
    w_loaded, w_hi, w_lo, init = sem("g_w"), sem("g_whi"), sem("g_wlo"), sem("g_init")
    idx_staged, go = sem("g_idx"), sem("g_go")
    x_loaded = [sem("g_x0"), sem("g_x1")]
    run_loaded = sem("g_run")
    ln_step, var_ready, std_ready, norm_ready, h_ready = (sem("g_" + n) for n in ("lnstep", "var", "std", "norm", "h"))
    a_ready, ns_step = sem("g_a"), sem("g_ns")
    tp_ready, tp_free, hT_hi = sem("g_tp"), sem("g_tpfree"), sem("g_hThi")
    o_ready, biased, out_ready, stored = sem("g_o"), sem("g_biased"), sem("g_out"), [sem("g_st0"), sem("g_st1")]
    GT = 2 * GROUP
    TW = F + 2
    with ExitStack() as st:
        sb = lambda n, s, d=F32: core.sb(st, "g_" + n, s, d)
        X = sb("X", [P, 2, 2, GROUP, XW])
        G = sb("G", [P, 2, GROUP, TW])
        H = sb("H", [P, 2, GROUP, F])
        V = sb("V", [P, 2, F])
        idx = sb("idx", [P, GT], I32)
        stt = core.stats(st, "g")
        ns = sb("ns", [P, 2, GT])
        hTh, hTl = sb("hTh", [P, 2, KF, GROUP * P], F32R), sb("hTl", [P, 2, KF, GROUP * P], F32R)
        Wraw = sb("Wraw", [P, KF, F])
        Wh, Wl = sb("Wh", [P, KF, F], F32R), sb("Wl", [P, KF, F], F32R)
        bias = sb("bias", [P, F])
        tp = core.ps(st, "g_tp_ps", [P, 2, 512])
        o = core.ps(st, "g_o_ps", [P, 4, 512])
        with nc.Block() as block:
            @block.sync
            def _(sp):
                def load(q, rb):
                    for b in range(2):
                        sp.dma_start(X[:, rb, b, :, :], group_rows(x2, q * 4 + (2 * rb + b), XW)).then_inc(x_loaded[rb], 16)

                load(0, 0)
                sp.dma_start(Wraw[:, :, :], a["W2nT"].rearrange("(k p) n -> p k n", p=P)).then_inc(w_loaded, 16)
                sp.dma_start(bias[:, :], a["L2_gnn_b"].rearrange("(o n) -> o n", o=1).broadcast_to([P, F])).then_inc(w_loaded, 16)
                load(0, 1)

                def store(q, rb):
                    for b in range(2):
                        sp.wait_ge(out_ready, q * 16 + (8 * rb + 4 * b + 4))
                        sp.dma_start(group_rows(x3, q * 4 + (2 * rb + b), F), X[:, rb, b, :, 0:F]).then_inc(stored[rb], 16)

                with sp.Fori(0, NR // 2 - 1) as q:
                    for rb in range(2):
                        store(q, rb)
                        sp.wait_ge(stored[rb], q * 32 + 32)
                        load(q + 1, rb)
                for rb in range(2):
                    store(NR // 2 - 1, rb)
                    if rb == 0:
                        sp.wait_ge(stored[0], 16 * NR)
                        load(0, 0)
                sp.wait_ge(stored[0], 16 * NR)
                sp.wait_ge(stored[1], 16 * NR)
                sp.wait_ge(x_loaded[0], 16 * NR + 32)

            @block.gpsimd
            def _(pool):
                pool.memset(G[:, :, :, :], 0.0).then_inc(init, 1)
                pool.wait_ge(init, 1)
                with pool.Fori(0, NR) as r:
                    pool.tensor_copy(idx[:, :], keep["slot"][:, bass.ds(r * GT, GT)]).then_inc(idx_staged, 1)
                    pool.wait_ge(idx_staged, r + 1)
                    pool.wait_ge(a_ready, r * GT)
                    pool.wait_ge(ns_step, r * 2)
                    pool.sem_inc(go, 1)
                    for i in range(GT):
                        pool.indirect_dma_start(G[:, i // GROUP, i % GROUP, :], None, T2[:, :],
                                                bass.IndirectOffsetOnAxis(idx[:, i:i + 1], 0),
                                                bounds_check=ROWS_E - 1, oob_is_err=False).then_inc(run_loaded, 16)
                    pool.wait_ge(run_loaded, r * 128 + 128)
                    pool.sem_inc(go, 1)

            @block.scalar
            def _(act):
                def norm(r, rb):
                    act.wait_ge(var_ready, r * GT + GT)
                    layer_norm_std(act, stt, keep["eps"]).then_inc(std_ready, 1)
                    act.wait_ge(norm_ready, r + 1)
                    act.wait_ge(a_ready, r * GT)
                    act.wait_ge(tp_ready, r * GT)
                    for i, x in enumerate(tiles(X[:, rb, :, :, :])):
                        relu_norm(act, H[:, i // GROUP, i % GROUP, :], x, stt, i).then_inc(h_ready, 1)

                norm(0, 0)
                split_on_act(act, Wraw[:, :, :], Wh[:, :, :], w_loaded, 32, w_hi)
                with act.Fori(0, NR // 2) as q:
                    for rb in range(2):
                        r = q * 2 + rb
                        for b in range(2):
                            for c in range(KF):
                                k = KF * b + c
                                act.wait_ge(tp_ready, r * GT + (k + 1))
                                act.copy(hTh[:, b, c, :], tp[:, k % 2, :]).then_inc(hT_hi, 1)
                        norm(r + 1, 1 - rb)

            @block.vector
            def _(dve):
                def norm(r, rb, loaded):
                    dve.wait_ge(x_loaded[rb], loaded)
                    layer_norm_stats(dve, tiles(X[:, rb, :, :, :]), stt, ln_step, r * 10, var_ready)
                    dve.wait_ge(std_ready, r + 1)
                    layer_norm_scale(dve, stt, ln_step, r * 10 + 9, norm_ready,
                                     keep["dis2"][:, bass.ds(r * GT, GT)])

                norm(0, 0, 32)
                split_on_dve(dve, Wraw[:, :, :], Wh[:, :, :], Wl[:, :, :], w_hi, 1, w_lo)
                with dve.Fori(0, NR // 2) as q:
                    for rb in range(2):
                        r = q * 2 + rb
                        dve.wait_ge(run_loaded, r * 128 + 128)
                        nsr = ns[:, rb, :]
                        dve.tensor_tensor(nsr, G[:, :, :, F:F + 1].rearrange("p b j c -> p (b j c)"),
                                          keep["dish"][:, bass.ds(r * GT, GT)], ALU.mult).then_inc(ns_step, 1)
                        dve.wait_ge(ns_step, r * 2 + 1)
                        dve.tensor_tensor(nsr, nsr, keep["dis2"][:, bass.ds(r * GT, GT)], ALU.add).then_inc(ns_step, 1)
                        for i in range(GT):
                            h = H[:, i // GROUP, i % GROUP, :]
                            dve.wait_ge(h_ready, r * GT + (i + 1))
                            dve.scalar_tensor_tensor(out=h, in0=G[:, i // GROUP, i % GROUP, 0:F],
                                                     scalar=keep["dish"][:, bass.ds(r * GT + i, 1)], in1=h,
                                                     op0=ALU.mult, op1=ALU.add).then_inc(a_ready, 1)
                        for b in range(2):
                            for c in range(KF):
                                k = KF * b + c
                                dve.wait_ge(hT_hi, r * GT + (k + 1))
                                dve.tensor_tensor(hTl[:, b, c, :], tp[:, k % 2, :], hTh[:, b, c, :].bitcast(F32),
                                                  ALU.subtract).then_inc(tp_free, 1)
                        norm(r + 1, 1 - rb, q * 32 + (64 if rb else 32))
                        dve.wait_ge(ns_step, r * 2 + 2)
                        for i in range(GT):
                            x = X[:, rb, i // GROUP, i % GROUP, 0:F]
                            dve.wait_ge(o_ready, r * GT + (i + 1))
                            if i >= 2:
                                dve.wait_ge(out_ready, r * GT + (i - 1))
                            dve.scalar_tensor_tensor(out=V[:, i % 2, :], in0=bias[:, :], scalar=ns[:, rb, i:i + 1],
                                                     in1=o[:, i % 4, :], op0=ALU.mult, op1=ALU.add).then_inc(biased, 1)
                            dve.wait_ge(biased, r * GT + (i + 1))
                            dve.scalar_tensor_tensor(out=x, in0=V[:, i % 2, :], scalar=0.0, in1=x, op0=ALU.max, op1=ALU.add
                                                     ).then_inc(out_ready, 1)

            @block.tensor
            def _(pe):
                pe.sem_inc(tp_free, 2)
                pe.wait_ge(w_lo, 1)
                with pe.Fori(0, NR) as r:
                    for b in range(2):
                        pe.wait_ge(a_ready, r * GT + (GROUP * b + GROUP))
                        for c in range(KF):
                            k = KF * b + c
                            pe.wait_ge(tp_free, r * GT + (k + 1))
                            for j in range(GROUP):
                                mm = pe.transpose(tp[:, k % 2, j * P:(j + 1) * P], H[:, b, j, c * P:(c + 1) * P], keep["ident"][:, :])
                            mm.then_inc(tp_ready, 1)
                    for b in range(2):
                        pe.wait_ge(tp_free, r * GT + (KF * b + KF + 2))
                        for j in range(GROUP):
                            i = GROUP * b + j
                            if i < 4:
                                pe.wait_ge(biased, r * GT)
                            else:
                                pe.wait_ge(biased, r * GT + (i - 3))
                            for c in range(KF):
                                mm = three(pe, o[:, i % 4, :], (hTh[:, b, c, j * P:(j + 1) * P], hTl[:, b, c, j * P:(j + 1) * P]),
                                           (Wh[:, c, :], Wl[:, c, :]), c == 0, c == KF - 1)
                            mm.then_inc(o_ready, 1)


def layer3_edges(nc, core, a, keep, x3, T3):
    sem = core.sem
    w_loaded, w_hi, w_lo, const_ready, const_out, init = (sem("h_" + n) for n in ("w", "whi", "wlo", "const", "constout", "init"))
    go = sem("h_go")
    x_loaded = [sem("h_x0"), sem("h_x1")]
    ln_step, var_ready, std_ready, norm_ready, h_ready = (sem("h_" + n) for n in ("lnstep", "var", "std", "norm", "h"))
    tp_ready, tp_free, hT_hi = sem("h_tp"), sem("h_tpfree"), sem("h_hThi")
    m_ready, m_out, y_ready, y_out, match_ready = sem("h_m"), sem("h_mout"), sem("h_y"), sem("h_yout"), sem("h_match")
    row_ready, next_ready, carry_ready, sum_ready = (sem("h_" + n) for n in ("row", "next", "carry", "sum"))
    sum_hi, sum_lo, z_ready, z_out = sem("h_sumhi"), sem("h_sumlo"), sem("h_z"), sem("h_zout")
    stored = [sem(f"h_st{b}") for b in range(GROUP)]
    D = FE
    GP = GROUP * P
    with ExitStack() as st:
        sb = lambda n, s, d=F32: core.sb(st, "h_" + n, s, d)
        X = sb("X", [P, ET, F])
        H = sb("H", [P, 2, GROUP, F])
        stt = core.stats(st, "h")
        hTh, hTl = sb("hTh", [P, KF, GP], F32R), sb("hTl", [P, KF, GP], F32R)
        Wraw, Wh, Wl = sb("Wraw", [P, KF, D]), sb("Wh", [P, KF, D], F32R), sb("Wl", [P, KF, D], F32R)
        Wf, Wfh, Wfl = sb("Wf", [P, F]), sb("Wfh", [P, F], F32R), sb("Wfl", [P, F], F32R)
        bg, bgw = sb("bg", [P, 1]), sb("bgw", [P, P])
        bf, const = sb("bf", [P, F]), sb("const", [P, F])
        M = sb("M", [P, GP])
        Y = sb("Y", [P, GROUP, D])
        carry = sb("carry", [1, D])
        match = sb("match", [P, 2, GROUP, P])
        Sh, Sl = sb("Sh", [P, GP], F32R), sb("Sl", [P, GP], F32R)
        Z = sb("Z", [P, GROUP, F])
        tp = core.ps(st, "h_tp_ps", [P, 2, 512])
        m = core.ps(st, "h_m_ps", [P, 512])
        y = core.ps(st, "h_y_ps", [P, 512])
        sT = core.ps(st, "h_s_ps", [P, 512])
        nx = core.ps(st, "h_nx_ps", [P, 512])
        z = core.ps(st, "h_z_ps", [P, 2, 512])

        def both(b):
            return slice(GROUP * b, GROUP * b + GROUP)

        def rounds(engine, body):
            with engine.Fori(0, ER - 1) as r:
                for b in range(2):
                    body(r * 2 + b, b, True, True)
            body(EG - 2, 0, True, False)
            body(EG - 1, 1, False, False)

        with nc.Block() as block:
            @block.sync
            def _(sp):
                sp.dma_start(Wraw[:, :, :], a["L3_gnn_W_gcn"].rearrange("(k p) n -> p k n", p=P)).then_inc(w_loaded, 16)
                sp.dma_start(Wf[:, :], a["WfT"]).then_inc(w_loaded, 16)
                sp.dma_start(bg[:, :], a["L3_gnn_b_gcn"].rearrange("(p o) -> p o", o=1)).then_inc(w_loaded, 16)
                sp.dma_start(bf[:, :], a["L3_gnn_b_fc"].rearrange("(o n) -> o n", o=1).broadcast_to([P, F])).then_inc(w_loaded, 16)
                with sp.Fori(0, EG) as g:
                    for j in range(GROUP):
                        sp.wait_ge(z_out, g * GROUP + (j + 1 + 2))
                        sp.dma_start(T3[bass.ds((g * GROUP + j) * P, P), :], Z[:, j, :]).then_inc(stored[j], 16)
                for j in range(GROUP):
                    sp.wait_ge(stored[j], 16 * EG)

            @block.gpsimd
            def _(pool):
                for t in range(ET):
                    g, j = t // GROUP, t % GROUP
                    if j == 0 and g >= 2:
                        pool.wait_ge(x_loaded[g % 2], 64 * (g // 2))
                        pool.sem_inc(go, 1)
                    pool.indirect_dma_start(X[:, t, :], None, x3[:, :], bass.IndirectOffsetOnAxis(keep["src"][:, t:t + 1], 0),
                                            bounds_check=ROWS_N - 1, oob_is_err=False).then_inc(x_loaded[g % 2], 16)

            @block.scalar
            def _(act):
                def root(g, b):
                    act.wait_ge(var_ready, g * 4 + 4)
                    act.activation(stt["std"][:, both(b)], stt["mv"][:, both(b), 1], ACT.Sqrt, bias=keep["eps"][:, 0:1]).then_inc(std_ready, 1)

                def norm_rows(g, b, rows):
                    act.wait_ge(norm_ready, g + 1)
                    for j in rows:
                        relu_norm(act, H[:, b, j, :], X[:, bass.ds(g * GROUP + j, 1), :].rearrange("p o f -> p (o f)"),
                                  stt, GROUP * b + j).then_inc(h_ready, 1)

                def turned(g, c):
                    act.wait_ge(m_ready, g)
                    act.wait_ge(tp_ready, g * 4 + (c + 1))
                    act.copy(hTh[:, c, :], tp[:, c % 2, :]).then_inc(hT_hi, 1)

                def messages(g):
                    act.wait_ge(m_ready, g + 1)
                    act.wait_ge(y_ready, g)
                    act.copy(M[:, :], m[:, :]).then_inc(m_out, 1)

                def first_row(g):
                    act.wait_ge(y_out, g + 1)
                    act.wait_ge(carry_ready, g)
                    act.copy(Y[0:1, 0, :], carry[0:1, :]).then_inc(row_ready, 1)

                def body(g, b, turn, norm):
                    for j in range(GROUP):
                        act.wait_ge(next_ready, g * GROUP + (j + 1))
                        if j < GROUP - 1:
                            act.copy(Y[0:1, j + 1, :], nx[0:1, 0:D]).then_inc(row_ready, 1)
                        else:
                            act.wait_ge(row_ready, g * GROUP + (j + 1))
                            act.copy(carry[0:1, :], nx[0:1, 0:D]).then_inc(carry_ready, 1)
                        if turn:
                            turned(g + 1, j)
                    act.wait_ge(sum_ready, g + 1)
                    act.wait_ge(z_ready, g * GROUP)
                    act.copy(Sh[:, :], sT[:, :]).then_inc(sum_hi, 1)
                    if norm:
                        root(g + 2, b)
                        norm_rows(g + 2, b, (0, 1))
                    if turn:
                        messages(g + 1)
                    if norm:
                        norm_rows(g + 2, b, (2, 3))
                    if turn:
                        first_row(g + 1)

                for g in range(2):
                    root(g, g)
                    norm_rows(g, g, range(GROUP))
                split_on_act(act, Wraw[:, :, :], Wh[:, :, :], w_loaded, 64, w_hi)
                split_on_act(act, Wf[:, :], Wfh[:, :], w_loaded, 64, w_hi)
                for c in range(KF):
                    turned(0, c)
                messages(0)
                act.wait_ge(init, 1)
                first_row(0)
                rounds(act, body)

            @block.vector
            def _(dve):
                def stats(g, b, j):
                    dve.bn_stats(stt["raw"][:, GROUP * b + j, :], X[:, bass.ds(g * GROUP + j, 1), :].rearrange("p o f -> p (o f)")
                                 ).then_inc(ln_step, 1)

                def mean(g, b):
                    dve.wait_ge(ln_step, g * 5 + 4)
                    dve.sem_inc(stt["go"], 1)
                    for i in range(GROUP * b, GROUP * b + GROUP):
                        dve.bn_aggr(stt["mv"][:, i, :], stt["raw"][:, i, :]).then_inc(var_ready, 1)

                def scale(g, b):
                    n = both(b)
                    dve.wait_ge(std_ready, g + 1)
                    dve.reciprocal(stt["rstd"][:, n], stt["std"][:, n]).then_inc(ln_step, 1)
                    dve.wait_ge(ln_step, g * 5 + 5)
                    dve.scalar_tensor_tensor(out=stt["shift"][:, n], in0=stt["mv"][:, n, 0], scalar=-1.0, in1=stt["rstd"][:, n],
                                             op0=ALU.mult, op1=ALU.mult).then_inc(norm_ready, 1)

                def build_match(g, b):
                    dve.tensor_tensor(match[:, b, :, :], keep["rows"][:, bass.ds(g * GP, GP)].rearrange("p (j q) -> p j q", q=P),
                                      over(keep["dst"][:, bass.ds(g * GROUP, GROUP)].unsqueeze(2), [P, GROUP, P]),
                                      ALU.is_equal).then_inc(match_ready, 1)

                def turned(g, c):
                    dve.wait_ge(hT_hi, g * 4 + (c + 1))
                    dve.tensor_tensor(hTl[:, c, :], tp[:, c % 2, :], hTh[:, c, :].bitcast(F32), ALU.subtract).then_inc(tp_free, 1)

                def weigh(g):
                    dve.wait_ge(y_ready, g + 1)
                    dve.tensor_tensor(Y[:, :, :], y[:, :].rearrange("p (j d) -> p j d", d=D),
                                      over(keep["wgt"][:, bass.ds(g * GROUP, GROUP)].unsqueeze(2), [P, GROUP, D]),
                                      ALU.mult).then_inc(y_out, 1)

                def out(g, j):
                    dve.wait_ge(z_ready, g * GROUP + (j + 1))
                    dve.wait_ge(stored[j], g * 16)
                    dve.tensor_tensor(Z[:, j, :], z[:, j % 2, :], const[:, :], ALU.add).then_inc(z_out, 1)

                def body(g, b, turn, norm):
                    if turn:
                        build_match(g + 1, 1 - b)
                    if norm:
                        dve.wait_ge(x_loaded[b], g * 32 + (128 - 32 * b))
                    for j in range(GROUP):
                        if norm:
                            stats(g + 2, b, j)
                        if turn:
                            turned(g + 1, j)
                    if norm:
                        mean(g + 2, b)
                    dve.wait_ge(sum_hi, g + 1)
                    dve.tensor_tensor(Sl[:, :], sT[:, :], Sh[:, :].bitcast(F32), ALU.subtract).then_inc(sum_lo, 1)
                    if norm:
                        scale(g + 2, b)
                    out(g, 0)
                    out(g, 1)
                    if turn:
                        weigh(g + 1)
                    out(g, 2)
                    out(g, 3)

                dve.memset(carry[:, :], 0.0).then_inc(init, 1)
                for g in range(2):
                    dve.wait_ge(x_loaded[g], 64)
                    for j in range(GROUP):
                        stats(g, g, j)
                    mean(g, g)
                    scale(g, g)
                split_on_dve(dve, Wraw[:, :, :], Wh[:, :, :], Wl[:, :, :], w_hi, 1, w_lo)
                split_on_dve(dve, Wf[:, :], Wfh[:, :], Wfl[:, :], w_hi, 2, w_lo)
                dve.tensor_copy(bgw[:, :], over(bg[:, 0:1], [P, P])).then_inc(w_lo, 1)
                build_match(0, 0)
                for c in range(KF):
                    turned(0, c)
                dve.wait_ge(const_ready, 1)
                dve.tensor_tensor(const[:, :], z[:, 0, :], bf[:, :], ALU.add).then_inc(const_out, 1)
                weigh(0)
                dve.wait_ge(const_out, 1)
                rounds(dve, body)

            @block.tensor
            def _(pe):
                def turn(g, b, c):
                    pe.wait_ge(h_ready, g * 4 + 4)
                    pe.wait_ge(tp_free, g * 4 + (c + 1))
                    for j in range(GROUP):
                        mm = pe.transpose(tp[:, c % 2, j * P:(j + 1) * P], H[:, b, j, c * P:(c + 1) * P], keep["ident"][:, :])
                    mm.then_inc(tp_ready, 1)

                def product(g):
                    pe.wait_ge(m_out, g)
                    for c in range(KF):
                        pe.wait_ge(tp_free, g * 4 + (c + 1 + 2))
                        mm = three(pe, m[:, :], (Wh[:, c, :], Wl[:, c, :]), (hTh[:, c, :], hTl[:, c, :]), c == 0, c == KF - 1)
                    mm.then_inc(m_ready, 1)

                def turn_back(g):
                    pe.wait_ge(m_out, g + 1)
                    pe.wait_ge(y_out, g)
                    for j in range(GROUP):
                        mm = pe.transpose(y[:, j * P:(j + 1) * P], M[:, j * P:(j + 1) * P], keep["ident"][:, :])
                    mm.then_inc(y_ready, 1)

                def out(g, j):
                    pe.wait_ge(z_out, g * GROUP + (j + 1))
                    three(pe, z[:, j % 2, :], (Sh[:, j * P:(j + 1) * P], Sl[:, j * P:(j + 1) * P]),
                          (Wfh[:, :], Wfl[:, :]), True, True).then_inc(z_ready, 1)

                def body(g, b, following, norm):
                    pe.wait_ge(match_ready, g + 1)
                    for j in range(GROUP):
                        pe.wait_ge(row_ready, g * GROUP + (j + 1))
                        if j == 0:
                            pe.wait_ge(carry_ready, g)
                        pe.matmul(nx[0:1, 0:D], match[:, b, j, 0:1], Y[:, j, :], start=True, stop=True).then_inc(next_ready, 1)
                        if j == 0:
                            pe.wait_ge(sum_lo, g)
                        mm = pe.matmul(sT[:, j * P:(j + 1) * P], Y[:, j, :], match[:, b, j, :], start=True, stop=True)
                        if j == GROUP - 1:
                            mm.then_inc(sum_ready, 1)
                        if following:
                            turn(g + 1, 1 - b, j)
                    if following:
                        product(g + 1)
                    pe.wait_ge(sum_lo, g + 1)
                    out(g, 0)
                    out(g, 1)
                    if following:
                        turn_back(g + 1)
                    out(g, 2)
                    out(g, 3)

                pe.sem_inc(tp_free, 2)
                pe.sem_inc(z_out, 2)
                for c in range(KF):
                    turn(0, 0, c)
                pe.wait_ge(w_lo, 3)
                pe.matmul(z[:, 0, :], bgw[:, :], Wf[:, :], start=True, stop=True).then_inc(const_ready, 1)
                product(0)
                turn_back(0)
                pe.wait_ge(const_out, 1)
                rounds(pe, body)


def layer3_nodes(nc, core, a, keep, x3, T3, out):
    sem = core.sem
    w_loaded, wide, const_ready, const_out = sem("i_w"), sem("i_wide"), sem("i_const"), sem("i_constout")
    idx_staged, go, filled = sem("i_idx"), sem("i_go"), sem("i_fill")
    x_loaded, run_loaded, stored = ([sem(f"i_{n}{b}") for b in range(2)] for n in ("x", "g", "st"))
    out_ready = sem("i_out")
    with ExitStack() as st:
        sb = lambda n, s, d=F32: core.sb(st, "i_" + n, s, d)
        X = sb("X", [P, 2, GROUP, F])
        G = sb("G", [P, 2, GROUP, F])
        idx = sb("idx", [P, 2, GROUP], I32)
        Wf, bf, const = sb("Wf", [P, F]), sb("bf", [P, F]), sb("const", [P, F])
        bg, bgw = sb("bg", [P, 1]), sb("bgw", [P, P])
        z = core.ps(st, "i_z_ps", [P, 512])
        with nc.Block() as block:
            @block.sync
            def _(sp):
                sp.dma_start(Wf[:, :], a["WfT"]).then_inc(w_loaded, 16)
                sp.dma_start(bg[:, :], a["L3_gnn_b_gcn"].rearrange("(p o) -> p o", o=1)).then_inc(w_loaded, 16)
                sp.dma_start(bf[:, :], a["L3_gnn_b_fc"].rearrange("(o n) -> o n", o=1).broadcast_to([P, F])).then_inc(w_loaded, 16)
                with sp.Fori(0, NR) as r:
                    for b in range(2):
                        sp.wait_ge(stored[b], r * 16)
                        sp.dma_start(X[:, b, :, :], group_rows(x3, r * 2 + b, F)).then_inc(x_loaded[b], 16)

            @block.gpsimd
            def _(pool):
                with pool.Fori(0, NR) as r:
                    for b in range(2):
                        g = r * 2 + b
                        pool.wait_ge(run_loaded[b], r * 64)
                        pool.sem_inc(go, 1)
                        pool.tensor_copy(idx[:, b, :], keep["slot"][:, bass.ds(g * GROUP, GROUP)]).then_inc(idx_staged, 1)
                        pool.wait_ge(idx_staged, g + 1)
                        pool.wait_ge(filled, g + 1)
                        pool.sem_inc(go, 1)
                        for i in range(GROUP):
                            pool.indirect_dma_start(G[:, b, i, :], None, T3[:, :], bass.IndirectOffsetOnAxis(idx[:, b, i:i + 1], 0),
                                                    bounds_check=ROWS_E - 1, oob_is_err=False).then_inc(run_loaded[b], 16)

            @block.scalar
            def _(act):
                def fill(b):
                    act.copy(G[:, b, :, :], over(const[:, :].unsqueeze(1), [P, GROUP, F])).then_inc(filled, 1)

                act.wait_ge(const_out, 1)
                fill(0)
                fill(1)
                with act.Fori(0, NR - 1) as r:
                    for b in range(2):
                        act.wait_ge(out_ready, r * 2 + (b + 1))
                        act.dma_start(group_rows(out, r * 2 + b, F), X[:, b, :, :]).then_inc(stored[b], 16)
                        fill(b)
                act.wait_ge(out_ready, NG - 1)
                act.dma_start(group_rows(out, NG - 2, F), X[:, 0, :, :]).then_inc(stored[0], 16)
                act.wait_ge(out_ready, NG)
                at = (NG - 1) * GROUP * P
                for j in range((NODES - at + P - 1) // P):
                    n = min(P, NODES - at - j * P)
                    act.dma_start(out[at + j * P:at + j * P + n, :], X[0:n, 1, j, :]).then_inc(stored[1], 16)
                act.wait_ge(stored[0], 16 * NR)
                act.wait_ge(stored[1], 16 * (NR - 1) + 48)

            @block.vector
            def _(dve):
                dve.wait_ge(w_loaded, 48)
                dve.tensor_copy(bgw[:, :], over(bg[:, 0:1], [P, P])).then_inc(wide, 1)
                dve.wait_ge(const_ready, 1)
                dve.tensor_tensor(const[:, :], z[:, :], bf[:, :], ALU.add).then_inc(const_out, 1)
                with dve.Fori(0, NR) as r:
                    for b in range(2):
                        dve.wait_ge(x_loaded[b], r * 16 + 16)
                        dve.wait_ge(run_loaded[b], r * 64 + 64)
                        dve.tensor_tensor(X[:, b, :, :], X[:, b, :, :], G[:, b, :, :], ALU.add).then_inc(out_ready, 1)

            @block.tensor
            def _(pe):
                pe.wait_ge(wide, 1)
                pe.matmul(z[:, :], bgw[:, :], Wf[:, :], start=True, stop=True).then_inc(const_ready, 1)


def program(nc, a, out, stop_after=9):
    core = Core(nc)
    with core.whole:
        outer = core.whole
        keep = {
            "src": core.sb(outer, "src", [P, ET + 2 * GROUP], I32), "dst": core.sb(outer, "dstk", [P, ET + 2 * GROUP], I32),
            "rows": core.sb(outer, "rows", [P, ROWS_E + GROUP * P], U16), "fac": core.sb(outer, "fac", [P, ET, HEADS]),
            "wgt": core.sb(outer, "wgt", [P, ET]), "ident": core.sb(outer, "ident", [P, P]), "eps": core.sb(outer, "eps", [P, 1]),
            "slot": core.sb(outer, "slot", [P, NT + 8], I32),
        }
        for n in ("dis", "dis2", "has", "dish"):
            keep[n] = core.sb(outer, n, [P, NT + 8])

        def table(name, rows, width, last):
            return out if last == stop_after else nc.dram_tensor(name, (rows, width), F32).ap()

        T0 = table("T0", ROWS_E, IN, 1)
        x1 = table("x1", ROWS_N, F, 2)
        T1 = table("T1", ROWS_E, F, 3)
        x2 = table("x2", ROWS_N, XW, 4)
        T2 = table("T2", ROWS_E, F + 2, 5)
        x3 = table("x3", ROWS_N, F, 6)
        T3 = table("T3", ROWS_E, F, 7)
        with ExitStack() as w:
            l0 = {"W1h": core.sb(w, "W1h", [P, KI, HID], F32R), "W1l": core.sb(w, "W1l", [P, KI, HID], F32R),
                  "W23h": core.sb(w, "W23h", [P, KH, IN], F32R), "W23l": core.sb(w, "W23l", [P, KH, IN], F32R),
                  "b1": core.sb(w, "b1", [P, KH]), "c2": core.sb(w, "c2", [P, IN])}
            core.run(prepare, a, keep, l0)
            core.run(spread_rows, a, keep)
            core.run(layer0_edges, a, keep, l0, T0)
        if stop_after >= 2:
            core.run(layer0_nodes, a, keep, T0, x1)
        if stop_after >= 3:
            with ExitStack() as w:
                msg = core.sb(w, "msg", [P, ET, F + HEADS])
                logit = core.sb(w, "logit", [P, ET, HEADS])
                core.run(layer1_messages, a, keep, x1, msg, logit)
                core.run(layer1_softmax, a, keep, logit)
                core.run(layer1_sums, a, keep, msg, logit, T1)
        if stop_after >= 4:
            core.run(layer1_nodes, a, keep, x1, T1, x2)
        if stop_after >= 5:
            core.run(layer2_edges, a, keep, x2, T2)
        if stop_after >= 6:
            core.run(layer2_nodes, a, keep, x2, T2, x3)
        if stop_after >= 7:
            core.run(layer3_edges, a, keep, x3, T3)
        if stop_after >= 8:
            core.run(layer3_nodes, a, keep, x3, T3, out)


def spread_rows(nc, core, a, keep):
    loaded, packed, spare = core.sem("r_loaded"), core.sem("r_packed"), core.sem("r_spare")
    with ExitStack() as st:
        raw = core.sb(st, "r_raw", [P, ROWS_E // 4], I32)
        with nc.Block() as block:
            @block.sync
            def _(sp):
                for q in range(4):
                    if q:
                        sp.wait_ge(packed, q)
                    sp.dma_start(raw[:, :], a["dst_row"][:, q * 1280:(q + 1) * 1280].broadcast_to([P, 1280])).then_inc(loaded, 16)

            @block.vector
            def _(dve):
                dve.memset(keep["rows"][:, ROWS_E:], 0).then_inc(spare, 1)
                for q in range(4):
                    dve.wait_ge(loaded, 16 * (q + 1))
                    dve.tensor_copy(keep["rows"][:, q * 1280:(q + 1) * 1280], raw[:, :]).then_inc(packed, 1)


def windows(v, np, tiles, front, back):
    at = NEW * np.arange(tiles)[None, :] - 1 + np.arange(P)[:, None]
    w = np.concatenate([np.full((1,) + v.shape[1:], front, v.dtype), v,
                        np.full((tiles * P,) + v.shape[1:], back, v.dtype)])
    return np.ascontiguousarray(w[at + 1])


def lay_out(inputs, np):
    a = {}
    for n in ("x", "L1_gnn_et_emb", "L0_gnn_W1", "L0_gnn_b1", "L0_gnn_b2", "L0_gnn_W3", "L0_gnn_b3", "L0_gnn_W4", "L0_gnn_b4",
              "L1_gnn_W", "L1_gnn_a_src", "L1_gnn_a_dst", "L1_gnn_ln_gamma", "L1_gnn_ln_beta", "L2_gnn_b",
              "L3_gnn_W_gcn", "L3_gnn_b_gcn", "L3_gnn_b_fc"):
        a[n] = np.ascontiguousarray(inputs[n])
    a["W2T"] = np.ascontiguousarray(np.asarray(inputs["L0_gnn_W2"]).T)
    a["W1T"] = np.ascontiguousarray(np.asarray(inputs["L1_gnn_W"]).T)
    a["W2nT"] = np.ascontiguousarray(np.asarray(inputs["L2_gnn_W"]).T)
    a["WfT"] = np.ascontiguousarray(np.asarray(inputs["L3_gnn_W_fc"]).T)
    dst, src = np.asarray(inputs["dst"]), np.asarray(inputs["src"])
    dw = windows(dst, np, ET, NODES + 1, NODES)
    a["dst_win"] = dw
    a["dst_wide"] = windows(dst, np, ET + 2 * GROUP, NODES + 1, NODES)
    nxt = windows(dst, np, ET + 1, NODES + 1, NODES)
    after = np.concatenate([nxt[1:, :ET], nxt[1:2, 1:]])
    after[0] = dw[0]
    a["dst_next"] = np.ascontiguousarray(after)
    sw = windows(src, np, ET + 2 * GROUP, 0, 0)
    a["src_win"] = sw
    count = windows(src, np, ET, ROWS_N, ROWS_N)
    count[0] = ROWS_N
    a["src_count"] = count
    row = dw.T.copy()
    a["dst_flat"] = row.reshape(1, -1).copy()
    row[:, 0] = row[:, P - 1]
    a["dst_row"] = np.ascontiguousarray(row.reshape(1, -1))
    a["type_win"] = windows(np.asarray(inputs["edge_type_8"]), np, ET, 0, 0)
    a["weight_win"] = windows(np.asarray(inputs["edge_weight"]), np, ET, 0, 0)
    at = windows(np.asarray(inputs["edge_attr_128"]), np, ET + 2 * GROUP, 0, 0)
    a["attr_win"] = np.ascontiguousarray(at.reshape(P, EG + 2, GROUP, FE))
    return a


def kernel(**inputs):
    import numpy as _np
    import concourse.bacc as _bacc
    from concourse import mybir as _mybir
    from concourse.bass_utils import run_bass_kernel_spmd as _run

    nc = _bacc.Bacc("TRN2", target_bir_lowering=False, num_devices=1, dynamic_dma_scratch_size=8192)
    arrays = lay_out(inputs, _np)
    args = {n: nc.dram_tensor("in_" + n, v.shape, _mybir.dt.from_np(v.dtype), kind="ExternalInput").ap()
            for n, v in arrays.items()}
    out = nc.dram_tensor("out_0", (NODES, F), _mybir.dt.float32, kind="ExternalOutput").ap()
    program(nc, args, out)
    r = _run(nc, [{"in_" + n: v for n, v in arrays.items()}], core_ids=[0])
    return r.results[0]["out_0"]
```

```python
import concourse.bass as bass
from concourse import mybir
from contextlib import ExitStack

F32 = mybir.dt.float32
F32R = mybir.dt.float32r
I32 = mybir.dt.int32
U32 = mybir.dt.uint32
U16 = mybir.dt.uint16
ALU = mybir.AluOpType
ACT = mybir.ActivationFunctionType

P = 128
NODES = 10000
EDGES = 5000
F = 512
FE = 128
IN = F + FE
HID = 2 * IN
KF = F // P
KI = IN // P
KH = HID // P
HEADS = 8
HD = F // HEADS
GW = F // 2
HALF = IN // 2
GROUP = 4
NEW = P - 1
ET = 40
EG = ET // GROUP
ER = EG // 2
NT = 80
NG = NT // GROUP
NR = NG // 2
ROWS_E = ET * P
ROWS_N = NT * P
EPS = 1e-5
XW = F + 4
FAR = 1.0e6
assert ET * NEW >= EDGES and NT * P >= NODES and (ET - 1) * NEW < EDGES


def group_rows(table, g, cols):
    return table[bass.ds(g * (GROUP * P), GROUP * P), 0:cols].rearrange("(j p) f -> p j f", p=P)


def tiles(x, width=F):
    return [x[:, i // GROUP, i % GROUP, 0:width] for i in range(2 * GROUP)]


def over(ap, shape):
    return ap.broadcast_to(shape)


def layer_norm_stats(dve, rows, st, steps, base, var_ready):
    for i, row in enumerate(rows):
        dve.bn_stats(st["raw"][:, i, :], row).then_inc(steps, 1)
    dve.wait_ge(steps, base + len(rows))
    dve.sem_inc(st["go"], 1)
    for i in range(len(rows)):
        dve.bn_aggr(st["mv"][:, i, :], st["raw"][:, i, :]).then_inc(var_ready, 1)


def layer_norm_std(act, st, eps):
    return act.activation(st["std"][:, :], st["mv"][:, :, 1], ACT.Sqrt, bias=eps[:, 0:1])


def layer_norm_scale(dve, st, steps, base, norm_ready, times=None):
    dve.reciprocal(st["rstd"][:, :], st["std"][:, :]).then_inc(steps, 1)
    dve.wait_ge(steps, base)
    if times is not None:
        dve.tensor_tensor(st["rstd"][:, :], st["rstd"][:, :], times, ALU.mult).then_inc(steps, 1)
        dve.wait_ge(steps, base + 1)
    dve.scalar_tensor_tensor(out=st["shift"][:, :], in0=st["mv"][:, :, 0], scalar=-1.0, in1=st["rstd"][:, :],
                             op0=ALU.mult, op1=ALU.mult).then_inc(norm_ready, 1)


def relu_norm(act, out, x, st, i):
    return act.activation(out, x, ACT.Relu, bias=st["shift"][:, i:i + 1], scale=st["rstd"][:, i:i + 1])


class Core:

    def __init__(self, nc):
        self.nc = nc
        self.whole = ExitStack()
        self.sems = []

    def run(self, build, *args):
        self.sems = []
        build(self.nc, self, *args)
        self.nc.clear_and_free_semaphores(self.sems)
        self.nc.all_engine_barrier()

    def sem(self, name):
        self.sems.append(self.nc.alloc_semaphore(name))
        return self.sems[-1]

    def sb(self, stack, name, shape, dt=F32):
        return stack.enter_context(self.nc.sbuf_tensor(name, shape, dt))

    def ps(self, stack, name, shape):
        return stack.enter_context(self.nc.psum_tensor(name, shape, F32))

    def stats(self, stack, name):
        return {"go": self.sem(name + "_lngo"), "raw": self.sb(stack, name + "_raw", [P, 2 * GROUP, 6]),
                "mv": self.sb(stack, name + "_mv", [P, 2 * GROUP, 2]),
                "std": self.sb(stack, name + "_std", [P, 2 * GROUP]),
                "rstd": self.sb(stack, name + "_rstd", [P, 2 * GROUP]),
                "shift": self.sb(stack, name + "_shift", [P, 2 * GROUP])}


def split_on_act(act, raw, hi, loaded, count, hi_done):
    act.wait_ge(loaded, count)
    act.copy(hi, raw).then_inc(hi_done, 1)


def split_on_dve(dve, raw, hi, lo, hi_done, count, lo_done):
    dve.wait_ge(hi_done, count)
    dve.tensor_tensor(lo, raw, hi.bitcast(F32), ALU.subtract).then_inc(lo_done, 1)


def three(pe, out, a, b, first, last):
    (ah, al), (bh, bl) = a, b
    pe.matmul(out, ah, bh, start=first, stop=False)
    pe.matmul(out, ah, bl, start=False, stop=False)
    return pe.matmul(out, al, bh, start=False, stop=last)


def prepare(nc, core, a, keep, l0):
    sem = core.sem
    idx_loaded, small_loaded, w1_loaded, rows_loaded, packed = (sem("a_" + n) for n in ("idx", "small", "w1", "rows", "packed"))
    w3_loaded = [sem(f"a_w3p{q}") for q in range(5)]
    w2_loaded = [sem("a_w2l0"), sem("a_w2l1")]
    iota_ready, zero_ready, ident_ready, dve_step = sem("a_iota"), sem("a_zero"), sem("a_ident"), sem("a_dve")
    onehot_ready, hist_read, hist_done = sem("a_onehot"), sem("a_hist_read"), sem("a_hist")
    count_ready, root_ready = sem("a_count"), sem("a_root")
    w3_hi, w3_lo, w2_hi, w2_lo, w1_hi, w1_lo, b2_hi, b2_lo = (
        sem("a_" + n) for n in ("w3hi", "w3lo", "w2hi", "w2lo", "w1hi", "w1lo", "b2hi", "b2lo"))
    fold_ready, fold_hi, fold_lo, c2_ready = sem("a_fold"), sem("a_fold_hi"), sem("a_fold_lo"), sem("a_c2")
    assert EG == KH
    QR = ROWS_E // 4

    with ExitStack() as st:
        sb = lambda n, s, d=F32: core.sb(st, "a_" + n, s, d)
        dst_i, nxt_i, src_i, typ_i = (sb(n, [P, ET], I32) for n in ("dst", "nxt", "src", "typ"))
        wgt = sb("wgt", [P, ET])
        emb = sb("emb", [P, HEADS * HEADS])
        hl = sb("hl", [P, 4, ET], I32)
        last = sb("last", [P, ET])
        val = sb("val", [P, ET])
        iota_i = sb("iotai", [P, P], I32)
        iota_f = sb("iotaf", [P, P])
        slot_i = sb("sloti", [P, ET], I32)
        pick = sb("pick", [P, ET])
        term = sb("term", [P, ET, HEADS])
        onehot = sb("onehot", [P, 4, GROUP, P])
        zeros = sb("zeros", [P, P])
        found = sb("found", [P, NT])
        root = sb("root", [P, NT])
        rows32 = sb("rows32", [P, QR], I32)
        raw = sb("raw", [P, KI * HID])
        W2m = sb("W2m", [P, 2, KH, P])
        W2h, W2l = sb("W2h", [P, 2, KH, P], F32R), sb("W2l", [P, 2, KH, P], F32R)
        b2c = sb("b2c", [P, KH])
        b2h, b2l = sb("b2h", [P, KH, P], F32R), sb("b2l", [P, KH, P], F32R)
        hist = core.ps(st, "a_hist_ps", [P, 2, 512])
        fold = core.ps(st, "a_fold_ps", [P, 4, 512])
        c2p = core.ps(st, "a_c2_ps", [P, 2, 512])
        by_block = lambda ap: ap.rearrange("p (k n) -> p k n", n=IN)
        W3raw = by_block(raw[:, :])
        W3h = by_block(l0["W1h"][:, :, :].rearrange("p k n -> p (k n)"))
        W3l = by_block(l0["W1l"][:, :, :].rearrange("p k n -> p (k n)"))
        W1raw = raw[:, :].rearrange("p (k n) -> p k n", n=HID)

        def blocks(engine, body):
            with engine.Fori(0, KH // 2 - 1) as it:
                for b in range(2):
                    body(it, b, True)
            body(KH // 2 - 1, 0, True)
            body(KH // 2 - 1, 1, False)

        with nc.Block() as block:
            @block.sync
            def _(sp):
                for q in range(5):
                    sp.dma_start(W3raw[:, 2 * q:2 * q + 2, :], a["L0_gnn_W3"][F + 2 * P * q:F + 2 * P * (q + 1), :]
                                 .rearrange("(k p) n -> p k n", p=P)).then_inc(w3_loaded[q], 16)
                for q in range(4):
                    if q:
                        sp.wait_ge(packed, q)
                    sp.dma_start(rows32[:, :], a["dst_row"][:, q * QR:(q + 1) * QR].broadcast_to([P, QR])).then_inc(rows_loaded, 16)
                for k in range(2, KH):
                    sp.wait_ge(w2_lo, k - 1)
                    sp.dma_start(W2m[:, k % 2, :, :], a["W2T"][:, k * P:(k + 1) * P].rearrange("(k p) m -> p k m", p=P)
                                 ).then_inc(w2_loaded[k % 2], 16)
                    if k == 3:
                        sp.wait_ge(w3_lo, 5)
                        sp.dma_start(W1raw, a["L0_gnn_W1"].rearrange("(k p) n -> p k n", p=P)).then_inc(w1_loaded, 16)

            @block.scalar
            def _(act):
                act.dma_start(dst_i[:, :], a["dst_win"]).then_inc(idx_loaded, 16)
                act.dma_start(nxt_i[:, :], a["dst_next"]).then_inc(idx_loaded, 16)
                act.dma_start(src_i[:, :], a["src_count"]).then_inc(idx_loaded, 16)
                act.dma_start(typ_i[:, :], a["type_win"]).then_inc(idx_loaded, 16)
                act.dma_start(keep["src"][:, :], a["src_win"]).then_inc(idx_loaded, 16)
                act.dma_start(keep["dst"][:, :], a["dst_wide"]).then_inc(idx_loaded, 16)
                act.dma_start(wgt[:, :], a["weight_win"]).then_inc(small_loaded, 16)
                act.dma_start(emb[:, :], a["L1_gnn_et_emb"].rearrange("(o k) h -> o (k h)", o=1).broadcast_to([P, HEADS * HEADS])
                              ).then_inc(small_loaded, 16)
                act.dma_start(b2c[:, :], a["L0_gnn_b2"].rearrange("(k p) -> p k", p=P),
                              allow_slow_non_contiguous=True).then_inc(small_loaded, 16)
                act.dma_start(l0["b1"][:, :], a["L0_gnn_b1"].rearrange("(k p) -> p k", p=P),
                              allow_slow_non_contiguous=True).then_inc(small_loaded, 16)
                for k in range(2):
                    act.dma_start(W2m[:, k, :, :], a["W2T"][:, k * P:(k + 1) * P].rearrange("(k p) m -> p k m", p=P)
                                  ).then_inc(w2_loaded[k], 16)
                act.wait_ge(small_loaded, 64)
                act.copy(b2h[:, :, :], over(b2c[:, :].unsqueeze(2), [P, KH, P])).then_inc(b2_hi, 1)
                def split(it, b):
                    act.wait_ge(w2_loaded[b], it * 16 + 16)
                    act.copy(W2h[:, b, :, :], W2m[:, b, :, :]).then_inc(w2_hi, 1)

                split(0, 0)
                for q in range(5):
                    act.wait_ge(w3_loaded[q], 16)
                    act.copy(W3h[:, 2 * q:2 * q + 2, :], W3raw[:, 2 * q:2 * q + 2, :]).then_inc(w3_hi, 1)

                def body(it, b, more):
                    if more:
                        act.wait_ge(fold_ready, it * 2 + b)
                        split(*((it, 1) if b == 0 else (it + 1, 0)))
                    act.wait_ge(fold_ready, it * 2 + (b + 1))
                    for h in range(2):
                        act.copy(l0["W23h"][:, it * 2 + b, h * HALF:(h + 1) * HALF],
                                 fold[:, 2 * b + h, 0:HALF]).then_inc(fold_hi, 1)

                blocks(act, body)
                act.wait_ge(count_ready, 1)
                act.activation(root[:, :], found[:, :], ACT.Sqrt).then_inc(root_ready, 1)
                act.wait_ge(w1_loaded, 16)
                act.wait_ge(c2_ready, 1)
                for k in range(KI):
                    act.copy(l0["W1h"][:, k, :], W1raw[:, k, :]).then_inc(w1_hi, 1)

            @block.gpsimd
            def _(pool):
                pool.iota(iota_i[:, :], [[1, P]], base=0, channel_multiplier=0).then_inc(iota_ready, 1)
                pool.iota(slot_i[:, :], [[P, ET]], base=1, channel_multiplier=1).then_inc(iota_ready, 1)
                pool.memset(zeros[:, :], 0.0).then_inc(zero_ready, 1)
                pool.memset(keep["ident"][:, :], 1.0).then_inc(ident_ready, 1)
                pool.wait_ge(ident_ready, 1)
                pool.affine_select(out=keep["ident"][:, :], in_=keep["ident"][:, :], compare_op=ALU.is_equal, fill=0.0,
                                   base=0, pattern=[[-1, P]], channel_multiplier=1).then_inc(ident_ready, 1)
                pool.memset(keep["rows"][:, ROWS_E:], 0).then_inc(zero_ready, 1)

            @block.vector
            def _(dve):
                n = 0

                def step(ins):
                    nonlocal n
                    n += 1
                    ins.then_inc(dve_step, 1)
                    dve.wait_ge(dve_step, n)

                def spread(q):
                    dve.wait_ge(rows_loaded, 16 * (q + 1))
                    dve.tensor_copy(keep["rows"][:, q * QR:(q + 1) * QR], rows32[:, :]).then_inc(packed, 1)

                step(dve.memset(keep["eps"][:, :], EPS))
                dve.wait_ge(iota_ready, 2)
                dve.wait_ge(idx_loaded, 16 * 6)
                step(dve.tensor_copy(iota_f[:, :], iota_i[:, :]))
                for k, ids in enumerate((src_i, dst_i)):
                    step(dve.tensor_scalar(hl[:, 2 * k, :], ids[:, :], 127, None, ALU.bitwise_and))
                    step(dve.tensor_scalar(hl[:, 2 * k + 1, :], ids[:, :], 7, None, ALU.logical_shift_right))
                step(dve.tensor_tensor(last[:, :], dst_i[:, :], nxt_i[:, :], ALU.not_equal))
                step(dve.tensor_tensor(val[:, :], last[:, :], slot_i[:, :], ALU.mult))
                spread(0)
                dve.wait_ge(b2_hi, 1)
                dve.tensor_tensor(b2l[:, :, :], over(b2c[:, :].unsqueeze(2), [P, KH, P]), b2h[:, :, :].bitcast(F32),
                                  ALU.subtract).then_inc(b2_lo, 1)
                spread(1)
                def split(it, b):
                    dve.wait_ge(w2_hi, it * 2 + (b + 1))
                    dve.tensor_tensor(W2l[:, b, :, :], W2m[:, b, :, :], W2h[:, b, :, :].bitcast(F32), ALU.subtract).then_inc(w2_lo, 1)

                split(0, 0)
                for q in range(5):
                    dve.wait_ge(w3_hi, q + 1)
                    dve.tensor_tensor(W3l[:, 2 * q:2 * q + 2, :], W3raw[:, 2 * q:2 * q + 2, :],
                                      W3h[:, 2 * q:2 * q + 2, :].bitcast(F32), ALU.subtract).then_inc(w3_lo, 1)
                    if q in (1, 3):
                        spread(q // 2 + 2)

                def body(it, b, more):
                    g = it * 2 + b
                    if more:
                        split(*((it, 1) if b == 0 else (it + 1, 0)))
                    dve.wait_ge(hist_read, g)
                    for q, (part, width) in enumerate(((0, P), (1, NT), (2, P), (3, NT))):
                        cols = over(hl[:, part, bass.ds(g * GROUP, GROUP)].unsqueeze(2), [P, GROUP, width])
                        dve.tensor_tensor(onehot[:, q, :, 0:width], over(iota_f[:, 0:width].unsqueeze(1), [P, GROUP, width]),
                                          cols, ALU.is_equal).then_inc(onehot_ready, 1)
                    dve.wait_ge(onehot_ready, g * 5 + 4)
                    dve.tensor_tensor(onehot[:, 3, :, 0:NT], onehot[:, 3, :, 0:NT],
                                      over(val[:, bass.ds(g * GROUP, GROUP)].unsqueeze(2), [P, GROUP, NT]),
                                      ALU.mult).then_inc(onehot_ready, 1)
                    for h in range(2):
                        dve.wait_ge(fold_hi, it * 4 + (2 * b + h + 1))
                        dve.tensor_tensor(l0["W23l"][:, it * 2 + b, h * HALF:(h + 1) * HALF], fold[:, 2 * b + h, 0:HALF],
                                          l0["W23h"][:, it * 2 + b, h * HALF:(h + 1) * HALF].bitcast(F32),
                                          ALU.subtract).then_inc(fold_lo, 1)

                fac = keep["fac"][:, :, :]

                def factors(types):
                    if 0 in types:
                        step(dve.memset(fac, 1.0))
                    for k in types:
                        step(dve.tensor_scalar(pick[:, :], typ_i[:, :], float(k), None, ALU.is_equal))
                        step(dve.tensor_tensor(term[:, :, :], over(pick[:, :].unsqueeze(2), [P, ET, HEADS]),
                                               over(emb[:, k * HEADS:(k + 1) * HEADS].unsqueeze(1), [P, ET, HEADS]), ALU.mult))
                        step(dve.tensor_tensor(fac, fac, term[:, :, :], ALU.add))
                    if HEADS - 1 in types:
                        step(dve.tensor_tensor(fac, fac, over(wgt[:, :].unsqueeze(2), [P, ET, HEADS]), ALU.mult))

                with dve.Fori(0, KH // 2 - 1) as it:
                    for b in range(2):
                        body(it, b, True)
                factors(range(HEADS // 2))
                body(KH // 2 - 1, 0, True)
                factors(range(HEADS // 2, HEADS))
                body(KH // 2 - 1, 1, False)
                step(dve.tensor_copy(keep["wgt"][:, :], wgt[:, :]))
                dve.wait_ge(hist_done, 1)
                dve.tensor_scalar(found[:, :], hist[:, 0, 0:NT], 1.0, None, ALU.add).then_inc(count_ready, 1)
                dve.wait_ge(root_ready, 1)
                step(dve.reciprocal(keep["dis"][:, 0:NT], root[:, :]))
                step(dve.tensor_scalar(keep["has"][:, 0:NT], hist[:, 1, 0:NT], 0.0, None, ALU.is_gt))
                step(dve.tensor_scalar(found[:, :], keep["has"][:, 0:NT], -FAR, FAR - 1.0, ALU.mult, ALU.add))
                step(dve.memset(keep["slot"][:, :], 1 << 20))
                step(dve.memset(keep["dis"][:, NT:NT + 8], 0.0))
                step(dve.memset(keep["has"][:, NT:NT + 8], 0.0))
                step(dve.tensor_tensor(keep["dis2"][:, :], keep["dis"][:, :], keep["dis"][:, :], ALU.mult))
                step(dve.tensor_tensor(keep["dish"][:, :], keep["dis"][:, :], keep["has"][:, :], ALU.mult))
                step(dve.tensor_tensor(keep["slot"][:, 0:NT], hist[:, 1, 0:NT], found[:, :], ALU.add))
                for k in range(KI):
                    dve.wait_ge(w1_hi, k + 1)
                    dve.tensor_tensor(l0["W1l"][:, k, :], W1raw[:, k, :], l0["W1h"][:, k, :].bitcast(F32),
                                      ALU.subtract).then_inc(w1_lo, 1)
                dve.wait_ge(c2_ready, 1)
                for h in range(2):
                    step(dve.tensor_copy(l0["c2"][:, h * HALF:(h + 1) * HALF], c2p[:, h, 0:HALF]))

            @block.tensor
            def _(pe):
                def body(it, b, more):
                    g = it * 2 + b
                    pe.wait_ge(w2_lo, g + 1)
                    pe.wait_ge(fold_lo, it * 4 + (2 * b + 2))
                    for h in range(2):
                        w = slice(h * HALF, (h + 1) * HALF)
                        for k in range(KH):
                            if h == 0 and k % 2 == 0:
                                pe.wait_ge(w3_lo, k // 2 + 1)
                            mm = three(pe, fold[:, 2 * b + h, 0:HALF], (W2h[:, b, k, :], W2l[:, b, k, :]),
                                       (W3h[:, k, w], W3l[:, k, w]), k == 0, k == KH - 1)
                    mm.then_inc(fold_ready, 1)
                    pe.wait_ge(onehot_ready, g * 5 + 5)
                    for j in range(GROUP):
                        for q in range(2):
                            mm = pe.matmul(hist[:, q, 0:NT], onehot[:, 2 * q, j, :], onehot[:, 2 * q + 1, j, 0:NT],
                                           start=False, stop=False)
                    mm.then_inc(hist_read, 1)

                pe.sem_inc(fold_lo, 4)
                pe.wait_ge(zero_ready, 1)
                for q in range(2):
                    pe.matmul(hist[:, q, 0:NT], zeros[:, :], zeros[:, 0:NT], start=True, stop=False)
                blocks(pe, body)
                for q in range(2):
                    mm = pe.matmul(hist[:, q, 0:NT], zeros[:, :], zeros[:, 0:NT], start=False, stop=True)
                mm.then_inc(hist_done, 1)
                pe.wait_ge(b2_lo, 1)
                for h in range(2):
                    w = slice(h * HALF, (h + 1) * HALF)
                    for k in range(KH):
                        mm = three(pe, c2p[:, h, 0:HALF], (b2h[:, k, :], b2l[:, k, :]), (W3h[:, k, w], W3l[:, k, w]),
                                   k == 0, k == KH - 1)
                mm.then_inc(c2_ready, 1)


def turn_plan(r, t):
    if t < GROUP:
        return r, 1, ((0, 1), (2, 3), (4,), ())[t], ()
    return r + 1, 0, ((0,), (1,), (2,), ())[t - GROUP], (3, 4) if t == 2 * GROUP - 1 else ()


def layer0_edges(nc, core, a, keep, l0, T0):
    sem = core.sem
    idx_staged, go = sem("b_idx"), sem("b_go")
    x_loaded = [sem("b_x0"), sem("b_x1")]
    attr_loaded = [sem("b_attr0"), sem("b_attr1")]
    dve_init = sem("b_init")
    ln_step, var_ready, std_ready, norm_ready, h_ready = (sem("b_" + n) for n in ("lnstep", "var", "std", "norm", "h"))
    tp_ready, tp_free, hT_hi = sem("b_tp"), sem("b_tpfree"), sem("b_hThi")
    hid_ready, relu_ready, hid_hi, hid_lo = sem("b_hid"), sem("b_relu"), sem("b_hidhi"), sem("b_hidlo")
    y_ready = [sem("b_y0"), sem("b_y1")]
    y_out = [sem("b_yo0"), sem("b_yo1")]
    y_hi, row_hi = sem("b_yhi"), sem("b_rowhi")
    row_ready, carry_ready, match_ready = sem("b_row"), sem("b_carry"), sem("b_match")
    sum_ready, cnt_inv, sum_scaled = sem("b_sum"), sem("b_cnt"), sem("b_scaled")
    sum_stored = sem("b_stored")

    with ExitStack() as st:
        sb = lambda n, s, d=F32: core.sb(st, "b_" + n, s, d)
        X = sb("X", [P, 2, GROUP, F])
        attr = sb("attr", [P, 2, GROUP, FE])
        idx = sb("idx", [P, 2 * GROUP], I32)
        stt = core.stats(st, "b")
        hTh, hTl = sb("hTh", [P, KI, GROUP * P], F32R), sb("hTl", [P, KI, GROUP * P], F32R)
        R = sb("R", [P, GROUP * P])
        Rh, Rl = sb("Rh", [P, KH, GROUP * P], F32R), sb("Rl", [P, KH, GROUP * P], F32R)
        Yh, Yl = sb("Yh", [P, 2, IN + 2], F32R), sb("Yl", [P, 2, IN + 2], F32R)
        carry = sb("carry", [1, IN + 2])
        match = sb("match", [P, GROUP, P], F32R)
        inv = sb("inv", [P, 1])
        ones = sb("ones", [P, 2])
        T = sb("T", [P, IN])
        tp = core.ps(st, "b_tp_ps", [P, 2, 512])
        hid = core.ps(st, "b_hid_ps", [P, 2, 512])
        y = core.ps(st, "b_y_ps", [P, 2, 512])
        s = core.ps(st, "b_s_ps", [P, 2, 512])
        rows16 = keep["rows"]
        SW = (HALF, HALF + 2)

        with nc.Block() as block:
            @block.gpsimd
            def _(pool):
                with pool.Fori(0, ER + 1) as r:
                    pool.tensor_copy(idx[:, :], keep["src"][:, bass.ds(r * (2 * GROUP), 2 * GROUP)]).then_inc(idx_staged, 1)
                    pool.wait_ge(idx_staged, r + 1)
                    pool.wait_ge(tp_ready, r * (2 * KI))
                    pool.sem_inc(go, 1)
                    for i in range(2 * GROUP):
                        pool.indirect_dma_start(X[:, i // GROUP, i % GROUP, :], None, a["x"][:, :],
                                                bass.IndirectOffsetOnAxis(idx[:, i:i + 1], 0),
                                                bounds_check=NODES - 1, oob_is_err=False).then_inc(x_loaded[i // GROUP], 16)
                    pool.wait_ge(x_loaded[0], r * 64 + 64)
                    pool.wait_ge(x_loaded[1], r * 64 + 64)
                    pool.sem_inc(go, 1)

            @block.sync
            def _(sp):
                for b in range(2):
                    sp.dma_start(attr[:, b, :, :], a["attr_win"][:, b, :, :]).then_inc(attr_loaded[b], 16)
                with sp.Fori(0, ER) as r:
                    for t in range(2 * GROUP):
                        sp.wait_ge(sum_scaled, (r * (2 * GROUP) + t) * 2 + 2)
                        sp.dma_start(T0[bass.ds((r * (2 * GROUP) + t) * P, P), :], T[:, :]).then_inc(sum_stored, 16)
                        if t in (4, 5):
                            b = t - 4
                            sp.wait_ge(tp_ready, r * (2 * KI) + 2 * KI)
                            sp.dma_start(attr[:, b, :, :], a["attr_win"][:, r * 2 + (2 + b), :, :]).then_inc(attr_loaded[b], 16)
                sp.wait_ge(sum_stored, 16 * ET)
                for b in range(2):
                    sp.wait_ge(attr_loaded[b], 16 * (ER + 1))

            @block.scalar
            def _(act):
                def root(r):
                    act.wait_ge(var_ready, r * 8 + 8)
                    layer_norm_std(act, stt, keep["eps"]).then_inc(std_ready, 1)
                    act.wait_ge(norm_ready, r + 1)

                def norm_rows(first):
                    for i in (first, first + 1):
                        xi = X[:, i // GROUP, i % GROUP, :]
                        relu_norm(act, xi, xi, stt, i).then_inc(h_ready, 1)

                def norm(r):
                    root(r)
                    for i in range(0, 8, 2):
                        norm_rows(i)

                def transposed(r, b, chunks):
                    for c in chunks:
                        if c == 0:
                            act.wait_ge(hid_ready, r * 20 + 10 * b)
                        act.wait_ge(tp_ready, r * 10 + (5 * b + c + 1))
                        act.copy(hTh[:, c, :], tp[:, (5 * b + c) % 2, :]).then_inc(hT_hi, 1)

                def hidden(r, b, m):
                    k = 10 * b + m
                    if m == 0:
                        act.wait_ge(y_ready[1], r * 8 + 4 * b)
                    act.wait_ge(hid_ready, r * 20 + (k + 1))
                    act.wait_ge(hid_lo, r * 20 + k)
                    act.activation(R[:, :], hid[:, m % 2, :], ACT.Relu, bias=l0["b1"][:, m:m + 1]).then_inc(relu_ready, 1)
                    act.activation(Rh[:, m, :], hid[:, m % 2, :], ACT.Relu, bias=l0["b1"][:, m:m + 1]).then_inc(hid_hi, 1)

                def carry_out(r, t):
                    act.wait_ge(sum_ready, r * 8 + (t + 1))
                    act.wait_ge(row_ready, r * 8 + (t + 1))
                    act.copy(carry[0:1, 0:HALF], s[0:1, 0, 0:HALF]).then_inc(carry_ready, 1)
                    act.copy(carry[0:1, HALF:IN + 2], s[0:1, 1, 0:HALF + 2]).then_inc(carry_ready, 1)

                def edge_rows(r, t):
                    nr, nb, during, last = turn_plan(r, t)
                    for h in range(2):
                        act.wait_ge(y_ready[h], r * 8 + (t + 1))
                        act.copy(Yh[:, t % 2, h * HALF:(h + 1) * HALF], y[:, h, 0:HALF]).then_inc(y_hi, 1)
                        if h == 0:
                            transposed(nr, nb, during[:1])
                    if t % 4:
                        carry_out(r, t - 1)
                    for h in range(2):
                        act.wait_ge(y_out[h], r * 8 + (t + 1))
                    act.wait_ge(carry_ready, r * 16 + 2 * t)
                    act.copy(Yh[0:1, t % 2, :], carry[0:1, :]).then_inc(row_hi, 1)
                    transposed(nr, nb, during[1:])
                    transposed(nr, nb, last)

                act.wait_ge(dve_init, 4)
                norm(0)
                transposed(0, 0, range(KI))
                with act.Fori(0, ER) as r:
                    for m in range(KH):
                        hidden(r, 0, m)
                    for t in range(4):
                        edge_rows(r, t)
                    for m in range(KH):
                        hidden(r, 1, m)
                        if m == 2:
                            carry_out(r, 3)
                        if m == 5:
                            root(r + 1)
                        if m >= 6:
                            norm_rows(2 * (m - 6))
                    for t in range(4, 8):
                        edge_rows(r, t)
                    carry_out(r, 7)

            @block.vector
            def _(dve):
                dve.memset(ones[:, :], 1.0).then_inc(dve_init, 1)
                dve.wait_ge(dve_init, 1)
                dve.tensor_copy(Yh[:, :, IN:IN + 2], over(ones[:, :].unsqueeze(1), [P, 2, 2])).then_inc(dve_init, 1)
                dve.tensor_scalar(Yl[:, :, IN:IN + 2], over(ones[:, :].unsqueeze(1), [P, 2, 2]), 0.0, None, ALU.mult).then_inc(dve_init, 1)
                dve.memset(carry[:, :], 0.0).then_inc(dve_init, 1)

                def norm(r):
                    dve.wait_ge(x_loaded[0], r * 64 + 64)
                    dve.wait_ge(x_loaded[1], r * 64 + 64)
                    layer_norm_stats(dve, tiles(X), stt, ln_step, r * 9, var_ready)
                    dve.wait_ge(std_ready, r + 1)
                    layer_norm_scale(dve, stt, ln_step, r * 9 + 9, norm_ready)

                def transposed(r, b, chunks):
                    for c in chunks:
                        dve.wait_ge(hT_hi, r * 10 + (5 * b + c + 1))
                        dve.tensor_tensor(hTl[:, c, :], tp[:, (5 * b + c) % 2, :], hTh[:, c, :].bitcast(F32),
                                          ALU.subtract).then_inc(tp_free, 1)

                def hidden(r, b, m):
                    dve.wait_ge(hid_hi, r * 20 + (10 * b + m + 1))
                    dve.tensor_tensor(Rl[:, m, :], R[:, :], Rh[:, m, :].bitcast(F32), ALU.subtract).then_inc(hid_lo, 1)

                def build_match(r, b):
                    dve.wait_ge(sum_ready, r * 8 + 4 * b)
                    g = r * 8 + 4 * b
                    dve.tensor_tensor(match[:, :, :], rows16[:, bass.ds(g * P, GROUP * P)].rearrange("p (j q) -> p j q", q=P),
                                      over(keep["dst"][:, bass.ds(g, GROUP)].unsqueeze(2), [P, GROUP, P]),
                                      ALU.is_equal).then_inc(match_ready, 1)

                def sums(r, t):
                    dve.wait_ge(carry_ready, r * 16 + (2 * t + 2))
                    dve.reciprocal(inv[:, :], s[:, 1, HALF:HALF + 1]).then_inc(cnt_inv, 1)
                    dve.wait_ge(cnt_inv, r * 8 + (t + 1))
                    dve.wait_ge(sum_stored, r * 128 + 16 * t)
                    for h in range(2):
                        dve.scalar_tensor_tensor(out=T[:, h * HALF:(h + 1) * HALF], in0=s[:, h, 0:HALF], scalar=inv[:, 0:1],
                                                 in1=l0["c2"][:, h * HALF:(h + 1) * HALF], op0=ALU.mult, op1=ALU.add
                                                 ).then_inc(sum_scaled, 1)

                def edge_rows(r, t):
                    nr, nb, during, last = turn_plan(r, t)
                    for h in range(2):
                        w = slice(h * HALF, (h + 1) * HALF)
                        dve.wait_ge(y_hi, r * 16 + (2 * t + h + 1))
                        dve.tensor_tensor(Yl[:, t % 2, w], y[:, h, 0:HALF], Yh[:, t % 2, w].bitcast(F32),
                                          ALU.subtract).then_inc(y_out[h], 1)
                        if h == 0:
                            transposed(nr, nb, during[:1])
                    dve.wait_ge(row_hi, r * 8 + (t + 1))
                    dve.tensor_tensor(Yl[0:1, t % 2, :], carry[0:1, :], Yh[0:1, t % 2, :].bitcast(F32),
                                      ALU.subtract).then_inc(row_ready, 1)
                    if t % 4:
                        sums(r, t - 1)
                    transposed(nr, nb, during[1:])
                    transposed(nr, nb, last)

                norm(0)
                transposed(0, 0, range(KI))
                with dve.Fori(0, ER) as r:
                    build_match(r, 0)
                    for m in range(KH):
                        hidden(r, 0, m)
                    for t in range(4):
                        edge_rows(r, t)
                    for m in range(KH):
                        hidden(r, 1, m)
                        if m == 2:
                            sums(r, 3)
                            build_match(r, 1)
                        if m == 4:
                            norm(r + 1)
                    for t in range(4, 8):
                        edge_rows(r, t)
                    sums(r, 7)

            @block.tensor
            def _(pe):
                def transpose(r, b, chunks):
                    for c in chunks:
                        k = 5 * b + c
                        if c == 0:
                            pe.wait_ge(h_ready, r * 8 + (4 * b + 4))
                        if c == KF:
                            pe.wait_ge(attr_loaded[b], r * 16 + 16)
                        pe.wait_ge(tp_free, r * 10 + (k + 1))
                        for j in range(GROUP):
                            rows = X[:, b, j, c * P:(c + 1) * P] if c < KF else attr[:, b, j, :]
                            mm = pe.transpose(tp[:, k % 2, j * P:(j + 1) * P], rows, keep["ident"][:, :])
                        mm.then_inc(tp_ready, 1)

                def first(r, b, m):
                    k = 10 * b + m
                    pe.wait_ge(hid_hi, r * 20 + max(k - 1, 0))
                    for c in range(KI):
                        if m == 0:
                            pe.wait_ge(tp_free, r * 10 + (5 * b + c + 1 + 2))
                        mm = three(pe, hid[:, m % 2, :],
                                   (l0["W1h"][:, c, m * P:(m + 1) * P], l0["W1l"][:, c, m * P:(m + 1) * P]),
                                   (hTh[:, c, :], hTl[:, c, :]), c == 0, c == KI - 1)
                    mm.then_inc(hid_ready, 1)

                def second(r, b, j):
                    t = 4 * b + j
                    nr, nb, during, last = turn_plan(r, t)
                    for h in range(2):
                        pe.wait_ge(y_out[h], r * 8 + t)
                        for k in range(KH):
                            if j == 0 and h == 0:
                                pe.wait_ge(hid_lo, r * 20 + (10 * b + k + 1))
                            w = slice(h * HALF, (h + 1) * HALF)
                            mm = three(pe, y[:, h, 0:HALF], (Rh[:, k, j * P:(j + 1) * P], Rl[:, k, j * P:(j + 1) * P]),
                                       (l0["W23h"][:, k, w], l0["W23l"][:, k, w]), k == 0, k == KH - 1)
                        mm.then_inc(y_ready[h], 1)
                        transpose(nr, nb, during[h:h + 1])
                    if j:
                        sum_runs(r, t - 1)
                    transpose(nr, nb, last)

                def sum_runs(r, t):
                    pe.wait_ge(row_ready, r * 8 + (t + 1))
                    pe.wait_ge(match_ready, r * 2 + (t // 4 + 1))
                    pe.wait_ge(sum_scaled, r * 16 + 2 * t)
                    pe.wait_ge(carry_ready, r * 16 + 2 * t)
                    for h in range(2):
                        w = slice(h * HALF, h * HALF + SW[h])
                        pe.matmul(s[:, h, 0:SW[h]], match[:, t % 4, :], Yh[:, t % 2, w], start=True, stop=False)
                        mm = pe.matmul(s[:, h, 0:SW[h]], match[:, t % 4, :], Yl[:, t % 2, w], start=False, stop=True)
                    mm.then_inc(sum_ready, 1)

                pe.sem_inc(tp_free, 2)
                transpose(0, 0, range(KI))
                with pe.Fori(0, ER) as r:
                    for m in range(KH):
                        first(r, 0, m)
                    for j in range(GROUP):
                        second(r, 0, j)
                    for m in range(KH):
                        first(r, 1, m)
                        if m == 1:
                            sum_runs(r, 3)
                    for j in range(GROUP):
                        second(r, 1, j)
                    sum_runs(r, 7)


Z_SLOT = ((0, 1), (2, 3), (4,), ())


def layer0_nodes(nc, core, a, keep, T0, x1):
    sem = core.sem
    w3_loaded, w_loaded, w_hi, w_lo, init = sem("c_w3"), sem("c_w"), sem("c_whi"), sem("c_wlo"), sem("c_init")
    x_loaded = [sem("c_x0"), sem("c_x1")]
    res_loaded = [sem("c_r0"), sem("c_r1")]
    run_loaded = [sem("c_g0"), sem("c_g1")]
    idx_staged, go, res_ready = sem("c_idx"), sem("c_go"), sem("c_res")
    ln_step, var_ready, std_ready, norm_ready, h_ready = (sem("c_" + n) for n in ("lnstep", "var", "std", "norm", "h"))
    tp_ready, tp_free, hT_hi = sem("c_tp"), sem("c_tpfree"), sem("c_hThi")
    u_ready, u_out, z_hi = sem("c_u"), sem("c_uout"), sem("c_zhi")
    o_ready, o_out = sem("c_o"), sem("c_oout")
    stored = [sem("c_st0"), sem("c_st1")]
    TPR = 2 * (KF + KI)
    GT = 2 * GROUP

    with ExitStack() as st:
        sb = lambda n, s, d=F32: core.sb(st, "c_" + n, s, d)
        X = sb("X", [P, 2, GROUP, F])
        XB = sb("XB", [P, 2, GROUP, F])
        G = sb("G", [P, 2, GROUP, IN])
        idx = sb("idx", [P, GT], I32)
        stt = core.stats(st, "c")
        hTh, hTl = sb("hTh", [P, 2, KF, GROUP * P], F32R), sb("hTl", [P, 2, KF, GROUP * P], F32R)
        U = sb("U", [P, 2, GROUP, IN])
        R = sb("R", [P, 2, GROUP * P])
        zh, zl = sb("zh", [P, 2, KI, GROUP * P], F32R), sb("zl", [P, 2, KI, GROUP * P], F32R)
        W3h, W3l = sb("W3h", [P, KF, IN], F32R), sb("W3l", [P, KF, IN], F32R)
        W4h, W4l = sb("W4h", [P, KI, F], F32R), sb("W4l", [P, KI, F], F32R)
        b3, b4 = sb("b3", [P, KI]), sb("b4", [P, F])
        tp = core.ps(st, "c_tp_ps", [P, 2, 512])
        u = core.ps(st, "c_u_ps", [P, 4, 512])
        o = core.ps(st, "c_o_ps", [P, 2, 512])
        W3raw = U[:, 0, :, :]
        W4raw = U[:, 1, :, :].rearrange("p j n -> p (j n)").rearrange("p (k n) -> p k n", k=KI)

        with nc.Block() as block:
            @block.sync
            def _(sp):
                def load(g, b):
                    sp.dma_start(X[:, b, :, :], group_rows(a["x"], g, F)).then_inc(x_loaded[b], 16)

                def load_last(buf, b, sems):
                    at = (NG - 1) * GROUP * P
                    left = NODES - at
                    for j in range((left + P - 1) // P):
                        n = min(P, left - j * P)
                        sp.dma_start(buf[0:n, b, j, :], a["x"][at + j * P:at + j * P + n, :]).then_inc(sems[b], 16)

                def residual(g, b):
                    sp.dma_start(XB[:, b, :, :], group_rows(a["x"], g, F)).then_inc(res_loaded[b], 16)

                def store(r, g, b):
                    sp.wait_ge(o_out, r * GT + (4 * b + 4 + 2))
                    sp.dma_start(group_rows(x1, g, F), XB[:, b, :, :]).then_inc(stored[b], 16)

                for b in range(2):
                    load(b, b)
                sp.dma_start(W3raw, a["L0_gnn_W3"][0:F, :].rearrange("(k p) n -> p k n", p=P)).then_inc(w3_loaded, 16)
                sp.dma_start(W4raw, a["L0_gnn_W4"].rearrange("(k p) n -> p k n", p=P)).then_inc(w_loaded, 16)
                sp.dma_start(b3[:, :], a["L0_gnn_b3"].rearrange("(k p) -> p k", p=P),
                             allow_slow_non_contiguous=True).then_inc(w_loaded, 16)
                sp.dma_start(b4[:, :], a["L0_gnn_b4"].rearrange("(o n) -> o n", o=1).broadcast_to([P, F])).then_inc(w_loaded, 16)
                sp.wait_ge(init, 2)
                with sp.Fori(0, NR - 2) as r:
                    sp.wait_ge(tp_ready, r * TPR + 2 * KF)
                    for b in range(2):
                        load(r * 2 + (2 + b), b)
                    for b in range(2):
                        sp.wait_ge(stored[b], r * 16)
                        residual(r * 2 + b, b)
                    for b in range(2):
                        store(r, r * 2 + b, b)
                for r in (NR - 2, NR - 1):
                    sp.wait_ge(tp_ready, r * TPR + 2 * KF)
                    for b in range(2):
                        if r == NR - 1:
                            load(b, b)
                        elif b:
                            load_last(X, b, x_loaded)
                        else:
                            load(2 * r + 2, b)
                    for b in range(2):
                        sp.wait_ge(stored[b], 16 * r)
                        if r == NR - 1 and b:
                            load_last(XB, b, res_loaded)
                        else:
                            residual(2 * r + b, b)
                    for b in range(2):
                        store(r, 2 * r + b, b)
                for b in range(2):
                    sp.wait_ge(stored[b], 16 * NR)
                    sp.wait_ge(x_loaded[b], 16 * (NR + 1) + 32 * b)

            @block.gpsimd
            def _(pool):
                pool.memset(G[:, :, :, :], 0.0).then_inc(init, 1)
                pool.memset(XB[:, 1, :, :], 0.0).then_inc(init, 1)
                pool.wait_ge(w_loaded, 48)
                pool.wait_ge(init, 2)

                def round_(r, late):
                    pool.tensor_copy(idx[:, :], keep["slot"][:, bass.ds(r * GT, GT)]).then_inc(idx_staged, 1)
                    pool.wait_ge(idx_staged, r + 1)
                    pool.wait_ge(u_out, r * (2 * GT) + 4)
                    pool.sem_inc(go, 1)
                    for i in range(GT):
                        pool.indirect_dma_start(G[:, i // GROUP, i % GROUP, :], None, T0[:, :],
                                                bass.IndirectOffsetOnAxis(idx[:, i:i + 1], 0),
                                                bounds_check=ROWS_E - 1, oob_is_err=False).then_inc(run_loaded[i // GROUP], 16)
                    for b in range(2):
                        pool.wait_ge(res_loaded[b], r * 16 + (16 + late * b))
                        pool.tensor_tensor(XB[:, b, :, :], XB[:, b, :, :], over(b4[:, :].unsqueeze(1), [P, GROUP, F]),
                                           ALU.add).then_inc(res_ready, 1)
                    for b in range(2):
                        pool.wait_ge(run_loaded[b], r * 64 + 64)
                    pool.sem_inc(go, 1)

                with pool.Fori(0, NR - 1) as r:
                    round_(r, 0)
                round_(NR - 1, 32)

            @block.scalar
            def _(act):
                def root(r):
                    act.wait_ge(var_ready, r * GT + GT)
                    layer_norm_std(act, stt, keep["eps"]).then_inc(std_ready, 1)
                    act.wait_ge(norm_ready, r + 1)

                def norm_rows(first):
                    for i in (first, first + 1):
                        x = X[:, i // GROUP, i % GROUP, :]
                        relu_norm(act, x, x, stt, i).then_inc(h_ready, 1)

                def turned_rows(r, chunks):
                    for k in chunks:
                        act.wait_ge(tp_ready, r * TPR + (k + 1))
                        act.copy(hTh[:, k // KF, k % KF, :], tp[:, k % 2, :]).then_inc(hT_hi, 1)

                def hidden(r, b, chunks):
                    for c in chunks:
                        k = 2 * KF + KI * b + c
                        act.wait_ge(o_ready, r * GT)
                        act.wait_ge(tp_ready, r * TPR + (k + 1))
                        act.activation(R[:, k % 2, :], tp[:, k % 2, :], ACT.Relu, bias=b3[:, c:c + 1]).then_inc(z_hi, 1)
                        act.activation(zh[:, b, c, :], tp[:, k % 2, :], ACT.Relu, bias=b3[:, c:c + 1]).then_inc(z_hi, 1)

                root(0)
                for i in range(GROUP):
                    norm_rows(2 * i)
                split_on_act(act, W3raw, W3h[:, :, :], w3_loaded, 16, w_hi)
                turned_rows(0, range(2 * KF))
                split_on_act(act, W4raw, W4h[:, :, :], w_loaded, 48, w_hi)
                with act.Fori(0, NR) as r:
                    for j in range(GROUP):
                        hidden(r, 0, Z_SLOT[j])
                    for j in range(GROUP):
                        hidden(r, 1, Z_SLOT[j])
                        if j == 0:
                            root(r + 1)
                        norm_rows(2 * j)
                    for j in range(GROUP):
                        turned_rows(r + 1, (2 * j, 2 * j + 1))

            @block.vector
            def _(dve):
                def stats(r, late, first):
                    if first % GROUP == 0:
                        b = first // GROUP
                        dve.wait_ge(x_loaded[b], r * 16 + (16 + late * b))
                    for i in (first, first + 1):
                        dve.bn_stats(stt["raw"][:, i, :], X[:, i // GROUP, i % GROUP, :]).then_inc(ln_step, 1)

                def scale(r):
                    dve.wait_ge(ln_step, r * 9 + GT)
                    dve.sem_inc(stt["go"], 1)
                    for i in range(GT):
                        dve.bn_aggr(stt["mv"][:, i, :], stt["raw"][:, i, :]).then_inc(var_ready, 1)
                    dve.wait_ge(std_ready, r + 1)
                    layer_norm_scale(dve, stt, ln_step, r * 9 + 9, norm_ready)

                def turned_rows(r, chunks):
                    for k in chunks:
                        dve.wait_ge(hT_hi, r * (2 * KF) + (k + 1))
                        dve.tensor_tensor(hTl[:, k // KF, k % KF, :], tp[:, k % 2, :], hTh[:, k // KF, k % KF, :].bitcast(F32),
                                          ALU.subtract).then_inc(tp_free, 1)

                def hidden(r, b, chunks):
                    for c in chunks:
                        k = KI * b + c
                        dve.wait_ge(z_hi, r * (4 * KI) + (2 * k + 2))
                        dve.tensor_tensor(zl[:, b, c, :], R[:, k % 2, :], zh[:, b, c, :].bitcast(F32),
                                          ALU.subtract).then_inc(tp_free, 1)

                def add_run(r, b, j):
                    t = GROUP * b + j
                    if j == 0:
                        dve.wait_ge(run_loaded[b], r * 64 + 64)
                    dve.wait_ge(u_ready, r * GT + (t + 1))
                    for h in range(2):
                        w = slice(h * HALF, (h + 1) * HALF)
                        dve.scalar_tensor_tensor(out=U[:, b, j, w], in0=G[:, b, j, w],
                                                 scalar=keep["has"][:, bass.ds(r * GT + t, 1)],
                                                 in1=u[:, 2 * (t % 2) + h, 0:HALF], op0=ALU.mult, op1=ALU.add
                                                 ).then_inc(u_out, 1)

                def add_residual(r, b, j):
                    t = GROUP * b + j
                    if j == 0:
                        dve.wait_ge(res_ready, r * 2 + (b + 1))
                    dve.wait_ge(o_ready, r * GT + (t + 1))
                    dve.tensor_tensor(XB[:, b, j, :], o[:, t % 2, :], XB[:, b, j, :], ALU.add).then_inc(o_out, 1)

                def round_(r, late):
                    for j in range(GROUP):
                        add_run(r, 0, j)
                    for j in range(GROUP):
                        add_run(r, 1, j)
                        hidden(r, 0, Z_SLOT[j])
                        stats(r + 1, late, 2 * j)
                    for j in range(GROUP):
                        if j == 0:
                            scale(r + 1)
                        add_residual(r, 0, j)
                        hidden(r, 1, Z_SLOT[j])
                    for j in range(GROUP):
                        add_residual(r, 1, j)
                        turned_rows(r + 1, (2 * j, 2 * j + 1))

                for i in range(GROUP):
                    stats(0, 0, 2 * i)
                scale(0)
                split_on_dve(dve, W3raw, W3h[:, :, :], W3l[:, :, :], w_hi, 1, w_lo)
                turned_rows(0, range(2 * KF))
                split_on_dve(dve, W4raw, W4h[:, :, :], W4l[:, :, :], w_hi, 2, w_lo)
                with dve.Fori(0, NR - 2) as r:
                    round_(r, 0)
                for r in (NR - 2, NR - 1):
                    round_(r, 32)

            @block.tensor
            def _(pe):
                def transpose(r, k, source):
                    pe.wait_ge(tp_free, r * TPR + (k + 1))
                    for j in range(GROUP):
                        mm = pe.transpose(tp[:, k % 2, j * P:(j + 1) * P], source(j), keep["ident"][:, :])
                    mm.then_inc(tp_ready, 1)

                def turn_rows(r, chunks):
                    for k in chunks:
                        b, c = k // KF, k % KF
                        if c == 0:
                            pe.wait_ge(h_ready, r * GT + (GROUP * b + GROUP))
                        transpose(r, k, lambda j: X[:, b, j, c * P:(c + 1) * P])

                def turn_sums(r, b, chunks):
                    for c in chunks:
                        pe.wait_ge(u_out, r * (2 * GT) + (2 * GROUP * (b + 1) + 4))
                        transpose(r, 2 * KF + KI * b + c, lambda j: U[:, b, j, c * P:(c + 1) * P])

                def first(r, b, j):
                    t = GROUP * b + j
                    if j == 0:
                        pe.wait_ge(tp_free, r * TPR + (KF * b + KF + 2))
                    pe.wait_ge(u_out, r * (2 * GT) + (2 * t + 2))
                    for h in range(2):
                        w = slice(h * HALF, (h + 1) * HALF)
                        for c in range(KF):
                            mm = three(pe, u[:, 2 * (t % 2) + h, 0:HALF],
                                       (hTh[:, b, c, j * P:(j + 1) * P], hTl[:, b, c, j * P:(j + 1) * P]),
                                       (W3h[:, c, w], W3l[:, c, w]), c == 0, c == KF - 1)
                    mm.then_inc(u_ready, 1)

                def second(r, b, j):
                    t = GROUP * b + j
                    if j == 0:
                        pe.wait_ge(tp_free, r * TPR + (2 * KF + KI * b + KI + 2))
                    pe.wait_ge(o_out, r * GT + (t + 1))
                    pe.wait_ge(w_lo, 2)
                    for c in range(KI):
                        mm = three(pe, o[:, t % 2, :], (zh[:, b, c, j * P:(j + 1) * P], zl[:, b, c, j * P:(j + 1) * P]),
                                   (W4h[:, c, :], W4l[:, c, :]), c == 0, c == KI - 1)
                    mm.then_inc(o_ready, 1)

                pe.sem_inc(tp_free, 2)
                pe.sem_inc(u_out, 4)
                pe.sem_inc(o_out, 2)
                turn_rows(0, range(2 * KF))
                pe.wait_ge(w_lo, 1)
                with pe.Fori(0, NR) as r:
                    for j in range(GROUP):
                        first(r, 0, j)
                    for j in range(GROUP):
                        first(r, 1, j)
                        turn_sums(r, 0, Z_SLOT[j])
                    for j in range(GROUP):
                        second(r, 0, j)
                        turn_sums(r, 1, Z_SLOT[j])
                    for j in range(GROUP):
                        second(r, 1, j)
                        turn_rows(r + 1, (2 * j, 2 * j + 1))


def layer1_messages(nc, core, a, keep, x1, msg, logit):
    sem = core.sem
    w_loaded, w_hi, w_lo, diag_set = sem("d_w"), sem("d_whi"), sem("d_wlo"), sem("d_diag")
    proj_ready = sem("d_proj")
    idx_staged, go = sem("d_idx"), sem("d_go")
    x_loaded = [sem("d_x0"), sem("d_x1")]
    ln_step, var_ready, std_ready, norm_ready, h_ready = (sem("d_" + n) for n in ("lnstep", "var", "std", "norm", "h"))
    tp_ready, tp_free, hT_hi = sem("d_tp"), sem("d_tpfree"), sem("d_hThi")
    m_ready, m_out = sem("d_m"), [sem("d_mo0"), sem("d_mo1")]
    dot_ready, dot_step, dot_read = sem("d_dot"), sem("d_dotstep"), sem("d_dotread")
    flat_ready, flat_out, go_pe = sem("d_flat"), sem("d_flatout"), sem("d_gope")
    MW = (F + HEADS) // 2

    with ExitStack() as st:
        sb = lambda n, s, d=F32: core.sb(st, "d_" + n, s, d)
        X = sb("X", [P, 2, 2, GROUP, F])
        idx = sb("idx", [P, 2, 2 * GROUP], I32)
        stt = core.stats(st, "d")
        hTh, hTl = sb("hTh", [P, 3, KF, GROUP * P], F32R), sb("hTl", [P, 3, KF, GROUP * P], F32R)
        Wh, Wl = sb("Wh", [P, KF, F + HEADS], F32R), sb("Wl", [P, KF, F + HEADS], F32R)
        Ah, Al = sb("Ah", [P, KF, HEADS], F32R), sb("Al", [P, KF, HEADS], F32R)
        Wraw = sb("Wraw", [P, KF, F])
        Wrow = sb("Wrow", [P, KF, F])
        diag = sb("diag", [P, 2, KF, HEADS])
        dots = sb("dots", [P, GROUP, HEADS])
        flat = sb("flat", [HEADS, GROUP * P])
        tp = core.ps(st, "d_tp_ps", [P, 2, 512])
        m = core.ps(st, "d_m_ps", [P, 4, 512])
        dot = core.ps(st, "d_dot_ps", [P, 512])
        proj = core.ps(st, "d_proj_ps", [P, 512])
        dotv = dot[:, 0:GROUP * HEADS].rearrange("p (j h) -> p j h", h=HEADS)
        projv = proj[:, 0:2 * KF * HEADS].rearrange("p (a k h) -> p a k h", a=2, h=HEADS)

        with nc.Block() as block:
            @block.sync
            def _(sp):
                sp.dma_start(Wraw[:, :, :], a["W1T"].rearrange("(k p) n -> p k n", p=P)).then_inc(w_loaded, 16)
                sp.dma_start(Wrow[:, :, :], a["L1_gnn_W"].rearrange("(k p) n -> p k n", p=P)).then_inc(w_loaded, 16)
                sp.wait_ge(diag_set, 1)
                for q, n in enumerate(("L1_gnn_a_src", "L1_gnn_a_dst")):
                    for h in range(HEADS):
                        sp.dma_start(diag[HD * (h % 2):HD * (h % 2) + HD, q, h // 2, h:h + 1],
                                     a[n][h:h + 1, :].rearrange("o d -> d o"), allow_slow_non_contiguous=True
                                     ).then_inc(w_loaded, 16)

            @block.gpsimd
            def _(pool):
                pool.memset(diag[:, :, :, :], 0.0).then_inc(diag_set, 1)

                def gather(g, b, before, turned):
                    pool.wait_ge(x_loaded[b], before)
                    pool.sem_inc(go, 1)
                    for q, n in enumerate(("src", "dst")):
                        pool.tensor_copy(idx[:, b, q * GROUP:(q + 1) * GROUP],
                                         keep[n][:, bass.ds(g * GROUP, GROUP)]).then_inc(idx_staged, 1)
                    pool.wait_ge(idx_staged, g * 2 + 2)
                    pool.wait_ge(tp_ready, turned)
                    pool.sem_inc(go, 1)
                    for i in range(2 * GROUP):
                        pool.indirect_dma_start(X[:, b, i // GROUP, i % GROUP, :], None, x1[:, :],
                                                bass.IndirectOffsetOnAxis(idx[:, b, i:i + 1], 0),
                                                bounds_check=ROWS_N - 1, oob_is_err=False).then_inc(x_loaded[b], 16)

                gather(0, 0, 0, 0)
                with pool.Fori(0, ER) as r:
                    gather(r * 2 + 1, 1, r * 128, r * 16)
                    gather(r * 2 + 2, 0, r * 128 + 128, r * 16 + 8)
                pool.wait_ge(x_loaded[0], 128 * (ER + 1))
                pool.wait_ge(x_loaded[1], 128 * ER)
                pool.sem_inc(go, 1)

            @block.scalar
            def _(act):
                def root(g, q):
                    n = slice(GROUP * q, GROUP * q + GROUP)
                    act.wait_ge(var_ready, g * 8 + (4 * q + 4))
                    act.activation(stt["std"][:, n], stt["mv"][:, n, 1], ACT.Sqrt, bias=keep["eps"][:, 0:1]).then_inc(std_ready, 1)

                def norm_rows(g, b, q, rows):
                    act.wait_ge(norm_ready, g * 2 + (q + 1))
                    for j in rows:
                        x = X[:, b, q, j, :]
                        relu_norm(act, x, x, stt, GROUP * q + j).then_inc(h_ready, 1)

                def turned(g, b, q, chunks, used):
                    if q == 0:
                        act.wait_ge(m_ready, used)
                    else:
                        act.wait_ge(flat_ready, used)
                    for c in chunks:
                        k = KF * q + c
                        act.wait_ge(tp_ready, g * 8 + (k + 1))
                        act.copy(hTh[:, 2 if q else b, c, :], tp[:, k % 2, :]).then_inc(hT_hi, 1)

                def message(g, j):
                    act.wait_ge(m_ready, g * 4 + (j + 1))
                    act.copy(msg[:, bass.ds(g * 4 + j, 1), 0:MW],
                             m[:, 2 * (j % 2):2 * (j % 2) + 1, 0:MW]).then_inc(m_out[0], 1)

                for q in range(2):
                    root(0, q)
                    norm_rows(0, 0, q, range(GROUP))
                split_on_act(act, Wraw[:, :, :], Wh[:, :, 0:F], w_loaded, 16 * 18, w_hi)
                split_on_act(act, projv[:, 0, :, :], Wh[:, :, F:F + HEADS], proj_ready, 1, w_hi)
                split_on_act(act, projv[:, 1, :, :], Ah[:, :, :], proj_ready, 1, w_hi)
                turned(0, 0, 0, range(KF), 0)
                with act.Fori(0, ER) as r:
                    for b in range(2):
                        g = r * 2 + b
                        message(g, 0)
                        turned(g, b, 1, (0, 1), g)
                        root(g + 1, 0)
                        norm_rows(g + 1, 1 - b, 0, (0,))
                        message(g, 1)
                        norm_rows(g + 1, 1 - b, 0, (1,))
                        turned(g, b, 1, (2,), g)
                        norm_rows(g + 1, 1 - b, 0, (2,))
                        turned(g, b, 1, (3,), g)
                        norm_rows(g + 1, 1 - b, 0, (3,))
                        message(g, 2)
                        act.wait_ge(flat_ready, g + 1)
                        act.wait_ge(dot_ready, g)
                        act.copy(flat[:, :], proj[0:HEADS, :]).then_inc(flat_out, 1)
                        turned(g + 1, 1 - b, 0, (0, 1), g * 4)
                        root(g + 1, 1)
                        message(g, 3)
                        turned(g + 1, 1 - b, 0, (2, 3), g * 4)
                        norm_rows(g + 1, 1 - b, 1, range(GROUP))

            @block.vector
            def _(dve):

                def stats(b, q, loaded):
                    if q == 0:
                        dve.wait_ge(x_loaded[b], loaded)
                    for j in range(GROUP):
                        dve.bn_stats(stt["raw"][:, GROUP * q + j, :], X[:, b, q, j, :]).then_inc(ln_step, 1)

                def scale(g, q):
                    n = slice(GROUP * q, GROUP * q + GROUP)
                    dve.wait_ge(ln_step, g * 10 + (5 * q + 4))
                    dve.sem_inc(stt["go"], 1)
                    for i in range(GROUP * q, GROUP * q + GROUP):
                        dve.bn_aggr(stt["mv"][:, i, :], stt["raw"][:, i, :]).then_inc(var_ready, 1)
                    dve.wait_ge(std_ready, g * 2 + (q + 1))
                    dve.reciprocal(stt["rstd"][:, n], stt["std"][:, n]).then_inc(ln_step, 1)
                    dve.wait_ge(ln_step, g * 10 + (5 * q + 5))
                    dve.scalar_tensor_tensor(out=stt["shift"][:, n], in0=stt["mv"][:, n, 0], scalar=-1.0, in1=stt["rstd"][:, n],
                                             op0=ALU.mult, op1=ALU.mult).then_inc(norm_ready, 1)

                def turned(g, b, q, chunks):
                    for c in chunks:
                        k = KF * q + c
                        at = 2 if q else b
                        dve.wait_ge(hT_hi, g * 8 + (k + 1))
                        dve.tensor_tensor(hTl[:, at, c, :], tp[:, k % 2, :], hTh[:, at, c, :].bitcast(F32),
                                          ALU.subtract).then_inc(tp_free, 1)

                def message(g, j):
                    dve.wait_ge(m_ready, g * 4 + (j + 1))
                    dve.tensor_copy(msg[:, bass.ds(g * 4 + j, 1), MW:2 * MW],
                                    m[:, 2 * (j % 2) + 1:2 * (j % 2) + 2, 0:MW]).then_inc(m_out[1], 1)

                def logits(g):
                    dve.wait_ge(dot_ready, g + 1)
                    dve.wait_ge(m_out[1], g * 4 + (4 + 2))
                    dve.tensor_tensor(dots[:, :, :], dotv, msg[:, bass.ds(g * 4, GROUP), F:F + HEADS], ALU.add
                                      ).then_inc(dot_step, 1)
                    dve.wait_ge(dot_step, g * 2 + 1)
                    dve.scalar_tensor_tensor(out=dots[:, :, :], in0=dots[:, :, :], scalar=0.2, in1=dots[:, :, :],
                                             op0=ALU.mult, op1=ALU.max).then_inc(dot_step, 1)
                    dve.wait_ge(dot_step, g * 2 + 2)
                    dve.tensor_tensor(logit[:, bass.ds(g * 4, GROUP), :], dots[:, :, :], keep["fac"][:, bass.ds(g * 4, GROUP), :],
                                      ALU.mult).then_inc(dot_read, 1)

                for q in range(2):
                    stats(0, q, 128)
                    scale(0, q)
                split_on_dve(dve, Wraw[:, :, :], Wh[:, :, 0:F], Wl[:, :, 0:F], w_hi, 1, w_lo)
                split_on_dve(dve, projv[:, 0, :, :], Wh[:, :, F:F + HEADS], Wl[:, :, F:F + HEADS], w_hi, 3, w_lo)
                split_on_dve(dve, projv[:, 1, :, :], Ah[:, :, :], Al[:, :, :], w_hi, 3, w_lo)
                turned(0, 0, 0, range(KF))
                with dve.Fori(0, ER) as r:
                    for b in range(2):
                        g = r * 2 + b
                        stats(1 - b, 0, r * 128 + 128 * (b + 1))
                        message(g, 0)
                        turned(g, b, 1, (0, 1))
                        scale(g + 1, 0)
                        message(g, 1)
                        turned(g, b, 1, (2, 3))
                        stats(1 - b, 1, None)
                        message(g, 2)
                        turned(g + 1, 1 - b, 0, (0, 1))
                        scale(g + 1, 1)
                        message(g, 3)
                        turned(g + 1, 1 - b, 0, (2, 3))
                        logits(g)

            @block.tensor
            def _(pe):
                pe.wait_ge(w_loaded, 16 * 18)
                for q in range(2):
                    for k in range(KF):
                        for c in range(KF):
                            mm = pe.matmul(projv[:, q, k, :], Wrow[:, c, k * P:(k + 1) * P], diag[:, q, c, :],
                                           start=(c == 0), stop=(c == KF - 1))
                mm.then_inc(proj_ready, 1)
                pe.sem_inc(tp_free, 2)
                pe.sem_inc(m_out[0], 2)
                pe.sem_inc(m_out[1], 2)

                def turn(g, b, q, chunks):
                    pe.wait_ge(h_ready, g * 8 + (GROUP * q + GROUP))
                    for c in chunks:
                        k = KF * q + c
                        pe.wait_ge(tp_free, g * 8 + (k + 1))
                        for j in range(GROUP):
                            mm = pe.transpose(tp[:, k % 2, j * P:(j + 1) * P],
                                              X[:, b, q, j, c * P:(c + 1) * P], keep["ident"][:, :])
                        mm.then_inc(tp_ready, 1)

                def message(g, b, j):
                    for h in range(2):
                        pe.wait_ge(m_out[h], g * 4 + (j + 1))
                        for c in range(KF):
                            if j == 0 and h == 0:
                                pe.wait_ge(tp_free, g * 8 + (c + 1 + 2))
                            mm = three(pe, m[:, 2 * (j % 2) + h, 0:MW],
                                       (hTh[:, b, c, j * P:(j + 1) * P], hTl[:, b, c, j * P:(j + 1) * P]),
                                       (Wh[:, c, MW * h:MW * h + MW], Wl[:, c, MW * h:MW * h + MW]),
                                       c == 0, c == KF - 1)
                    mm.then_inc(m_ready, 1)

                turn(0, 0, 0, range(KF))
                pe.wait_ge(w_lo, 3)
                with pe.Fori(0, ER) as r:
                    for b in range(2):
                        g = r * 2 + b
                        message(g, b, 0)
                        turn(g, b, 1, (0, 1))
                        message(g, b, 1)
                        turn(g, b, 1, (2, 3))
                        message(g, b, 2)
                        pe.wait_ge(tp_free, g * 8 + (8 + 2))
                        pe.wait_ge(flat_out, g)
                        for c in range(KF):
                            mm = three(pe, proj[0:HEADS, :], (Ah[:, c, :], Al[:, c, :]), (hTh[:, 2, c, :], hTl[:, 2, c, :]),
                                       c == 0, c == KF - 1)
                        mm.then_inc(flat_ready, 1)
                        turn(g + 1, 1 - b, 0, (0, 1))
                        message(g, b, 3)
                        turn(g + 1, 1 - b, 0, (2, 3))
                        pe.wait_ge(flat_out, g + 1)
                        pe.wait_ge(dot_read, g)
                        pe.sem_inc(go_pe, 1)
                        for j in range(GROUP):
                            mm = pe.transpose(dotv[:, j, :], flat[:, j * P:(j + 1) * P], keep["ident"][0:HEADS, 0:HEADS])
                        mm.then_inc(dot_ready, 1)


def layer1_softmax(nc, core, a, keep, logit):
    sem = core.sem
    loaded, same_ready, turned, flat, fwd_done, bwd_done, shifted, exped, back, out_done = (
        sem("s_" + n) for n in ("loaded", "same", "turned", "flat", "fwd", "bwd", "shift", "exp", "back", "out"))
    with ExitStack() as st:
        sb = lambda n, s, d=F32: core.sb(st, "s_" + n, s, d)
        L = sb("L", [HEADS, ROWS_E])
        top = sb("top", [HEADS, ROWS_E])
        ids = sb("ids", [HEADS, ROWS_E], I32)
        same = sb("same", [HEADS, ROWS_E + 1], U16)
        turn = core.ps(st, "s_turn_ps", [P, 4, 512])
        rows = core.ps(st, "s_rows_ps", [P, 512])
        rowsv = rows[:, 0:ET * HEADS].rearrange("p (t h) -> p t h", h=HEADS)
        with nc.Block() as block:
            @block.sync
            def _(sp):
                sp.dma_start(ids[:, :], a["dst_flat"].broadcast_to([HEADS, ROWS_E])).then_inc(loaded, 16)

            @block.tensor
            def _(pe):
                for g in range(EG):
                    if g >= 4:
                        pe.wait_ge(flat, g - 3)
                    for j in range(GROUP):
                        mm = pe.transpose(turn[0:HEADS, g % 4, j * P:(j + 1) * P], logit[:, GROUP * g + j, :], keep["ident"][:, :])
                    mm.then_inc(turned, 1)
                pe.wait_ge(exped, 1)
                for t in range(ET):
                    mm = pe.transpose(rowsv[:, t, :], L[:, t * P:(t + 1) * P], keep["ident"][0:HEADS, 0:HEADS])
                mm.then_inc(back, 1)

            @block.scalar
            def _(act):
                for g in range(EG):
                    act.wait_ge(turned, g + 1)
                    act.copy(L[:, g * 512:(g + 1) * 512], turn[0:HEADS, g % 4, :]).then_inc(flat, 1)
                act.wait_ge(shifted, 1)
                act.activation(L[:, :], L[:, :], ACT.Exp).then_inc(exped, 1)

            @block.vector
            def _(dve):
                dve.memset(same[:, 0:1], 0).then_inc(same_ready, 1)
                dve.memset(same[:, ROWS_E:ROWS_E + 1], 0).then_inc(same_ready, 1)
                dve.wait_ge(loaded, 16)
                dve.tensor_tensor(same[:, 1:ROWS_E], ids[:, 1:ROWS_E], ids[:, 0:ROWS_E - 1], ALU.is_equal).then_inc(same_ready, 1)
                dve.wait_ge(same_ready, 3)
                dve.wait_ge(flat, EG)
                dve.tensor_tensor_scan(top[:, :], same[:, 0:ROWS_E], L[:, :], 0.0, ALU.mult, ALU.max).then_inc(fwd_done, 1)
                dve.wait_ge(fwd_done, 1)
                dve.tensor_tensor_scan(top[:, ::-1], same[:, ROWS_E:0:-1], top[:, ::-1], 0.0, ALU.mult, ALU.max).then_inc(bwd_done, 1)
                dve.wait_ge(bwd_done, 1)
                dve.tensor_tensor(L[:, :], L[:, :], top[:, :], ALU.subtract).then_inc(shifted, 1)
                dve.wait_ge(back, 1)
                dve.tensor_copy(logit[:, :, :], rowsv).then_inc(out_done, 1)


def layer1_sums(nc, core, a, keep, msg, prob, T1):
    sem = core.sem
    init, weighed, match_ready, carry_ready = (sem("e_" + n) for n in ("init", "weighed", "match", "carry"))
    y_hi, y_lo, bulk_ready = sem("e_yhi"), sem("e_ylo"), sem("e_bulk")
    sum_ready, den_step, scaled, go = (sem("e_" + n) for n in ("sum", "denstep", "scaled", "go"))
    stored = [sem(f"e_st{b}") for b in range(GROUP)]
    LW = (GW, GW + HEADS)
    with ExitStack() as st:
        sb = lambda n, s, d=F32: core.sb(st, "e_" + n, s, d)
        Y = sb("Y", [P, GROUP, 1, F + HEADS])
        Yh, Yl = sb("Yh", [P, GROUP, F + HEADS], F32R), sb("Yl", [P, GROUP, F + HEADS], F32R)
        carry = sb("carry", [1, 2, GW + HEADS])
        match = sb("match", [P, 2, GROUP, P], F32R)
        den, inv = sb("den", [P, HEADS]), sb("inv", [P, HEADS])
        T = sb("T", [P, GROUP, F])
        s = core.ps(st, "e_s_ps", [P, 2 * GROUP, 512])
        half = HEADS // 2
        with nc.Block() as block:
            @block.sync
            def _(sp):
                with sp.Fori(0, EG) as g:
                    for j in range(GROUP):
                        sp.wait_ge(scaled, g * GROUP + (j + 1 + GROUP))
                        sp.dma_start(T1[bass.ds((g * GROUP + j) * P, P), :], T[:, j, :]).then_inc(stored[j], 16)
                for j in range(GROUP):
                    sp.wait_ge(stored[j], 16 * EG)

            @block.scalar
            def _(act):
                def split(g, j):
                    t = g * GROUP + j
                    act.wait_ge(weighed, t * 2 + 2)
                    act.wait_ge(bulk_ready, t + 1)
                    act.copy(Yh[:, j % GROUP, :], Y[:, j % GROUP, 0, :]).then_inc(y_hi, 1)

                def group(g, last):
                    for j in range(GROUP):
                        for h in range(2):
                            act.wait_ge(sum_ready, g * (2 * GROUP) + (2 * j + h + 1))
                            act.copy(carry[0:1, h, 0:LW[h]], s[0:1, 2 * j + h, 0:LW[h]]).then_inc(carry_ready, 1)
                        if not (last and j >= 2):
                            split(g, j + 2)

                split(0, 0)
                split(0, 1)
                with act.Fori(0, EG - 1) as g:
                    group(g, False)
                group(EG - 1, True)

            @block.gpsimd
            def _(pool):
                pool.wait_ge(init, 2)

                with pool.Fori(0, EG) as g:
                    for j in range(GROUP):
                        t = g * GROUP + j
                        pool.wait_ge(y_lo, t + 1)
                        pool.sem_inc(go, 1)
                        pool.tensor_tensor(Y[:, j, :, 0:F].rearrange("p o (h d) -> p (o h) d", d=HD),
                                           msg[:, bass.ds(t, 1), 0:F].rearrange("p o (h d) -> p (o h) d", d=HD),
                                           over(prob[:, bass.ds(t, 1), :].rearrange("p o h -> p (o h)").unsqueeze(2), [P, HEADS, HD]),
                                           ALU.mult).then_inc(weighed, 1)
                        pool.tensor_copy(Y[:, j, :, F:F + HEADS], prob[:, bass.ds(t, 1), :]).then_inc(weighed, 1)

            @block.vector
            def _(dve):
                dve.memset(carry[:, :, :], 0.0).then_inc(init, 1)
                dve.memset(prob[0:1, :, :], 0.0).then_inc(init, 1)

                def build_match(g, b):
                    dve.tensor_tensor(match[:, b, :, :], keep["rows"][:, bass.ds(g * (GROUP * P), GROUP * P)].rearrange("p (j q) -> p j q", q=P),
                                      over(keep["dst"][:, bass.ds(g * GROUP, GROUP)].unsqueeze(2), [P, GROUP, P]),
                                      ALU.is_equal).then_inc(match_ready, 1)

                def sums(g, j):
                    t = g * GROUP + j
                    dve.wait_ge(carry_ready, t * 2 + 3)
                    dve.tensor_scalar(den[:, :], s[:, 2 * j + 1, GW:GW + HEADS], 1e-10, None, ALU.add).then_inc(den_step, 1)
                    dve.wait_ge(den_step, t * 2 + 1)
                    dve.reciprocal(inv[:, :], den[:, :]).then_inc(den_step, 1)
                    dve.wait_ge(den_step, t * 2 + 2)
                    dve.wait_ge(stored[j], g * 16)
                    dve.tensor_tensor(T[:, j, :].rearrange("p (a h d) -> p a h d", a=2, d=HD),
                                      s[:, 2 * j:2 * j + 2, 0:GW].rearrange("p a (h d) -> p a h d", d=HD),
                                      over(inv[:, :].rearrange("p (a h) -> p a h", a=2).unsqueeze(3), [P, 2, half, HD]),
                                      ALU.mult).then_inc(scaled, 1)

                def split(g, j):
                    dve.wait_ge(y_hi, g * GROUP + (j + 1))
                    dve.tensor_tensor(Yl[:, j % GROUP, :], Y[:, j % GROUP, 0, :], Yh[:, j % GROUP, :].bitcast(F32),
                                      ALU.subtract).then_inc(y_lo, 1)

                def group(g, b, last):
                    if not last:
                        build_match(g + 1, 1 - b)
                    for j in range(GROUP):
                        if not (last and j >= 2):
                            split(g, j + 2)
                        sums(g, j)

                build_match(0, 0)
                split(0, 0)
                split(0, 1)
                with dve.Fori(0, EG // 2 - 1) as q:
                    for b in range(2):
                        group(q * 2 + b, b, False)
                group(EG - 2, 0, False)
                group(EG - 1, 1, True)

            @block.tensor
            def _(pe):
                pe.sem_inc(y_lo, GROUP)
                pe.sem_inc(carry_ready, 1)
                pe.sem_inc(bulk_ready, GROUP)
                pe.sem_inc(scaled, GROUP)
                pe.wait_ge(init, 2)
                with pe.Fori(0, EG // 2) as q:
                    for b in range(2):
                        g = q * 2 + b
                        pe.wait_ge(match_ready, g + 1)
                        for j in range(GROUP):
                            t = g * GROUP + j
                            pe.wait_ge(y_lo, t + (1 + GROUP))
                            pe.wait_ge(scaled, t + 1)
                            for h in range(2):
                                pe.matmul(s[:, 2 * j + h, 0:LW[h]], match[:, b, j, :],
                                          Yh[:, j, GW * h:GW * h + LW[h]], start=True, stop=False)
                                mm = pe.matmul(s[:, 2 * j + h, 0:LW[h]], match[:, b, j, :],
                                               Yl[:, j, GW * h:GW * h + LW[h]], start=False, stop=False)
                            mm.then_inc(bulk_ready, 1)
                            for h in range(2):
                                pe.wait_ge(carry_ready, t * 2 + h)
                                pe.matmul(s[:, 2 * j + h, 0:LW[h]], match[0:1, b, j, :].bitcast(F32), carry[0:1, h, 0:LW[h]],
                                          start=False, stop=True).then_inc(sum_ready, 1)


def layer1_nodes(nc, core, a, keep, x1, T1, x2):
    sem = core.sem
    w_loaded, init, idx_staged, go = sem("n_w"), sem("n_init"), sem("n_idx"), sem("n_go")
    x_loaded = [sem("n_x0"), sem("n_x1")]
    run_loaded = [sem("n_g0"), sem("n_g1")]
    ln_step, var_ready, std_ready, norm_ready, h_ready = (sem("n_" + n) for n in ("lnstep", "var", "std", "norm", "h"))
    ln2_step, var2_ready, std2_ready, norm2_ready, n_ready = (sem("n2_" + n) for n in ("lnstep", "var", "std", "norm", "n"))
    res_ready, added, times_gamma, out_ready = sem("n_res"), sem("n_added"), sem("n_gamma"), sem("n_out")
    stored = sem("n_stored")
    GT = 2 * GROUP

    with ExitStack() as st:
        sb = lambda n, s, d=F32: core.sb(st, "n_" + n, s, d)
        X = sb("X", [P, 2, 2, GROUP, F])
        G = sb("G", [P, 2, 2, GROUP, F])
        H = sb("H", [P, 2, GROUP, F])
        O = sb("O", [P, 2, GROUP, XW])
        idx = sb("idx", [P, GT], I32)
        one, two = core.stats(st, "n1"), core.stats(st, "n2")
        gamma, beta = sb("gamma", [P, F]), sb("beta", [P, F])

        def rounds(engine, body):
            with engine.Fori(0, NR // 2 - 1) as q:
                for rb in range(2):
                    body(q, rb, True, True)
            body(NR // 2 - 1, 0, True, False)
            body(NR // 2 - 1, 1, False, False)

        def following(q, rb):
            return (q, 1) if rb == 0 else (q + 1, 0)

        with nc.Block() as block:
            @block.sync
            def _(sp):
                sp.dma_start(gamma[:, :], a["L1_gnn_ln_gamma"].rearrange("(o n) -> o n", o=1).broadcast_to([P, F])).then_inc(w_loaded, 16)
                sp.dma_start(beta[:, :], a["L1_gnn_ln_beta"].rearrange("(o n) -> o n", o=1).broadcast_to([P, F])).then_inc(w_loaded, 16)
                def load(q, rb):
                    for b in range(2):
                        sp.dma_start(X[:, rb, b, :, :], group_rows(x1, q * 4 + (2 * rb + b), F)).then_inc(x_loaded[rb], 16)

                def body(q, rb, one_more, two_more):
                    for b in range(2):
                        sp.wait_ge(out_ready, q * 16 + (8 * rb + 4 * b + 4))
                        sp.dma_start(group_rows(x2, q * 4 + (2 * rb + b), XW), O[:, b, :, :]).then_inc(stored, 16)
                    if two_more:
                        load(q + 1, rb)

                load(0, 0)
                load(0, 1)
                rounds(sp, body)
                sp.wait_ge(stored, 16 * NG)

            @block.gpsimd
            def _(pool):
                pool.memset(G[:, :, :, :, :], 0.0).then_inc(init, 1)
                pool.wait_ge(w_loaded, 32)
                pool.wait_ge(init, 1)

                def gather(q, rb):
                    r = q * 2 + rb
                    pool.tensor_copy(idx[:, :], keep["slot"][:, bass.ds(r * GT, GT)]).then_inc(idx_staged, 1)
                    pool.wait_ge(idx_staged, r + 1)
                    pool.sem_inc(go, 1)
                    for i in range(GT):
                        pool.indirect_dma_start(G[:, rb, i // GROUP, i % GROUP, :], None, T1[:, :],
                                                bass.IndirectOffsetOnAxis(idx[:, i:i + 1], 0),
                                                bounds_check=ROWS_E - 1, oob_is_err=False).then_inc(run_loaded[rb], 16)
                    pool.wait_ge(run_loaded[rb], q * 128 + 128)
                    pool.sem_inc(go, 1)

                def body(q, rb, one_more, two_more):
                    r = q * 2 + rb
                    pool.wait_ge(h_ready, r * GT + GT)
                    pool.sem_inc(go, 1)
                    for b in range(2):
                        pool.tensor_tensor(X[:, rb, b, :, :], X[:, rb, b, :, :], over(beta[:, :].unsqueeze(1), [P, GROUP, F]),
                                           ALU.add).then_inc(res_ready, 1)
                    if one_more:
                        pool.wait_ge(out_ready, r * GT)
                        pool.sem_inc(go, 1)
                        gather(*following(q, rb))

                gather(0, 0)
                rounds(pool, body)

            @block.scalar
            def _(act):
                def norm1(q, rb):
                    r = q * 2 + rb
                    act.wait_ge(var_ready, r * GT + GT)
                    layer_norm_std(act, one, keep["eps"]).then_inc(std_ready, 1)
                    act.wait_ge(norm_ready, r + 1)
                    act.wait_ge(added, r * GT)
                    for i in range(GT):
                        relu_norm(act, H[:, i // GROUP, i % GROUP, :], X[:, rb, i // GROUP, i % GROUP, :], one, i).then_inc(h_ready, 1)

                def body(q, rb, one_more, two_more):
                    r = q * 2 + rb
                    act.wait_ge(var2_ready, r * GT + GT)
                    layer_norm_std(act, two, keep["eps"]).then_inc(std2_ready, 1)
                    act.wait_ge(norm2_ready, r + 1)
                    for i in range(GT):
                        g = G[:, rb, i // GROUP, i % GROUP, :]
                        act.activation(g, g, ACT.Identity, bias=two["shift"][:, i:i + 1],
                                       scale=two["rstd"][:, i:i + 1]).then_inc(n_ready, 1)
                    if one_more:
                        norm1(*following(q, rb))

                norm1(0, 0)
                rounds(act, body)

            @block.vector
            def _(dve):
                dve.wait_ge(w_loaded, 32)

                def stats1(q, rb, rows):
                    if 0 in rows:
                        dve.wait_ge(x_loaded[rb], q * 32 + 32)
                    for i in rows:
                        dve.bn_stats(one["raw"][:, i, :], X[:, rb, i // GROUP, i % GROUP, :]).then_inc(ln_step, 1)

                def mean1(q, rb):
                    r = q * 2 + rb
                    dve.wait_ge(ln_step, r * 9 + GT)
                    dve.sem_inc(one["go"], 1)
                    for i in range(GT):
                        dve.bn_aggr(one["mv"][:, i, :], one["raw"][:, i, :]).then_inc(var_ready, 1)

                def scale1(q, rb):
                    r = q * 2 + rb
                    dve.wait_ge(std_ready, r + 1)
                    layer_norm_scale(dve, one, ln_step, r * 9 + 9, norm_ready)

                def body(q, rb, one_more, two_more):
                    r = q * 2 + rb
                    sums = [G[:, rb, i // GROUP, i % GROUP, :] for i in range(GT)]
                    dve.wait_ge(run_loaded[rb], q * 128 + 128)
                    for i in range(GT + 1):
                        if i < GT:
                            dve.wait_ge(h_ready, r * GT + (i + 1))
                            dve.scalar_tensor_tensor(out=sums[i], in0=sums[i], scalar=keep["has"][:, bass.ds(r * GT + i, 1)],
                                                     in1=H[:, i // GROUP, i % GROUP, :], op0=ALU.mult, op1=ALU.add
                                                     ).then_inc(added, 1)
                        if i:
                            dve.wait_ge(added, r * GT + i)
                            dve.bn_stats(two["raw"][:, i - 1, :], sums[i - 1]).then_inc(ln2_step, 1)
                    if one_more:
                        nxt = following(q, rb)
                        stats1(*nxt, (0, 1))
                    dve.wait_ge(ln2_step, r * 9 + GT)
                    dve.sem_inc(two["go"], 1)
                    for i in range(GT):
                        dve.bn_aggr(two["mv"][:, i, :], two["raw"][:, i, :]).then_inc(var2_ready, 1)
                    if one_more:
                        stats1(*nxt, (2,))
                    dve.wait_ge(std2_ready, r + 1)
                    layer_norm_scale(dve, two, ln2_step, r * 9 + 9, norm2_ready)
                    if one_more:
                        stats1(*nxt, (3, 4, 5, 6, 7))
                        mean1(*nxt)
                    dve.wait_ge(stored, r * 32)
                    dve.tensor_copy(O[:, :, :, F:XW].rearrange("p b j c -> p (b j) c"),
                                    over(keep["dis"][:, bass.ds(r * GT, GT)].unsqueeze(2), [P, GT, XW - F])).then_inc(times_gamma, 1)
                    for i in range(GT + 1):
                        if i < GT:
                            dve.wait_ge(n_ready, r * GT + (i + 1))
                            dve.tensor_tensor(sums[i], sums[i], gamma[:, :], ALU.mult).then_inc(times_gamma, 1)
                        if i == GT - 1 and one_more:
                            scale1(*nxt)
                        if i:
                            if (i - 1) % GROUP == 0:
                                dve.wait_ge(res_ready, r * 2 + ((i - 1) // GROUP + 1))
                            dve.wait_ge(times_gamma, r * 9 + (i + 1))
                            dve.tensor_tensor(O[:, (i - 1) // GROUP, (i - 1) % GROUP, 0:F], sums[i - 1],
                                              X[:, rb, (i - 1) // GROUP, (i - 1) % GROUP, :], ALU.add).then_inc(out_ready, 1)

                stats1(0, 0, range(GT))
                mean1(0, 0)
                scale1(0, 0)
                rounds(dve, body)


def layer2_edges(nc, core, a, keep, x2, T2):
    sem = core.sem
    go = sem("f_go")
    x_loaded = [sem("f_x0"), sem("f_x1")]
    ln_step, var_ready, std_ready, norm_ready, h_ready = (sem("f_" + n) for n in ("lnstep", "var", "std", "norm", "h"))
    init, masked, carry_ready, match_ready, sum_ready, out_ready = (
        sem("f_" + n) for n in ("init", "masked", "carry", "match", "sum", "out"))
    y_hi, y_lo, bulk_ready = sem("f_yhi"), sem("f_ylo"), sem("f_bulk")
    stored = [sem(f"f_st{b}") for b in range(GROUP)]
    GT = 2 * GROUP
    W = XW
    HW = W // 2
    with ExitStack() as st:
        sb = lambda n, s, d=F32: core.sb(st, "f_" + n, s, d)
        X = sb("X", [P, ET, XW])
        stt = core.stats(st, "f")
        carry = sb("carry", [1, 2, HW])
        match = sb("match", [P, 2, GROUP, P], F32R)
        Yh, Yl = sb("Yh", [P, GROUP, W], F32R), sb("Yl", [P, GROUP, W], F32R)
        T = sb("T", [P, GROUP, W])
        s = core.ps(st, "f_s_ps", [P, 2 * GROUP, 512])

        def tile(r, i, width=F):
            return X[:, bass.ds(r * GT + i, 1), 0:width].rearrange("p o f -> p (o f)")

        with nc.Block() as block:
            @block.sync
            def _(sp):
                with sp.Fori(0, EG) as g:
                    for j in range(GROUP):
                        sp.wait_ge(out_ready, g * GROUP + (j + 1 + GROUP))
                        sp.dma_start(T2[bass.ds((g * GROUP + j) * P, P), :], T[:, j, 0:F + 2]).then_inc(stored[j], 16)
                for j in range(GROUP):
                    sp.wait_ge(stored[j], 16 * EG)

            @block.gpsimd
            def _(pool):
                for t in range(ET):
                    r, i = t // GT, t % GT
                    if i == 0 and r >= 2:
                        pool.wait_ge(x_loaded[r % 2], 128 * (r // 2))
                        pool.sem_inc(go, 1)
                    pool.indirect_dma_start(X[:, t, :], None, x2[:, :], bass.IndirectOffsetOnAxis(keep["src"][:, t:t + 1], 0),
                                            bounds_check=ROWS_N - 1, oob_is_err=False).then_inc(x_loaded[r % 2], 16)

            @block.scalar
            def _(act):
                def norm_row(r, i):
                    relu_norm(act, tile(r, i), tile(r, i), stt, i).then_inc(h_ready, 1)

                def root(r):
                    act.wait_ge(var_ready, r * GT + GT)
                    layer_norm_std(act, stt, keep["eps"]).then_inc(std_ready, 1)
                    act.wait_ge(norm_ready, r + 1)

                def split(r, i):
                    act.wait_ge(h_ready, r * GT + (i + 1))
                    act.wait_ge(masked, r + (i // GT + 1))
                    act.wait_ge(bulk_ready, r * GT + (i + 1))
                    act.copy(Yh[:, i % GROUP, :], tile(r, i, W)).then_inc(y_hi, 1)

                def round_(r, last):
                    for i in range(GT):
                        for h in range(2):
                            act.wait_ge(sum_ready, r * (2 * GT) + (2 * i + h + 1))
                            act.copy(carry[0:1, h, :], s[0:1, 2 * (i % GROUP) + h, 0:HW]).then_inc(carry_ready, 1)
                        if not (last and i >= GT - 2):
                            split(r, i + 2)
                        if i >= GROUP and not last:
                            if i == GROUP:
                                root(r + 1)
                            norm_row(r + 1, 2 * i - GT)
                            norm_row(r + 1, 2 * i - GT + 1)

                root(0)
                for i in range(GT):
                    norm_row(0, i)
                split(0, 0)
                split(0, 1)
                with act.Fori(0, ER - 1) as r:
                    round_(r, False)
                round_(ER - 1, True)

            @block.vector
            def _(dve):
                dve.memset(carry[:, :, :], 0.0).then_inc(init, 1)

                def stats(r, i):
                    dve.bn_stats(stt["raw"][:, i, :], tile(r, i)).then_inc(ln_step, 1)

                def scale(r):
                    ends = X[:, bass.ds(r * GT, GT), F:XW]
                    own = X[0:1, bass.ds(r * GT, GT), F:XW]
                    dve.tensor_scalar(own, own, 0.0, None, ALU.mult).then_inc(masked, 1)
                    dve.wait_ge(ln_step, r * 10 + GT)
                    dve.sem_inc(stt["go"], 1)
                    for i in range(GT):
                        dve.bn_aggr(stt["mv"][:, i, :], stt["raw"][:, i, :]).then_inc(var_ready, 1)
                    dve.wait_ge(masked, r + 1)
                    dve.wait_ge(std_ready, r + 1)
                    layer_norm_scale(dve, stt, ln_step, r * 10 + 9, norm_ready, ends[:, :, 0])

                def build_match(g, b):
                    dve.tensor_tensor(match[:, b, :, :], keep["rows"][:, bass.ds(g * (GROUP * P), GROUP * P)].rearrange("p (j q) -> p j q", q=P),
                                      over(keep["dst"][:, bass.ds(g * GROUP, GROUP)].unsqueeze(2), [P, GROUP, P]),
                                      ALU.is_equal).then_inc(match_ready, 1)

                def split(r, i):
                    dve.wait_ge(y_hi, r * GT + (i + 1))
                    dve.tensor_tensor(Yl[:, i % GROUP, :], tile(r, i, W), Yh[:, i % GROUP, :].bitcast(F32),
                                      ALU.subtract).then_inc(y_lo, 1)

                def round_(r, last, loaded):
                    for i in range(GT):
                        j = i % GROUP
                        if i == 0:
                            build_match(r * 2 + 1, 1)
                        if i == GROUP and not last:
                            build_match(r * 2 + 2, 0)
                        if i < GROUP and not last:
                            if i == 0:
                                for b in range(2):
                                    dve.wait_ge(x_loaded[b], loaded[b])
                            stats(r + 1, 2 * i)
                            stats(r + 1, 2 * i + 1)
                        if not (last and i >= GT - 2):
                            split(r, i + 2)
                        dve.wait_ge(carry_ready, r * (2 * GT) + (2 * i + 3))
                        dve.wait_ge(stored[j], r * 32 + 16 * (i // GROUP))
                        dve.tensor_copy(T[:, j, :].rearrange("p (a f) -> p a f", a=2), s[:, 2 * j:2 * j + 2, 0:HW]).then_inc(out_ready, 1)
                        if i == GROUP - 1 and not last:
                            scale(r + 1)

                dve.wait_ge(x_loaded[0], 128)
                for i in range(GT):
                    stats(0, i)
                scale(0)
                build_match(0, 0)
                split(0, 0)
                split(0, 1)
                with dve.Fori(0, 2) as q:
                    round_(q * 2, False, (q * 128 + 128, q * 128 + 128))
                    round_(q * 2 + 1, False, (q * 128 + 256, q * 128 + 128))
                round_(ER - 1, True, None)

            @block.tensor
            def _(pe):
                pe.sem_inc(out_ready, GROUP)
                pe.sem_inc(bulk_ready, GROUP)
                pe.sem_inc(carry_ready, 1)
                pe.wait_ge(init, 1)
                with pe.Fori(0, ER) as r:
                    for i in range(GT):
                        j, b = i % GROUP, i // GROUP
                        t = r * GT + i
                        if j == 0:
                            pe.wait_ge(match_ready, r * 2 + (b + 1))
                        pe.wait_ge(y_lo, t + 1)
                        pe.wait_ge(out_ready, t + 1)
                        for h in range(2):
                            w = slice(HW * h, HW * h + HW)
                            pe.matmul(s[:, 2 * j + h, 0:HW], match[:, b, j, :], Yh[:, j, w], start=True, stop=False)
                            mm = pe.matmul(s[:, 2 * j + h, 0:HW], match[:, b, j, :], Yl[:, j, w], start=False, stop=False)
                        mm.then_inc(bulk_ready, 1)
                        for h in range(2):
                            pe.wait_ge(carry_ready, t * 2 + h)
                            pe.matmul(s[:, 2 * j + h, 0:HW], match[0:1, b, j, :].bitcast(F32), carry[0:1, h, :],
                                      start=False, stop=True).then_inc(sum_ready, 1)


def layer2_nodes(nc, core, a, keep, x2, T2, x3):
    sem = core.sem
    w_loaded, w_hi, w_lo, init = sem("g_w"), sem("g_whi"), sem("g_wlo"), sem("g_init")
    idx_staged, go = sem("g_idx"), sem("g_go")
    RING = 4
    x_loaded = [sem(f"g_x{u}") for u in range(RING)]
    run_loaded, stored = ([sem(f"g_{n}{b}") for b in range(2)] for n in ("run", "st"))
    ln_step, var_ready, std_ready, norm_ready, h_ready = (sem("g_" + n) for n in ("lnstep", "var", "std", "norm", "h"))
    a_ready, ns_step = sem("g_a"), sem("g_ns")
    tp_ready, tp_free, hT_hi = sem("g_tp"), sem("g_tpfree"), sem("g_hThi")
    o_ready, biased, relu_ready, out_ready = sem("g_o"), sem("g_biased"), sem("g_relu"), sem("g_out")
    TW = F + 2
    with ExitStack() as st:
        sb = lambda n, s, d=F32: core.sb(st, "g_" + n, s, d)
        X = sb("X", [P, RING, GROUP, XW])
        G = sb("G", [P, 2, GROUP, TW])
        H = sb("H", [P, 2, GROUP, F])
        V = sb("V", [P, GROUP, F])
        O = sb("O", [P, 2, GROUP, F])
        idx = sb("idx", [P, 2, GROUP], I32)
        stt = core.stats(st, "g")
        ns = sb("ns", [P, RING, GROUP])
        hTh, hTl = sb("hTh", [P, 2, KF, GROUP * P], F32R), sb("hTl", [P, 2, KF, GROUP * P], F32R)
        Wraw = sb("Wraw", [P, KF, F])
        Wh, Wl = sb("Wh", [P, KF, F], F32R), sb("Wl", [P, KF, F], F32R)
        bias = sb("bias", [P, F])
        tp = core.ps(st, "g_tp_ps", [P, 2, 512])
        o = core.ps(st, "g_o_ps", [P, GROUP, 512])

        def groups(engine, body):
            with engine.Fori(0, NG // RING - 1) as it:
                for u in range(RING):
                    body(it, u)
            for u in range(RING):
                body(NG // RING - 1, u)

        def there(it, u, ahead):
            return not isinstance(it, int) or it * RING + u + ahead < NG

        def cols(u):
            return slice(GROUP * (u % 2), GROUP * (u % 2) + GROUP)

        with nc.Block() as block:
            @block.sync
            def _(sp):
                def load(it, u):
                    sp.dma_start(X[:, u, :, :], group_rows(x2, it * RING + u, XW)).then_inc(x_loaded[u], 16)

                def body(it, u):
                    b = u % 2
                    sp.wait_ge(out_ready, it * 16 + (4 * u + 4 + GROUP))
                    sp.dma_start(group_rows(x3, it * RING + u, F), O[:, b, :, :]).then_inc(stored[b], 16)
                    if there(it, u, RING):
                        load(it + 1, u)

                load(0, 0)
                load(0, 1)
                sp.dma_start(Wraw[:, :, :], a["W2nT"].rearrange("(k p) n -> p k n", p=P)).then_inc(w_loaded, 16)
                sp.dma_start(bias[:, :], a["L2_gnn_b"].rearrange("(o n) -> o n", o=1).broadcast_to([P, F])).then_inc(w_loaded, 16)
                load(0, 2)
                load(0, 3)
                groups(sp, body)
                for b in range(2):
                    sp.wait_ge(stored[b], 16 * NR)

            @block.gpsimd
            def _(pool):
                pool.memset(G[:, :, :, :], 0.0).then_inc(init, 1)
                pool.wait_ge(init, 1)

                def gather(it, u):
                    g, b = it * RING + u, u % 2
                    if not (isinstance(it, int) and it == 0 and u < 2):
                        pool.wait_ge(run_loaded[b], it * 128 + 64 * (u // 2))
                        pool.wait_ge(a_ready, it * 16 + (4 * u - 4))
                        pool.sem_inc(go, 1)
                    pool.tensor_copy(idx[:, b, :], keep["slot"][:, bass.ds(g * GROUP, GROUP)]).then_inc(idx_staged, 1)
                    pool.wait_ge(idx_staged, g + 1)
                    pool.sem_inc(go, 1)
                    for j in range(GROUP):
                        pool.indirect_dma_start(G[:, b, j, :], None, T2[:, :],
                                                bass.IndirectOffsetOnAxis(idx[:, b, j:j + 1], 0),
                                                bounds_check=ROWS_E - 1, oob_is_err=False).then_inc(run_loaded[b], 16)

                def body(it, u):
                    if there(it, u, 3):
                        gather(*((it, 3) if u == 0 else (it + 1, u - 1)))
                    for j in range(GROUP):
                        pool.wait_ge(relu_ready, it * 16 + (4 * u + j + 1))
                        if j == 0:
                            pool.wait_ge(stored[u % 2], it * 32 + 16 * (u // 2))
                        pool.sem_inc(go, 1)
                        pool.tensor_tensor(O[:, u % 2, j, :], V[:, j, :], X[:, u, j, 0:F], ALU.add).then_inc(out_ready, 1)

                for u in range(3):
                    gather(0, u)
                groups(pool, body)

            @block.scalar
            def _(act):
                def root(it, u):
                    n = cols(u)
                    act.wait_ge(var_ready, it * 16 + (4 * u + 4))
                    act.activation(stt["std"][:, n], stt["mv"][:, n, 1], ACT.Sqrt, bias=keep["eps"][:, 0:1]).then_inc(std_ready, 1)

                def norm_rows(it, u, rows):
                    act.wait_ge(norm_ready, it * RING + (u + 1))
                    if not isinstance(it, int) or it * RING + u >= 2:
                        act.wait_ge(tp_ready, it * 16 + (4 * u - 4))
                    for j in rows:
                        relu_norm(act, H[:, u % 2, j, :], X[:, u, j, 0:F], stt, GROUP * (u % 2) + j).then_inc(h_ready, 1)

                def turned(it, u, c):
                    if not isinstance(it, int) or it * RING + u >= 1:
                        act.wait_ge(o_ready, it * 16 + (4 * u - 4))
                    act.wait_ge(tp_ready, it * 16 + (4 * u + c + 1))
                    act.copy(hTh[:, u % 2, c, :], tp[:, c % 2, :]).then_inc(hT_hi, 1)

                def relu(it, u, j):
                    act.wait_ge(biased, it * 16 + (4 * u + j + 1 + GROUP))
                    act.activation(V[:, j, :], V[:, j, :], ACT.Relu).then_inc(relu_ready, 1)

                def body(it, u):
                    nxt = (it, u + 1) if u < 3 else (it + 1, 0)
                    two = (it, u + 2) if u < 2 else (it + 1, u - 2)
                    turn, norm = there(it, u, 1), there(it, u, 2)
                    if turn:
                        turned(*nxt, 0)
                    if norm:
                        root(*two)
                    relu(it, u, 0)
                    if turn:
                        turned(*nxt, 1)
                    if norm:
                        norm_rows(*two, (0, 1))
                    relu(it, u, 1)
                    if norm:
                        norm_rows(*two, (2,))
                    if turn:
                        turned(*nxt, 2)
                        turned(*nxt, 3)
                    if norm:
                        norm_rows(*two, (3,))
                    relu(it, u, 2)
                    relu(it, u, 3)

                for u in range(2):
                    root(0, u)
                    norm_rows(0, u, range(GROUP))
                split_on_act(act, Wraw[:, :, :], Wh[:, :, :], w_loaded, 32, w_hi)
                for c in range(KF):
                    turned(0, 0, c)
                groups(act, body)

            @block.vector
            def _(dve):
                def stats(it, u):
                    dve.wait_ge(x_loaded[u], it * 16 + 16)
                    for j in range(GROUP):
                        dve.bn_stats(stt["raw"][:, GROUP * (u % 2) + j, :], X[:, u, j, 0:F]).then_inc(ln_step, 1)
                    dve.wait_ge(ln_step, it * 24 + (6 * u + 4))
                    dve.sem_inc(stt["go"], 1)
                    for j in range(GROUP * (u % 2), GROUP * (u % 2) + GROUP):
                        dve.bn_aggr(stt["mv"][:, j, :], stt["raw"][:, j, :]).then_inc(var_ready, 1)

                def scale(it, u):
                    n, g = cols(u), it * RING + u
                    dve.wait_ge(std_ready, it * RING + (u + 1))
                    dve.reciprocal(stt["rstd"][:, n], stt["std"][:, n]).then_inc(ln_step, 1)
                    dve.wait_ge(ln_step, it * 24 + (6 * u + 5))
                    dve.tensor_tensor(stt["rstd"][:, n], stt["rstd"][:, n], keep["dis2"][:, bass.ds(g * GROUP, GROUP)],
                                      ALU.mult).then_inc(ln_step, 1)
                    dve.wait_ge(ln_step, it * 24 + (6 * u + 6))
                    dve.scalar_tensor_tensor(out=stt["shift"][:, n], in0=stt["mv"][:, n, 0], scalar=-1.0, in1=stt["rstd"][:, n],
                                             op0=ALU.mult, op1=ALU.mult).then_inc(norm_ready, 1)

                def norms(it, u):
                    g = it * RING + u
                    dve.wait_ge(run_loaded[u % 2], it * 128 + 64 * (u // 2 + 1))
                    dve.tensor_tensor(ns[:, u, :], G[:, u % 2, :, F:F + 1].rearrange("p j c -> p (j c)"),
                                      keep["dish"][:, bass.ds(g * GROUP, GROUP)], ALU.mult).then_inc(ns_step, 1)
                    dve.wait_ge(ns_step, it * 8 + (2 * u + 1))
                    dve.tensor_tensor(ns[:, u, :], ns[:, u, :], keep["dis2"][:, bass.ds(g * GROUP, GROUP)], ALU.add).then_inc(ns_step, 1)

                def add_runs(it, u, rows):
                    for j in rows:
                        h = H[:, u % 2, j, :]
                        dve.wait_ge(h_ready, it * 16 + (4 * u + j + 1))
                        dve.scalar_tensor_tensor(out=h, in0=G[:, u % 2, j, 0:F],
                                                 scalar=keep["dish"][:, bass.ds((it * RING + u) * GROUP + j, 1)], in1=h,
                                                 op0=ALU.mult, op1=ALU.add).then_inc(a_ready, 1)

                def turned(it, u, c):
                    dve.wait_ge(hT_hi, it * 16 + (4 * u + c + 1))
                    dve.tensor_tensor(hTl[:, u % 2, c, :], tp[:, c % 2, :], hTh[:, u % 2, c, :].bitcast(F32),
                                      ALU.subtract).then_inc(tp_free, 1)

                def add_bias(it, u, j):
                    if j == 0:
                        dve.wait_ge(ns_step, it * 8 + (2 * u + 2))
                    dve.wait_ge(o_ready, it * 16 + (4 * u + j + 1))
                    dve.wait_ge(out_ready, it * 16 + (4 * u + j + 1))
                    dve.scalar_tensor_tensor(out=V[:, j, :], in0=bias[:, :], scalar=ns[:, u, j:j + 1],
                                             in1=o[:, j, :], op0=ALU.mult, op1=ALU.add).then_inc(biased, 1)

                def body(it, u):
                    nxt = (it, u + 1) if u < 3 else (it + 1, 0)
                    two = (it, u + 2) if u < 2 else (it + 1, u - 2)
                    turn, norm = there(it, u, 1), there(it, u, 2)
                    if norm:
                        stats(*two)
                    if turn:
                        turned(*nxt, 0)
                    add_bias(it, u, 0)
                    if norm:
                        scale(*two)
                    if turn:
                        turned(*nxt, 1)
                    add_bias(it, u, 1)
                    if norm:
                        norms(*two)
                        add_runs(*two, (0, 1))
                    if turn:
                        turned(*nxt, 2)
                        turned(*nxt, 3)
                    add_bias(it, u, 2)
                    if norm:
                        add_runs(*two, (2, 3))
                    add_bias(it, u, 3)

                for u in range(2):
                    stats(0, u)
                    scale(0, u)
                split_on_dve(dve, Wraw[:, :, :], Wh[:, :, :], Wl[:, :, :], w_hi, 1, w_lo)
                for u in range(2):
                    norms(0, u)
                    add_runs(0, u, range(GROUP))
                for c in range(KF):
                    turned(0, 0, c)
                groups(dve, body)

            @block.tensor
            def _(pe):
                def turn(it, u, c):
                    pe.wait_ge(a_ready, it * 16 + (4 * u + 4))
                    pe.wait_ge(tp_free, it * 16 + (4 * u + c + 1))
                    for j in range(GROUP):
                        mm = pe.transpose(tp[:, c % 2, j * P:(j + 1) * P], H[:, u % 2, j, c * P:(c + 1) * P], keep["ident"][:, :])
                    mm.then_inc(tp_ready, 1)

                def product(it, u, j):
                    pe.wait_ge(biased, it * 16 + (4 * u + j + 1))
                    for c in range(KF):
                        if j == 0:
                            pe.wait_ge(tp_free, it * 16 + (4 * u + c + 1 + 2))
                        mm = three(pe, o[:, j, :], (hTh[:, u % 2, c, j * P:(j + 1) * P], hTl[:, u % 2, c, j * P:(j + 1) * P]),
                                   (Wh[:, c, :], Wl[:, c, :]), c == 0, c == KF - 1)
                    mm.then_inc(o_ready, 1)

                def body(it, u):
                    nxt = (it, u + 1) if u < 3 else (it + 1, 0)
                    for j in range(GROUP):
                        product(it, u, j)
                        if there(it, u, 1):
                            for c in ((0,), (1,), (2, 3), ())[j]:
                                turn(*nxt, c)

                pe.sem_inc(tp_free, 2)
                pe.sem_inc(biased, GROUP)
                pe.sem_inc(out_ready, GROUP)
                for c in range(KF):
                    turn(0, 0, c)
                pe.wait_ge(w_lo, 1)
                groups(pe, body)


def layer3_edges(nc, core, a, keep, x3, T3):
    sem = core.sem
    w_loaded, w_hi, w_lo, const_ready, const_out, init = (sem("h_" + n) for n in ("w", "whi", "wlo", "const", "constout", "init"))
    go = sem("h_go")
    x_loaded = [sem("h_x0"), sem("h_x1")]
    ln_step, var_ready, std_ready, norm_ready, h_ready = (sem("h_" + n) for n in ("lnstep", "var", "std", "norm", "h"))
    tp_ready, tp_free, hT_hi = sem("h_tp"), sem("h_tpfree"), sem("h_hThi")
    m_ready, m_out, y_ready, y_out, match_ready = sem("h_m"), sem("h_mout"), sem("h_y"), sem("h_yout"), sem("h_match")
    row_ready, next_ready, carry_ready, sum_ready = (sem("h_" + n) for n in ("row", "next", "carry", "sum"))
    sum_hi, sum_lo, z_ready, z_out = sem("h_sumhi"), sem("h_sumlo"), sem("h_z"), sem("h_zout")
    stored = [sem(f"h_st{b}") for b in range(GROUP)]
    D = FE
    GP = GROUP * P
    with ExitStack() as st:
        sb = lambda n, s, d=F32: core.sb(st, "h_" + n, s, d)
        X = sb("X", [P, ET, F])
        H = sb("H", [P, 2, GROUP, F])
        stt = core.stats(st, "h")
        hTh, hTl = sb("hTh", [P, KF, GP], F32R), sb("hTl", [P, KF, GP], F32R)
        Wraw, Wh, Wl = sb("Wraw", [P, KF, D]), sb("Wh", [P, KF, D], F32R), sb("Wl", [P, KF, D], F32R)
        Wf, Wfh, Wfl = sb("Wf", [P, F]), sb("Wfh", [P, F], F32R), sb("Wfl", [P, F], F32R)
        bg, bgw = sb("bg", [P, 1]), sb("bgw", [P, P])
        bf, const = sb("bf", [P, F]), sb("const", [P, F])
        M = sb("M", [P, GP])
        Y = sb("Y", [P, GROUP, D])
        carry = sb("carry", [1, D])
        match = sb("match", [P, 2, GROUP, P])
        Sh, Sl = sb("Sh", [P, GP], F32R), sb("Sl", [P, GP], F32R)
        Z = sb("Z", [P, GROUP, F])
        tp = core.ps(st, "h_tp_ps", [P, 2, 512])
        m = core.ps(st, "h_m_ps", [P, 512])
        y = core.ps(st, "h_y_ps", [P, 512])
        sT = core.ps(st, "h_s_ps", [P, 512])
        nx = core.ps(st, "h_nx_ps", [P, 512])
        z = core.ps(st, "h_z_ps", [P, 2, 512])

        def both(b):
            return slice(GROUP * b, GROUP * b + GROUP)

        def rounds(engine, body):
            with engine.Fori(0, ER - 1) as r:
                for b in range(2):
                    body(r * 2 + b, b, True, True)
            body(EG - 2, 0, True, False)
            body(EG - 1, 1, False, False)

        with nc.Block() as block:
            @block.sync
            def _(sp):
                sp.dma_start(Wraw[:, :, :], a["L3_gnn_W_gcn"].rearrange("(k p) n -> p k n", p=P)).then_inc(w_loaded, 16)
                sp.dma_start(Wf[:, :], a["WfT"]).then_inc(w_loaded, 16)
                sp.dma_start(bg[:, :], a["L3_gnn_b_gcn"].rearrange("(p o) -> p o", o=1)).then_inc(w_loaded, 16)
                sp.dma_start(bf[:, :], a["L3_gnn_b_fc"].rearrange("(o n) -> o n", o=1).broadcast_to([P, F])).then_inc(w_loaded, 16)
                with sp.Fori(0, EG) as g:
                    for j in range(GROUP):
                        sp.wait_ge(z_out, g * GROUP + (j + 1 + 2))
                        sp.dma_start(T3[bass.ds((g * GROUP + j) * P, P), :], Z[:, j, :]).then_inc(stored[j], 16)
                for j in range(GROUP):
                    sp.wait_ge(stored[j], 16 * EG)

            @block.gpsimd
            def _(pool):
                for t in range(ET):
                    g, j = t // GROUP, t % GROUP
                    if j == 0 and g >= 2:
                        pool.wait_ge(x_loaded[g % 2], 64 * (g // 2))
                        pool.sem_inc(go, 1)
                    pool.indirect_dma_start(X[:, t, :], None, x3[:, :], bass.IndirectOffsetOnAxis(keep["src"][:, t:t + 1], 0),
                                            bounds_check=ROWS_N - 1, oob_is_err=False).then_inc(x_loaded[g % 2], 16)

            @block.scalar
            def _(act):
                def root(g, b):
                    act.wait_ge(var_ready, g * 4 + 4)
                    act.activation(stt["std"][:, both(b)], stt["mv"][:, both(b), 1], ACT.Sqrt, bias=keep["eps"][:, 0:1]).then_inc(std_ready, 1)

                def norm_rows(g, b, rows):
                    act.wait_ge(norm_ready, g + 1)
                    for j in rows:
                        relu_norm(act, H[:, b, j, :], X[:, bass.ds(g * GROUP + j, 1), :].rearrange("p o f -> p (o f)"),
                                  stt, GROUP * b + j).then_inc(h_ready, 1)

                def turned(g, c):
                    act.wait_ge(m_ready, g)
                    act.wait_ge(tp_ready, g * 4 + (c + 1))
                    act.copy(hTh[:, c, :], tp[:, c % 2, :]).then_inc(hT_hi, 1)

                def messages(g):
                    act.wait_ge(m_ready, g + 1)
                    act.wait_ge(y_ready, g)
                    act.copy(M[:, :], m[:, :]).then_inc(m_out, 1)

                def first_row(g):
                    act.wait_ge(y_out, g + 1)
                    act.wait_ge(carry_ready, g)
                    act.copy(Y[0:1, 0, :], carry[0:1, :]).then_inc(row_ready, 1)

                def body(g, b, turn, norm):
                    for j in range(GROUP):
                        act.wait_ge(next_ready, g * GROUP + (j + 1))
                        if j < GROUP - 1:
                            act.copy(Y[0:1, j + 1, :], nx[0:1, 0:D]).then_inc(row_ready, 1)
                        else:
                            act.wait_ge(row_ready, g * GROUP + (j + 1))
                            act.copy(carry[0:1, :], nx[0:1, 0:D]).then_inc(carry_ready, 1)
                        if turn:
                            turned(g + 1, j)
                    act.wait_ge(sum_ready, g + 1)
                    act.wait_ge(z_ready, g * GROUP)
                    act.copy(Sh[:, :], sT[:, :]).then_inc(sum_hi, 1)
                    if norm:
                        root(g + 2, b)
                        norm_rows(g + 2, b, (0, 1))
                    if turn:
                        messages(g + 1)
                    if norm:
                        norm_rows(g + 2, b, (2, 3))
                    if turn:
                        first_row(g + 1)

                for g in range(2):
                    root(g, g)
                    norm_rows(g, g, range(GROUP))
                split_on_act(act, Wraw[:, :, :], Wh[:, :, :], w_loaded, 64, w_hi)
                split_on_act(act, Wf[:, :], Wfh[:, :], w_loaded, 64, w_hi)
                for c in range(KF):
                    turned(0, c)
                messages(0)
                act.wait_ge(init, 1)
                first_row(0)
                rounds(act, body)

            @block.vector
            def _(dve):
                def stats(g, b, j):
                    dve.bn_stats(stt["raw"][:, GROUP * b + j, :], X[:, bass.ds(g * GROUP + j, 1), :].rearrange("p o f -> p (o f)")
                                 ).then_inc(ln_step, 1)

                def mean(g, b):
                    dve.wait_ge(ln_step, g * 5 + 4)
                    dve.sem_inc(stt["go"], 1)
                    for i in range(GROUP * b, GROUP * b + GROUP):
                        dve.bn_aggr(stt["mv"][:, i, :], stt["raw"][:, i, :]).then_inc(var_ready, 1)

                def scale(g, b):
                    n = both(b)
                    dve.wait_ge(std_ready, g + 1)
                    dve.reciprocal(stt["rstd"][:, n], stt["std"][:, n]).then_inc(ln_step, 1)
                    dve.wait_ge(ln_step, g * 5 + 5)
                    dve.scalar_tensor_tensor(out=stt["shift"][:, n], in0=stt["mv"][:, n, 0], scalar=-1.0, in1=stt["rstd"][:, n],
                                             op0=ALU.mult, op1=ALU.mult).then_inc(norm_ready, 1)

                def build_match(g, b):
                    dve.tensor_tensor(match[:, b, :, :], keep["rows"][:, bass.ds(g * GP, GP)].rearrange("p (j q) -> p j q", q=P),
                                      over(keep["dst"][:, bass.ds(g * GROUP, GROUP)].unsqueeze(2), [P, GROUP, P]),
                                      ALU.is_equal).then_inc(match_ready, 1)

                def turned(g, c):
                    dve.wait_ge(hT_hi, g * 4 + (c + 1))
                    dve.tensor_tensor(hTl[:, c, :], tp[:, c % 2, :], hTh[:, c, :].bitcast(F32), ALU.subtract).then_inc(tp_free, 1)

                def weigh(g):
                    dve.wait_ge(y_ready, g + 1)
                    dve.tensor_tensor(Y[:, :, :], y[:, :].rearrange("p (j d) -> p j d", d=D),
                                      over(keep["wgt"][:, bass.ds(g * GROUP, GROUP)].unsqueeze(2), [P, GROUP, D]),
                                      ALU.mult).then_inc(y_out, 1)

                def out(g, j):
                    dve.wait_ge(z_ready, g * GROUP + (j + 1))
                    dve.wait_ge(stored[j], g * 16)
                    dve.tensor_tensor(Z[:, j, :], z[:, j % 2, :], const[:, :], ALU.add).then_inc(z_out, 1)

                def body(g, b, turn, norm):
                    if turn:
                        build_match(g + 1, 1 - b)
                    if norm:
                        dve.wait_ge(x_loaded[b], g * 32 + (128 - 32 * b))
                    for j in range(GROUP):
                        if norm:
                            stats(g + 2, b, j)
                        if turn:
                            turned(g + 1, j)
                    if norm:
                        mean(g + 2, b)
                    dve.wait_ge(sum_hi, g + 1)
                    dve.tensor_tensor(Sl[:, :], sT[:, :], Sh[:, :].bitcast(F32), ALU.subtract).then_inc(sum_lo, 1)
                    if norm:
                        scale(g + 2, b)
                    out(g, 0)
                    out(g, 1)
                    if turn:
                        weigh(g + 1)
                    out(g, 2)
                    out(g, 3)

                dve.memset(carry[:, :], 0.0).then_inc(init, 1)
                for g in range(2):
                    dve.wait_ge(x_loaded[g], 64)
                    for j in range(GROUP):
                        stats(g, g, j)
                    mean(g, g)
                    scale(g, g)
                split_on_dve(dve, Wraw[:, :, :], Wh[:, :, :], Wl[:, :, :], w_hi, 1, w_lo)
                split_on_dve(dve, Wf[:, :], Wfh[:, :], Wfl[:, :], w_hi, 2, w_lo)
                dve.tensor_copy(bgw[:, :], over(bg[:, 0:1], [P, P])).then_inc(w_lo, 1)
                build_match(0, 0)
                for c in range(KF):
                    turned(0, c)
                dve.wait_ge(const_ready, 1)
                dve.tensor_tensor(const[:, :], z[:, 0, :], bf[:, :], ALU.add).then_inc(const_out, 1)
                weigh(0)
                dve.wait_ge(const_out, 1)
                rounds(dve, body)

            @block.tensor
            def _(pe):
                def turn(g, b, c):
                    pe.wait_ge(h_ready, g * 4 + 4)
                    pe.wait_ge(tp_free, g * 4 + (c + 1))
                    for j in range(GROUP):
                        mm = pe.transpose(tp[:, c % 2, j * P:(j + 1) * P], H[:, b, j, c * P:(c + 1) * P], keep["ident"][:, :])
                    mm.then_inc(tp_ready, 1)

                def product(g):
                    pe.wait_ge(m_out, g)
                    for c in range(KF):
                        pe.wait_ge(tp_free, g * 4 + (c + 1 + 2))
                        mm = three(pe, m[:, :], (Wh[:, c, :], Wl[:, c, :]), (hTh[:, c, :], hTl[:, c, :]), c == 0, c == KF - 1)
                    mm.then_inc(m_ready, 1)

                def turn_back(g):
                    pe.wait_ge(m_out, g + 1)
                    pe.wait_ge(y_out, g)
                    for j in range(GROUP):
                        mm = pe.transpose(y[:, j * P:(j + 1) * P], M[:, j * P:(j + 1) * P], keep["ident"][:, :])
                    mm.then_inc(y_ready, 1)

                def out(g, j):
                    pe.wait_ge(z_out, g * GROUP + (j + 1))
                    three(pe, z[:, j % 2, :], (Sh[:, j * P:(j + 1) * P], Sl[:, j * P:(j + 1) * P]),
                          (Wfh[:, :], Wfl[:, :]), True, True).then_inc(z_ready, 1)

                def body(g, b, following, norm):
                    pe.wait_ge(match_ready, g + 1)
                    for j in range(GROUP):
                        pe.wait_ge(row_ready, g * GROUP + (j + 1))
                        if j == 0:
                            pe.wait_ge(carry_ready, g)
                        pe.matmul(nx[0:1, 0:D], match[:, b, j, 0:1], Y[:, j, :], start=True, stop=True).then_inc(next_ready, 1)
                        if j == 0:
                            pe.wait_ge(sum_lo, g)
                        mm = pe.matmul(sT[:, j * P:(j + 1) * P], Y[:, j, :], match[:, b, j, :], start=True, stop=True)
                        if j == GROUP - 1:
                            mm.then_inc(sum_ready, 1)
                        if following:
                            turn(g + 1, 1 - b, j)
                    if following:
                        product(g + 1)
                    pe.wait_ge(sum_lo, g + 1)
                    out(g, 0)
                    out(g, 1)
                    if following:
                        turn_back(g + 1)
                    out(g, 2)
                    out(g, 3)

                pe.sem_inc(tp_free, 2)
                pe.sem_inc(z_out, 2)
                for c in range(KF):
                    turn(0, 0, c)
                pe.wait_ge(w_lo, 3)
                pe.matmul(z[:, 0, :], bgw[:, :], Wf[:, :], start=True, stop=True).then_inc(const_ready, 1)
                product(0)
                turn_back(0)
                pe.wait_ge(const_out, 1)
                rounds(pe, body)


def layer3_nodes(nc, core, a, keep, x3, T3, out):
    sem = core.sem
    w_loaded, wide, const_ready, const_out = sem("i_w"), sem("i_wide"), sem("i_const"), sem("i_constout")
    idx_staged, go, filled = sem("i_idx"), sem("i_go"), sem("i_fill")
    x_loaded, run_loaded, stored = ([sem(f"i_{n}{b}") for b in range(2)] for n in ("x", "g", "st"))
    out_ready = sem("i_out")
    with ExitStack() as st:
        sb = lambda n, s, d=F32: core.sb(st, "i_" + n, s, d)
        X = sb("X", [P, 2, GROUP, F])
        G = sb("G", [P, 2, GROUP, F])
        idx = sb("idx", [P, 2, GROUP], I32)
        Wf, bf, const = sb("Wf", [P, F]), sb("bf", [P, F]), sb("const", [P, F])
        bg, bgw = sb("bg", [P, 1]), sb("bgw", [P, P])
        z = core.ps(st, "i_z_ps", [P, 512])
        with nc.Block() as block:
            @block.sync
            def _(sp):
                sp.dma_start(Wf[:, :], a["WfT"]).then_inc(w_loaded, 16)
                sp.dma_start(bg[:, :], a["L3_gnn_b_gcn"].rearrange("(p o) -> p o", o=1)).then_inc(w_loaded, 16)
                sp.dma_start(bf[:, :], a["L3_gnn_b_fc"].rearrange("(o n) -> o n", o=1).broadcast_to([P, F])).then_inc(w_loaded, 16)
                with sp.Fori(0, NR) as r:
                    for b in range(2):
                        sp.wait_ge(stored[b], r * 16)
                        sp.dma_start(X[:, b, :, :], group_rows(x3, r * 2 + b, F)).then_inc(x_loaded[b], 16)

            @block.gpsimd
            def _(pool):
                with pool.Fori(0, NR) as r:
                    for b in range(2):
                        g = r * 2 + b
                        pool.wait_ge(run_loaded[b], r * 64)
                        pool.sem_inc(go, 1)
                        pool.tensor_copy(idx[:, b, :], keep["slot"][:, bass.ds(g * GROUP, GROUP)]).then_inc(idx_staged, 1)
                        pool.wait_ge(idx_staged, g + 1)
                        pool.wait_ge(filled, g + 1)
                        pool.sem_inc(go, 1)
                        for i in range(GROUP):
                            pool.indirect_dma_start(G[:, b, i, :], None, T3[:, :], bass.IndirectOffsetOnAxis(idx[:, b, i:i + 1], 0),
                                                    bounds_check=ROWS_E - 1, oob_is_err=False).then_inc(run_loaded[b], 16)

            @block.scalar
            def _(act):
                def fill(b):
                    act.copy(G[:, b, :, :], over(const[:, :].unsqueeze(1), [P, GROUP, F])).then_inc(filled, 1)

                act.wait_ge(const_out, 1)
                fill(0)
                fill(1)
                with act.Fori(0, NR - 1) as r:
                    for b in range(2):
                        act.wait_ge(out_ready, r * 2 + (b + 1))
                        act.dma_start(group_rows(out, r * 2 + b, F), X[:, b, :, :]).then_inc(stored[b], 16)
                        fill(b)
                act.wait_ge(out_ready, NG - 1)
                act.dma_start(group_rows(out, NG - 2, F), X[:, 0, :, :]).then_inc(stored[0], 16)
                act.wait_ge(out_ready, NG)
                at = (NG - 1) * GROUP * P
                for j in range((NODES - at + P - 1) // P):
                    n = min(P, NODES - at - j * P)
                    act.dma_start(out[at + j * P:at + j * P + n, :], X[0:n, 1, j, :]).then_inc(stored[1], 16)
                act.wait_ge(stored[0], 16 * NR)
                act.wait_ge(stored[1], 16 * (NR - 1) + 48)

            @block.vector
            def _(dve):
                dve.wait_ge(w_loaded, 48)
                dve.tensor_copy(bgw[:, :], over(bg[:, 0:1], [P, P])).then_inc(wide, 1)
                dve.wait_ge(const_ready, 1)
                dve.tensor_tensor(const[:, :], z[:, :], bf[:, :], ALU.add).then_inc(const_out, 1)
                with dve.Fori(0, NR) as r:
                    for b in range(2):
                        dve.wait_ge(x_loaded[b], r * 16 + 16)
                        dve.wait_ge(run_loaded[b], r * 64 + 64)
                        dve.tensor_tensor(X[:, b, :, :], X[:, b, :, :], G[:, b, :, :], ALU.add).then_inc(out_ready, 1)

            @block.tensor
            def _(pe):
                pe.wait_ge(wide, 1)
                pe.matmul(z[:, :], bgw[:, :], Wf[:, :], start=True, stop=True).then_inc(const_ready, 1)


def program(nc, a, out, stop_after=9):
    core = Core(nc)
    with core.whole:
        outer = core.whole
        keep = {
            "src": core.sb(outer, "src", [P, ET + 2 * GROUP], I32), "dst": core.sb(outer, "dstk", [P, ET + 2 * GROUP], I32),
            "rows": core.sb(outer, "rows", [P, ROWS_E + GROUP * P], U16), "fac": core.sb(outer, "fac", [P, ET, HEADS]),
            "wgt": core.sb(outer, "wgt", [P, ET]), "ident": core.sb(outer, "ident", [P, P]), "eps": core.sb(outer, "eps", [P, 1]),
            "slot": core.sb(outer, "slot", [P, NT + 8], I32),
        }
        for n in ("dis", "dis2", "has", "dish"):
            keep[n] = core.sb(outer, n, [P, NT + 8])

        def table(name, rows, width, last):
            return out if last == stop_after else nc.dram_tensor(name, (rows, width), F32).ap()

        T0 = table("T0", ROWS_E, IN, 1)
        x1 = table("x1", ROWS_N, F, 2)
        T1 = table("T1", ROWS_E, F, 3)
        x2 = table("x2", ROWS_N, XW, 4)
        T2 = table("T2", ROWS_E, F + 2, 5)
        x3 = table("x3", ROWS_N, F, 6)
        T3 = table("T3", ROWS_E, F, 7)
        with ExitStack() as w:
            l0 = {"W1h": core.sb(w, "W1h", [P, KI, HID], F32R), "W1l": core.sb(w, "W1l", [P, KI, HID], F32R),
                  "W23h": core.sb(w, "W23h", [P, KH, IN], F32R), "W23l": core.sb(w, "W23l", [P, KH, IN], F32R),
                  "b1": core.sb(w, "b1", [P, KH]), "c2": core.sb(w, "c2", [P, IN])}
            core.run(prepare, a, keep, l0)
            core.run(layer0_edges, a, keep, l0, T0)
        if stop_after >= 2:
            core.run(layer0_nodes, a, keep, T0, x1)
        if stop_after >= 3:
            with ExitStack() as w:
                msg = core.sb(w, "msg", [P, ET, F + HEADS])
                logit = core.sb(w, "logit", [P, ET, HEADS])
                core.run(layer1_messages, a, keep, x1, msg, logit)
                core.run(layer1_softmax, a, keep, logit)
                core.run(layer1_sums, a, keep, msg, logit, T1)
        if stop_after >= 4:
            core.run(layer1_nodes, a, keep, x1, T1, x2)
        if stop_after >= 5:
            core.run(layer2_edges, a, keep, x2, T2)
        if stop_after >= 6:
            core.run(layer2_nodes, a, keep, x2, T2, x3)
        if stop_after >= 7:
            core.run(layer3_edges, a, keep, x3, T3)
        if stop_after >= 8:
            core.run(layer3_nodes, a, keep, x3, T3, out)


def windows(v, np, tiles, front, back):
    at = NEW * np.arange(tiles)[None, :] - 1 + np.arange(P)[:, None]
    w = np.concatenate([np.full((1,) + v.shape[1:], front, v.dtype), v,
                        np.full((tiles * P,) + v.shape[1:], back, v.dtype)])
    return np.ascontiguousarray(w[at + 1])


def lay_out(inputs, np):
    a = {}
    for n in ("x", "L1_gnn_et_emb", "L0_gnn_W1", "L0_gnn_b1", "L0_gnn_b2", "L0_gnn_W3", "L0_gnn_b3", "L0_gnn_W4", "L0_gnn_b4",
              "L1_gnn_W", "L1_gnn_a_src", "L1_gnn_a_dst", "L1_gnn_ln_gamma", "L1_gnn_ln_beta", "L2_gnn_b",
              "L3_gnn_W_gcn", "L3_gnn_b_gcn", "L3_gnn_b_fc"):
        a[n] = np.ascontiguousarray(inputs[n])
    a["W2T"] = np.ascontiguousarray(np.asarray(inputs["L0_gnn_W2"]).T)
    a["W1T"] = np.ascontiguousarray(np.asarray(inputs["L1_gnn_W"]).T)
    a["W2nT"] = np.ascontiguousarray(np.asarray(inputs["L2_gnn_W"]).T)
    a["WfT"] = np.ascontiguousarray(np.asarray(inputs["L3_gnn_W_fc"]).T)
    dst, src = np.asarray(inputs["dst"]), np.asarray(inputs["src"])
    dw = windows(dst, np, ET, NODES + 1, NODES)
    a["dst_win"] = dw
    a["dst_wide"] = windows(dst, np, ET + 2 * GROUP, NODES + 1, NODES)
    nxt = windows(dst, np, ET + 1, NODES + 1, NODES)
    after = np.concatenate([nxt[1:, :ET], nxt[1:2, 1:]])
    after[0] = dw[0]
    a["dst_next"] = np.ascontiguousarray(after)
    sw = windows(src, np, ET + 2 * GROUP, 0, 0)
    a["src_win"] = sw
    count = windows(src, np, ET, ROWS_N, ROWS_N)
    count[0] = ROWS_N
    a["src_count"] = count
    row = dw.T.copy()
    a["dst_flat"] = row.reshape(1, -1).copy()
    row[:, 0] = row[:, P - 1]
    a["dst_row"] = np.ascontiguousarray(row.reshape(1, -1))
    a["type_win"] = windows(np.asarray(inputs["edge_type_8"]), np, ET, 0, 0)
    a["weight_win"] = windows(np.asarray(inputs["edge_weight"]), np, ET, 0, 0)
    at = windows(np.asarray(inputs["edge_attr_128"]), np, ET + 2 * GROUP, 0, 0)
    a["attr_win"] = np.ascontiguousarray(at.reshape(P, EG + 2, GROUP, FE))
    return a


def kernel(**inputs):
    import numpy as _np
    import concourse.bacc as _bacc
    from concourse import mybir as _mybir
    from concourse.bass_utils import run_bass_kernel_spmd as _run

    nc = _bacc.Bacc("TRN2", target_bir_lowering=False, num_devices=1, dynamic_dma_scratch_size=6144)
    arrays = lay_out(inputs, _np)
    args = {n: nc.dram_tensor("in_" + n, v.shape, _mybir.dt.from_np(v.dtype), kind="ExternalInput").ap()
            for n, v in arrays.items()}
    out = nc.dram_tensor("out_0", (NODES, F), _mybir.dt.float32, kind="ExternalOutput").ap()
    program(nc, args, out)
    r = _run(nc, [{"in_" + n: v for n, v in arrays.items()}], core_ids=[0])
    return r.results[0]["out_0"]
```
